# Optimizing a Trainium2 kernel written in Bass

```python
import numpy as np
import jax
import jax.numpy as jnp

def _softmax(x, axis=-1):
    return jax.nn.softmax(x, axis=axis)

def _gelu(x):
    return jax.nn.gelu(x, approximate=True)

def _silu(x):
    return jax.nn.silu(x)

def _sigmoid(x):
    return jax.nn.sigmoid(x)

def _layernorm(x, axis=-1, eps=1e-05):
    m = jnp.mean(x, axis=axis, keepdims=True)
    v = jnp.var(x, axis=axis, keepdims=True)
    return (x - m) / jnp.sqrt(v + eps)

def _scatter_add(tgt, idx, src, axis=0):
    return tgt.at[idx].add(src)

def _segment_sum(src, seg, n):
    return jax.ops.segment_sum(src, seg, n)
kernel_name = 'mk_adaln_d1_jaxref_r8_571bf2'

def setup_inputs(seed: int=0):
    np.random.seed(seed)
    _w = jnp.asarray

    def _L0_attn_setup():
        import jax, jax.numpy as jnp
        import numpy as np
        ROPE_THETA = 10000.0

        def rope(t, rot_dim):
            S = t.shape[-2]
            half = rot_dim // 2
            inv_freq = 1.0 / ROPE_THETA ** (jnp.arange(0, rot_dim, 2, dtype=jnp.float32) / rot_dim)
            freqs = jnp.arange(S, dtype=jnp.float32)[:, None] * inv_freq[None, :]
            freqs = jnp.repeat(freqs, 2, axis=-1)
            cos, sin = (jnp.cos(freqs), jnp.sin(freqs))
            t_rot, t_pass = (t[..., :rot_dim], t[..., rot_dim:])
            x = t_rot.reshape(*t_rot.shape[:-1], half, 2)
            rh = jnp.stack([-x[..., 1], x[..., 0]], axis=-1).reshape(t_rot.shape)
            t_rot = t_rot * cos + rh * sin
            return jnp.concatenate([t_rot, t_pass], axis=-1)

        def feature_map(x):
            norm = jnp.sqrt(jnp.sum(x * x, axis=-1, keepdims=True))
            return x / jnp.maximum(norm, 1e-12)
        key = jax.random.key(seed)
        kx, kwi, kwo = jax.random.split(key, 3)
        B, S, D = (8, 512, 256)
        scale = 0.02
        return {'X': jax.random.normal(kx, (B, S, D), dtype=jnp.float32), 'W_in': jax.random.normal(kwi, (3 * D, D), dtype=jnp.float32) * scale, 'b_in': jnp.zeros((3 * D,), dtype=jnp.float32), 'W_out': jax.random.normal(kwo, (D, D), dtype=jnp.float32) * scale, 'b_out': jnp.zeros((D,), dtype=jnp.float32)}
    _L0_attn_in = _L0_attn_setup()

    def _L0_ffn_setup():
        import jax, jax.numpy as jnp
        import numpy as np
        E = 8
        H = 256
        F = 704
        TOPK = 2
        key = jax.random.key(seed)
        ks = jax.random.split(key, 5)
        std = 0.02
        x = jax.random.normal(ks[0], (4, 256, H), dtype=jnp.float32)
        router_w = jax.random.normal(ks[1], (E, H), dtype=jnp.float32) * std
        Wg = jax.random.normal(ks[2], (E, F, H), dtype=jnp.float32) * std
        Wu = jax.random.normal(ks[3], (E, F, H), dtype=jnp.float32) * std
        Wd = jax.random.normal(ks[4], (E, H, F), dtype=jnp.float32) * std
        return {'x': x, 'router_w': router_w, 'Wg': Wg, 'Wu': Wu, 'Wd': Wd}
    _L0_ffn_in = _L0_ffn_setup()
    _L0_c = _w((lambda *s: np.random.randn(*s).astype(np.float32) * 0.05)(4, 256))
    _L0_wmod = _w((lambda *s: np.random.randn(*s).astype(np.float32) * 0.05)(256, 6 * 256) * 256 ** (-0.5))
    _d = {'L0_attn_X': _L0_attn_in['X'], 'L0_attn_W_in': _L0_attn_in['W_in'], 'L0_attn_b_in': _L0_attn_in['b_in'], 'L0_attn_W_out': _L0_attn_in['W_out'], 'L0_attn_b_out': _L0_attn_in['b_out'], 'L0_ffn_router_w': _L0_ffn_in['router_w'], 'L0_ffn_Wg': _L0_ffn_in['Wg'], 'L0_ffn_Wu': _L0_ffn_in['Wu'], 'L0_ffn_Wd': _L0_ffn_in['Wd'], 'L0_c': _L0_c, 'L0_wmod': _L0_wmod}
    _x0 = _d['L0_attn_X']
    _d['L0_attn_X'] = jax.random.normal(jax.random.fold_in(jax.random.key(seed), 1), (4, 256, 256), dtype=_x0.dtype)
    del _x0
    return _d

def reference(L0_attn_X, L0_attn_W_in, L0_attn_b_in, L0_attn_W_out, L0_attn_b_out, L0_ffn_router_w, L0_ffn_Wg, L0_ffn_Wu, L0_ffn_Wd, L0_c, L0_wmod):

    def _L0_attn_ref(X, W_in, b_in, W_out, b_out):
        import jax, jax.numpy as jnp
        import numpy as np
        ROPE_THETA = 10000.0

        def rope(t, rot_dim):
            S = t.shape[-2]
            half = rot_dim // 2
            inv_freq = 1.0 / ROPE_THETA ** (jnp.arange(0, rot_dim, 2, dtype=jnp.float32) / rot_dim)
            freqs = jnp.arange(S, dtype=jnp.float32)[:, None] * inv_freq[None, :]
            freqs = jnp.repeat(freqs, 2, axis=-1)
            cos, sin = (jnp.cos(freqs), jnp.sin(freqs))
            t_rot, t_pass = (t[..., :rot_dim], t[..., rot_dim:])
            x = t_rot.reshape(*t_rot.shape[:-1], half, 2)
            rh = jnp.stack([-x[..., 1], x[..., 0]], axis=-1).reshape(t_rot.shape)
            t_rot = t_rot * cos + rh * sin
            return jnp.concatenate([t_rot, t_pass], axis=-1)

        def feature_map(x):
            norm = jnp.sqrt(jnp.sum(x * x, axis=-1, keepdims=True))
            return x / jnp.maximum(norm, 1e-12)
        D = X.shape[-1]
        QKV = jnp.einsum('bsd,ed->bse', X, W_in) + b_in
        Q, K, V = jnp.split(QKV, 3, axis=-1)
        rot_dim = D // 2
        Q = rope(Q, rot_dim)
        K = rope(K, rot_dim)
        A = jnp.sum(feature_map(K) * V, axis=-2)
        Y = A[:, None, :] * Q
        Y = jnp.einsum('bsd,ed->bse', Y, W_out) + b_out
        return Y + X

    def _L0_ffn_ref(x, router_w, Wg, Wu, Wd):
        import jax, jax.numpy as jnp
        import numpy as np
        E = 8
        H = 256
        F = 704
        TOPK = 2
        orig_shape = x.shape
        xt = x.reshape(-1, orig_shape[-1])
        logits = xt @ router_w.T
        probs = jax.nn.softmax(logits, axis=-1)
        topk_w, topk_idx = jax.lax.top_k(probs, TOPK)
        topk_w = topk_w / jnp.sum(topk_w, axis=-1, keepdims=True)
        onehot = jax.nn.one_hot(topk_idx, E, dtype=topk_w.dtype)
        comb = jnp.einsum('tk,tke->te', topk_w, onehot)
        out = jnp.zeros_like(xt)
        for e in range(E):
            gate = jax.nn.silu(xt @ Wg[e].T)
            up = xt @ Wu[e].T
            out = out + gate * up @ Wd[e].T * comb[:, e:e + 1]
        return out.reshape(orig_shape)
    x = L0_attn_X
    mod = (_silu(L0_c) @ L0_wmod).reshape(L0_c.shape[0], 6, 1, -1)
    sa, ca, ga, sb, cb, gb = (mod[:, 0], mod[:, 1], mod[:, 2], mod[:, 3], mod[:, 4], mod[:, 5])
    ga = (2 * (ga >= 0) - 1) * jnp.maximum(jnp.abs(ga), 0.25)
    gb = (2 * (gb >= 0) - 1) * jnp.maximum(jnp.abs(gb), 0.25)
    h = _layernorm(x, axis=-1) * (1 + ca) + sa
    x = x + ga * _L0_attn_ref(h, L0_attn_W_in, L0_attn_b_in, L0_attn_W_out, L0_attn_b_out)
    h = _layernorm(x, axis=-1) * (1 + cb) + sb
    x = x + gb * _L0_ffn_ref(h, L0_ffn_router_w, L0_ffn_Wg, L0_ffn_Wu, L0_ffn_Wd)
    return x

_drawn_inputs = setup_inputs


def setup_inputs(seed=0):
    import zlib

    import numpy as np

    out = dict(_drawn_inputs(seed))
    spreads = {'L0_attn_b_in': (0.0, 0.66), 'L0_attn_b_out': (0.0, 0.348)}
    factors = {'L0_attn_W_in': 3.551,
     'L0_attn_W_out': 3.371,
     'L0_ffn_router_w': 8.0,
     'L0_ffn_Wg': 8.0,
     'L0_ffn_Wu': 8.0,
     'L0_ffn_Wd': 8.0}
    for name, (base, spread) in spreads.items():
        noise = np.random.default_rng([zlib.crc32(name.encode()), seed]).standard_normal(out[name].shape)
        drawn = base * np.exp(spread * noise) if base else spread * noise
        out[name] = jnp.asarray(drawn.astype(out[name].dtype))
    for name, factor in factors.items():
        out[name] = (out[name] * factor).astype(out[name].dtype)
    return out
```

```python
from contextlib import ExitStack

import numpy as np
import concourse.bass as bass
from concourse import mybir

ALU = mybir.AluOpType
ACT = mybir.ActivationFunctionType
AX = mybir.AxisListType
F32 = mybir.dt.float32
U32 = mybir.dt.uint32
I32 = mybir.dt.int32

P = 128
B, S, D = 4, 256, 256
E, F = 8, 704
TOKENS = B * S
TT = TOKENS // P
TB = S // P
DC = D // P
FC = (F + P - 1) // P
F_LAST = F - (FC - 1) * P
SLOT_TILES = (2 * TOKENS + E * (P - 1)) // P
SLOTS = SLOT_TILES * P
ROW = D + 4
DEST, WEIGHT = D, D + 1
NOWHERE = 1 << 20
PIECE = 256
PIECES = [min(PIECE, F - PIECE * n) for n in range((F + PIECE - 1) // PIECE)]
W1_COLS = 2 * F
W1_EXP = DC * W1_COLS
W2_EXP = FC * D
MODS = 6
SHIFT_A, SCALE_A, GATE_A, SHIFT_B, SCALE_B, GATE_B = range(MODS)
EPS = 1e-5
TINY = 1e-24
GATE_MIN = 0.25
UNROLL = 4
TURNS = (SLOT_TILES - 1) // UNROLL
PEELED_LAST = range(1 + TURNS * UNROLL, SLOT_TILES)

C_ID, C_TRI, C_ONE = 0, P, 2 * P
C_REV = 3 * P
C_STEP = C_REV + E
C_TILE = C_STEP + 8
C_TOKEN = C_TILE + 24
C_COLS = C_TOKEN + 2 * TT
R_C, R_BIN, R_BOUT, R_ROUTER = 0, B * DC, B * DC + 6, B * DC + 8
R_ALL = R_ROUTER + E * DC


def shape_constants():
    keep = np.zeros((P, C_COLS), np.float32)
    keep[:, C_ID:C_ID + P] = np.eye(P)
    keep[:, C_TRI:C_TRI + P] = np.triu(np.ones((P, P)), 1)
    keep[:, C_ONE:C_ONE + P] = 1.0
    keep[:, C_REV:C_REV + E] = E - np.arange(E)
    keep[:, C_STEP:C_STEP + 8] = P * (1 + np.arange(8))
    keep[:, C_TILE:C_TILE + 24] = np.arange(24)
    token = np.arange(TT)[None, :] * P + np.arange(P)[:, None]
    keep[:, C_TOKEN:C_TOKEN + TT] = token
    keep[:, C_TOKEN + TT:C_TOKEN + 2 * TT] = token + TOKENS
    half = D // 4
    inv = (1.0 / 10000.0 ** (np.arange(0, D // 2, 2, dtype=np.float32) / np.float32(D // 2))).astype(np.float32)
    freqs = (np.arange(S, dtype=np.float32)[:, None] * inv[None, :]).astype(np.float32)
    cos, sin = np.cos(freqs), np.sin(freqs)
    cos2, sin2 = np.repeat(cos, 2, axis=1), np.repeat(sin, 2, axis=1)
    swap = np.zeros((P, P), np.float32)
    for i in range(half):
        swap[2 * i + 1, 2 * i] = -1.0
        swap[2 * i, 2 * i + 1] = 1.0
    by_feature = np.concatenate([cos2.T, sin2.T], axis=1)
    sign = np.where(np.arange(P) % 2 == 0, -1.0, 1.0)[None, :]
    by_token = np.concatenate([cos2[:P], cos2[P:], (sin2 * sign)[:P], (sin2 * sign)[P:]], axis=1)
    return keep, swap, np.ascontiguousarray(by_feature, np.float32), by_token.astype(np.float32)


def layer(nc, X, W_in, b_in, W_out, b_out, router_w, Wg, Wu, Wd, cond, wmod,
          keep_d, swap_d, rot_feature_d, rot_token_d, out):
    ctx = ExitStack()
    with ctx:
        def sb(name, cols, dt=F32, parts=P):
            return ctx.enter_context(nc.sbuf_tensor(name, [parts, cols], dt))

        def sem(name):
            return ctx.enter_context(nc.semaphore(name))

        slots_d = nc.dram_tensor("slot_rows", (SLOTS, ROW), F32, kind="Internal").ap()
        parts_d = nc.dram_tensor("expert_parts", (2 * TOKENS, D), F32, kind="Internal").ap()
        modrow_d = nc.dram_tensor("mod_rows", (B, 3 * D), F32, kind="Internal").ap()

        bank = [ctx.enter_context(nc.psum_tensor(f"bank{i}", [P, 512], F32)) for i in range(8)]

        W1 = sb("W1", E * W1_EXP)
        W2 = sb("W2", E * W2_EXP)
        staged = [sb(f"staged{m}", FC * D) for m in range(3)]
        x = sb("x", TT * D)
        rows1 = sb("rows1", TT * ROW)
        rows2 = sb("rows2", TT * ROW)
        gate_b = sb("gate_b", B * D)
        keep = sb("keep", C_COLS)
        swap = sb("swap", P)
        small_rows = sb("small_rows", P, parts=R_ALL)
        smallT = sb("smallT", R_ALL)
        condT = sb("condT", B * DC)
        mod = sb("mod", MODS * DC * B)
        gatetmp = sb("gatetmp", 2 * DC * B)
        gate_bias = sb("gate_bias", DC * B)
        bias_q = sb("bias_q", 1)
        half_neg = sb("half_neg", 8)
        stats = sb("stats", TT * 6)
        mean_var = sb("mean_var", TT * 2)
        var_eps = sb("var_eps", TT)
        rstd = sb("rstd", TT)
        stats2 = sb("stats2", TT * 6)
        mean_var2 = sb("mean_var2", TT * 2)
        var_eps2 = sb("var_eps2", TT)
        rstd2 = sb("rstd2", TT)
        ksq = sb("ksq", TT)
        ksq_max = sb("ksq_max", TT)
        kinv = sb("kinv", TT)
        attn_sum = sb("attn_sum", B * DC)
        modrow = sb("modrow", 3 * D, parts=B)
        modtmp = sb("modtmp", 2 * D, parts=B)
        empty = sb("empty", ROW)

        def under(buf, start):
            at = [start]

            def take(n):
                at[0] += n
                return buf[:, at[0] - n:at[0]]
            return take

        early1, early2 = under(W1, 4 * W1_EXP), under(W2, 4 * W2_EXP)
        wmod_sb = early1(DC * MODS * D)
        w_inT = early1(DC * 7 * P)
        xn = early1(TB * D)
        w_in_nat = early2(6 * D)
        w_out_nat = early2(DC * D)
        bias_kv = early2(2 * D)
        rot_token = early2(4 * P)
        late1, late2 = under(W1, 6 * W1_EXP), under(W2, 6 * W2_EXP)
        hT = late1(DC * TOKENS)
        mod_b = late1(B * 2 * D)
        wA = late1(2 * DC * D)
        w_outT = late1(DC * D)
        kv = late2(2 * TB * 2 * D)
        rot_feature = late2(2 * S)
        sink = late2(D)
        ksw = late2(D)
        qT = rows2[:, 0:DC * TOKENS]
        kvp = rows1[:, 0:TT * D]
        qsin = sb("qsin", S)[:]
        xn2 = [sb(f"xn2_{k}", TB * D) for k in range(2)]
        h2T = sb("h2T", DC * S)

        xs = [staged[0][:, r * ROW:(r + 1) * ROW] for r in range(4)]
        slotT = staged[1][:, 0:D]
        sig = staged[1][:, D:D + F]
        y_sb = [staged[1][:, D + F + r * D:D + F + (r + 1) * D] for r in range(2)]
        act = staged[2][:, 0:F]
        actT = staged[2][:, F:F + FC * P]
        dest = [sb(f"dest{r}", 1, U32) for r in range(2)]
        part1 = W1[:, 0:TT * D]
        part2 = W1[:, TT * D:2 * TT * D]

        NR = TT * E
        lg = sb("lg", NR)
        rt = [sb(f"rt{i}", NR) for i in range(8)]
        chosen = sb("chosen", E + NR)
        r8 = [sb(f"r8_{i}", TT) for i in range(8)]
        cnt = sb("cnt", 8 * E)
        stp = sb("stp", E * 8)
        til = sb("til", 24 * E)
        tile_e = sb("tile_e", 24)
        tile_ei = sb("tile_ei", 24, I32)
        slot_i = [sb(f"slot_i{k}", TT, U32) for k in range(2)]

        def v3(ap, a):
            return ap.rearrange("p (a b) -> p a b", a=a)

        def turned(k):
            return keep[:, C_ID:C_ID + P] if k == P else keep[0:k, C_ID:C_ID + k]

        def modcol(m, dc, b):
            c = (m * DC + dc) * B + b
            return mod[:, c:c + 1]

        def kv_b(b):
            return kv[:, (b % 2) * TB * 2 * D:(b % 2 + 1) * TB * 2 * D]

        def kv_at(b, t):
            return kv_b(b)[:, t * 2 * D:(t + 1) * 2 * D]

        def kvp_col(b, t, dc):
            return (b * TB + t) * D + dc * P

        smallT_r = smallT[:, R_ROUTER:R_ALL].rearrange("p (e c) -> p e c", c=DC)

        names = """const_in small_in rotf_in rott_in win_in wout_in wmod_in bkv_in modrow_out modb_in gateb_in
            empty_ok empty_out half_ok smallsrc small_done smallT_ok cond_ok modT_done modrow_done bq_done mod_ok dchain
            modrow_ok turn_done turn_act turn_dve stat_ok veps_ok rstd_ok xn_ok t_done hT_ok kv_done q_done kvsb_ok
            ksq_ok kchain kvp_ok kinv_ok q0_ok qr_ok q1_ok hg_ok a_done asum_ok wA_ok y_done z_ok tz_done x2_ok stat2_ok veps2_ok
            rstd2_ok xn2_ok h2chain h2_ok th_done h2T_ok r_done expo_ok sub_ok sel_ok cnt_done tile_ok slots_ok ids1_ok ids2_ok
            slots_out gu_done sig_ok act_ok xt_done slotT_ok at_done actT_a actT_v down_done y_ok
            fin_ok finchain out_done""".split()
        s = {n: sem(n) for n in names}
        x_in = [sem(f"x_in{b}") for b in range(B)]
        w_in = [sem(f"expert_in{m}") for m in range(3)]
        xs_in = [sem(f"xs_in{r}") for r in range(4)]
        y_out = [sem(f"y_out{r}") for r in range(2)]
        part_in = [sem(f"part_in{b}") for b in range(B)]

        FIRST = 5
        GROUPS_E = 9

        def count_groups(upto, odd):
            return (upto + (0 if odd else 1)) // 2

        def w1_col(kc, m, f):
            n, w = f // PIECE, PIECES[f // PIECE]
            return kc * W1_COLS + 2 * PIECE * n + m * w + f % PIECE

        def group_moves(g):
            if g < 3:
                return [(0, 512, P, v3(w_inT, DC)[:, :, 2 * g * P:2 * g * P + 2 * P], DC)]
            if g == 3:
                return [(0, 256, P, v3(w_inT, DC)[:, :, 6 * P:7 * P], DC)]
            if g == 4:
                return [(0, 512, P, w_outT, None)]
            e, k = (g - FIRST) // GROUPS_E, (g - FIRST) % GROUPS_E
            if k < 6:
                m, n = k % 2, k // 2
                w = PIECES[n]
                c = w1_col(0, m, PIECE * n)
                return [(0, DC * w, P, v3(W1[:, e * W1_EXP:(e + 1) * W1_EXP], DC)[:, :, c:c + w], DC)]
            n = k - 6
            base = e * W2_EXP + 2 * n * D
            if n < 2:
                return [(0, 512, P, W2[:, base:base + 512], None)]
            return [(0, D, P, W2[:, base:base + D], None),
                    (D, D, F_LAST, W2[0:F_LAST, base + D:base + 2 * D], None)]

        def evacuate(copy, g):
            for c, n, parts, place, a in group_moves(g):
                src = bank[g % 2][0:parts, c:c + n]
                last = copy(place, v3(src, a) if a else src)
            return last

        EXPERT_STEP = {0: 3, 1: 4, 2: 6, 3: 7, 4: 9, 5: 10, 6: 13, 7: 14}
        STEPS = 15

        def step_experts(k):
            return [e for e in range(E) if EXPERT_STEP[e] == k]

        def groups_of(e):
            return range(FIRST + GROUPS_E * e, FIRST + GROUPS_E * (e + 1))

        def at_step(k, off):
            b = k - off
            return [b] if 0 <= b < B else []

        def turns(eng, step):
            step(0, 0)
            with eng.Fori(0, TURNS) as i:
                for c in range(1, 1 + UNROLL):
                    step(i, c)
            for j in PEELED_LAST:
                step(0, j)

        block = ctx.enter_context(nc.Block())

        @block.sync
        def _(sp):
            def load_x(b):
                sp.dma_start(v3(x[:, b * TB * D:(b + 1) * TB * D], TB),
                             X[b].rearrange("(t p) d -> p t d", p=P)).then_inc(x_in[b], 16)
            sp.dma_start(keep[:], keep_d).then_inc(s["const_in"], 16)
            load_x(0)
            sp.dma_start(v3(wmod_sb, DC), wmod.rearrange("(c p) n -> p c n", p=P)).then_inc(s["wmod_in"], 16)
            sp.dma_start(v3(w_in_nat, 6), W_in.rearrange("(c p) d -> p c d", p=P)).then_inc(s["win_in"], 16)
            for b in range(1, B):
                load_x(b)
            sp.dma_start(rot_token, rot_token_d).then_inc(s["rott_in"], 16)
            sp.dma_start(rot_feature, rot_feature_d).then_inc(s["rotf_in"], 16)
            sp.dma_start(bias_kv, b_in[D:3 * D].rearrange("(a n) -> a n", a=1).to_broadcast([P, 2 * D])).then_inc(s["bkv_in"], 16)
            sp.dma_start(v3(w_out_nat, DC), W_out.rearrange("(c p) d -> p c d", p=P)).then_inc(s["wout_in"], 16)

            def load_expert(e):
                for m, W in enumerate((Wg, Wu)):
                    if e:
                        sp.wait_ge(s["turn_done"], groups_of(e - 1)[4 + m] + 1)
                    full = (FC - 1) * P
                    sp.dma_start(v3(staged[m][:, 0:(FC - 1) * D], FC - 1),
                                 W[e, 0:full].rearrange("(c p) d -> p c d", p=P)).then_inc(w_in[m], 16)
                    sp.dma_start(staged[m][0:F_LAST, (FC - 1) * D:FC * D], W[e, full:F]).then_inc(w_in[m], 16)
                if e:
                    sp.wait_ge(s["turn_done"], groups_of(e - 1)[8] + 1)
                sp.dma_start(v3(staged[2][:, 0:DC * F], DC),
                             Wd[e].rearrange("(c p) f -> p c f", p=P)).then_inc(w_in[2], 32)

            load_expert(0)
            sp.wait_ge(s["modrow_ok"], 3)
            sp.dma_start(modrow_d, modrow[:]).then_inc(s["modrow_out"], 16)
            sp.wait_ge(s["empty_ok"], 2)
            sp.dma_start(slots_d.rearrange("(j p) n -> p j n", p=P),
                         empty[:].rearrange("p (a n) -> p a n", a=1).to_broadcast([P, SLOT_TILES, ROW])).then_inc(s["empty_out"], 16)
            load_expert(1)
            sp.wait_ge(s["modrow_out"], 16)
            for b in range(B):
                sp.dma_start(mod_b[:, b * 2 * D:(b + 1) * 2 * D],
                             modrow_d[b:b + 1, 0:2 * D].to_broadcast([P, 2 * D])).then_inc(s["modb_in"], 16)
                sp.dma_start(gate_b[:, b * D:(b + 1) * D],
                             modrow_d[b:b + 1, 2 * D:3 * D].to_broadcast([P, D])).then_inc(s["gateb_in"], 16)
            for e in range(2, E):
                load_expert(e)

            sp.wait_ge(s["slots_out"], 16 * 2 * TT)
            sp.wait_ge(s["turn_done"], FIRST + GROUPS_E * E)

            def load_slots(i, r):
                if not (isinstance(i, int) and i == 0):
                    sp.wait_ge(s["y_ok"], 4 * i + r - 3)
                sp.dma_start(xs[r], slots_d[bass.ds((4 * i + r) * P, P), :]).then_inc(xs_in[r], 16)

            for r in range(4):
                load_slots(0, r)
            with sp.Fori(1, SLOT_TILES // 4) as i:
                for r in range(4):
                    load_slots(i, r)
            for r in range(SLOT_TILES % 4):
                load_slots(SLOT_TILES // 4, r)

            for r in range(2):
                sp.wait_ge(y_out[r], 16 * len(range(r, SLOT_TILES, 2)))
            for b in range(B):
                for k, part in enumerate((part1, part2)):
                    sp.dma_start(v3(part[:, b * TB * D:(b + 1) * TB * D], TB),
                                 parts_d[k * TOKENS + b * S:k * TOKENS + (b + 1) * S].rearrange("(t p) d -> p t d", p=P)
                                 ).then_inc(part_in[b], 16)
            for b in range(B):
                sp.wait_ge(s["fin_ok"], b + 1)
                sp.dma_start(out[b].rearrange("(t p) d -> p t d", p=P),
                             v3(x[:, b * TB * D:(b + 1) * TB * D], TB)).then_inc(s["out_done"], 16)
            sp.wait_ge(s["out_done"], 16 * B)

        @block.tensor
        def _(pe):
            def turn(g):
                if g >= 2:
                    pe.wait_ge(s["turn_dve" if g % 2 else "turn_act"], count_groups(g, g % 2))
                bk = bank[g % 2]
                if g < 3:
                    for j in range(2):
                        for dc in range(DC):
                            ec = 2 * g + j
                            mm = pe.transpose(bk[:, (dc * 2 + j) * P:(dc * 2 + j + 1) * P],
                                              w_in_nat[:, ec * D + dc * P:ec * D + (dc + 1) * P], turned(P))
                elif g == 3:
                    for dc in range(DC):
                        mm = pe.matmul(bk[:, dc * P:(dc + 1) * P], w_in_nat[:, dc * P:(dc + 1) * P],
                                       swap[:], start=True, stop=True)
                elif g == 4:
                    for ec in range(DC):
                        for dc in range(DC):
                            mm = pe.transpose(bk[:, dc * D + ec * P:dc * D + (ec + 1) * P],
                                              w_out_nat[:, ec * D + dc * P:ec * D + (dc + 1) * P], turned(P))
                else:
                    e, k = (g - FIRST) // GROUPS_E, (g - FIRST) % GROUPS_E
                    if k < 6:
                        m, n = k % 2, k // 2
                        if n == 0:
                            pe.wait_ge(w_in[m], 32 * (e + 1))
                        for fc in (2 * n, 2 * n + 1):
                            rows = min(P, F - fc * P)
                            for kc in range(DC):
                                c = kc * PIECES[n] + (fc % 2) * P
                                mm = pe.transpose(bk[:, c:c + rows],
                                                  staged[m][0:rows, fc * D + kc * P:fc * D + (kc + 1) * P],
                                                  turned(rows))
                    else:
                        n = k - 6
                        if n == 0:
                            pe.wait_ge(w_in[2], 32 * (e + 1))
                        for fc in (2 * n, 2 * n + 1):
                            rows = min(P, F - fc * P)
                            for hc in range(DC):
                                c = (fc % 2) * D + hc * P
                                mm = pe.transpose(bk[0:rows, c:c + P],
                                                  staged[2][:, hc * F + fc * P:hc * F + fc * P + rows], turned(P))
                mm.then_inc(s["turn_done"], 1)

            pe.wait_ge(s["const_in"], 16)
            pe.wait_ge(s["smallsrc"], 16 * 5)
            pe.transpose(bank[2][:, 0:R_ALL], small_rows[0:R_ALL, :], turned(R_ALL)).then_inc(s["small_done"], 1)
            pe.wait_ge(s["cond_ok"], 1)
            pe.wait_ge(s["wmod_in"], 16)
            for m in range(MODS * DC):
                for kc in range(DC):
                    mm = pe.matmul(bank[3][:, m * B:(m + 1) * B],
                                   v3(wmod_sb, DC)[:, kc, m * P:(m + 1) * P],
                                   condT[:, kc * B:(kc + 1) * B], start=(kc == 0), stop=(kc == DC - 1))
            mm.then_inc(s["modT_done"], 1)
            for n, (c0, w) in enumerate(((SHIFT_B * D, 2 * D), (GATE_B * D, D))):
                for kc in range(DC):
                    mm = pe.matmul(bank[4 + n][0:B, 0:w], condT[:, kc * B:(kc + 1) * B],
                                   v3(wmod_sb, DC)[:, kc, c0:c0 + w], start=(kc == 0), stop=(kc == DC - 1))
            mm.then_inc(s["modrow_done"], 1)
            pe.wait_ge(s["win_in"], 16)
            for g in range(3):
                turn(g)
            pe.wait_ge(s["small_in"], 16)
            turn(3)
            pe.matmul(bank[6][:, 0:1], swap[:], smallT[:, R_BIN:R_BIN + 1],
                      start=True, stop=True).then_inc(s["bq_done"], 1)
            pe.wait_ge(s["wout_in"], 16)
            turn(4)
            pe.wait_ge(s["bq_done"], 1)

            for k in range(STEPS):
                for b in at_step(k, 0):
                    pe.wait_ge(s["xn_ok"], b + 1)
                    if b:
                        pe.wait_ge(s["hT_ok"], DC * b)
                    for t in range(TB):
                        for dc in range(DC):
                            mm = pe.transpose(bank[2][:, dc * S + t * P:dc * S + (t + 1) * P],
                                              xn[:, t * D + dc * P:t * D + (dc + 1) * P], turned(P))
                    mm.then_inc(s["t_done"], 1)
                for b in at_step(k, 1):
                    pe.wait_ge(s["hT_ok"], DC * (b + 1))
                    if b == 0:
                        pe.wait_ge(s["turn_act"], 3)
                        pe.wait_ge(s["turn_dve"], 2)
                        pe.wait_ge(s["mod_ok"], 1)
                        pe.wait_ge(s["modrow_ok"], 3)
                    for t in range(TB):
                        if b:
                            pe.wait_ge(s["kvsb_ok"], TB * (b - 1) + t + 1)
                        for dc in range(DC):
                            col = dc * TOKENS + b * S + t * P
                            mm = pe.matmul(bank[3 + t][:, :], hT[:, col:col + P],
                                           v3(w_inT, DC)[:, dc, D:3 * D], start=(dc == 0), stop=(dc == DC - 1))
                        mm.then_inc(s["kv_done"], 1)
                    if b:
                        pe.wait_ge(s["q0_ok"], 2 * b)
                        pe.wait_ge(s["q1_ok"], b)
                    for bk, c, w0 in ((5, 0, 0), (5, S, 6 * P), (6, 0, P)):
                        for dc in range(DC):
                            mm = pe.matmul(bank[bk][:, c:c + S], v3(w_inT, DC)[:, dc, w0:w0 + P],
                                           hT[:, dc * TOKENS + b * S:dc * TOKENS + (b + 1) * S],
                                           start=(dc == 0), stop=(dc == DC - 1))
                    mm.then_inc(s["q_done"], 1)
                for b in at_step(k, 5):
                    pe.wait_ge(s["kvp_ok"], b + 1)
                    pe.wait_ge(s["kinv_ok"], b + 1)
                    if b == 0:
                        pe.wait_ge(s["q1_ok"], B)
                    else:
                        pe.wait_ge(s["asum_ok"], b)
                    for dc in range(DC):
                        for t in range(TB):
                            mm = pe.matmul(bank[6][:, dc:dc + 1], kvp[:, kvp_col(b, t, dc):kvp_col(b, t, dc) + P],
                                           kinv[:, b * TB + t:b * TB + t + 1],
                                           start=(t == 0), stop=(t == TB - 1))
                    mm.then_inc(s["a_done"], 1)
                for b in at_step(k, 6):
                    pe.wait_ge(s["wA_ok"], DC * (b + 1))
                    pe.wait_ge(s["qr_ok"], b + 1)
                    if b:
                        pe.wait_ge(s["z_ok"], DC * b)
                    for ec in range(DC):
                        for dc in range(DC):
                            c = (b % 2) * DC * D + dc * D + ec * P
                            mm = pe.matmul(bank[7][:, ec * S:(ec + 1) * S], wA[:, c:c + P],
                                           qT[:, dc * TOKENS + b * S:dc * TOKENS + (b + 1) * S],
                                           start=(dc == 0), stop=(dc == DC - 1))
                    mm.then_inc(s["y_done"], 1)
                for b in at_step(k, 7):
                    pe.wait_ge(s["z_ok"], DC * (b + 1))
                    pe.wait_ge(s["x2_ok"], b) if b else pe.wait_ge(s["q0_ok"], 2 * B)
                    for t in range(TB):
                        for dc in range(DC):
                            mm = pe.transpose(bank[5][:, t * D + dc * P:t * D + (dc + 1) * P],
                                              hT[:, dc * TOKENS + b * S + t * P:dc * TOKENS + b * S + (t + 1) * P],
                                              turned(P))
                    mm.then_inc(s["tz_done"], 1)
                for b in at_step(k, 8):
                    pe.wait_ge(s["h2_ok"], b + 1)
                    if b:
                        pe.wait_ge(s["h2T_ok"], b)
                    for t in range(TB):
                        for dc in range(DC):
                            c = (b * TB + t) * ROW + dc * P
                            mm = pe.transpose(bank[2][:, dc * S + t * P:dc * S + (t + 1) * P],
                                              rows1[:, c:c + P], turned(P))
                    mm.then_inc(s["th_done"], 1)
                for b in at_step(k, 9):
                    pe.wait_ge(s["h2T_ok"], b + 1)
                    for t in range(TB):
                        for dc in range(DC):
                            mm = pe.matmul(bank[3][:, (b * TB + t) * E:(b * TB + t + 1) * E],
                                           h2T[:, dc * S + t * P:dc * S + (t + 1) * P],
                                           smallT_r[:, :, dc], start=(dc == 0), stop=(dc == DC - 1))
                    mm.then_inc(s["r_done"], 1)
                for e in step_experts(k):
                    for g in groups_of(e):
                        turn(g)
                if k == 13:
                    pe.wait_ge(s["sel_ok"], 1)
                    pe.matmul(bank[4][:, 0:NR], keep[:, C_TRI:C_TRI + P], chosen[:, E:E + NR], start=True, stop=False)
                    for d in range(2, TT):
                        pe.matmul(bank[4][:, d * E:NR], keep[:, C_ONE:C_ONE + P], chosen[:, E:E + (TT - d) * E],
                                  start=False, stop=False, skip_group_check=True)
                    pe.matmul(bank[4][:, 0:NR], keep[:, C_ONE:C_ONE + P], chosen[:, 0:NR], start=False,
                              stop=True)
                    for t in range(TT):
                        mm = pe.matmul(bank[7][:, 0:E], keep[:, C_ONE:C_ONE + P], chosen[:, E + t * E:E + (t + 1) * E],
                                       start=(t == 0), stop=(t == TT - 1))
                    mm.then_inc(s["cnt_done"], 1)

            def turn_slots(i, c):
                pe.wait_ge(xs_in[c % 4], 16 * (i + c // 4) + 16)
                for dc in range(DC):
                    mm = pe.transpose(bank[0][:, dc * P:(dc + 1) * P], xs[c % 4][:, dc * P:(dc + 1) * P], turned(P))
                mm.then_inc(s["xt_done"], 1)

            def gate_up(i, c):
                e = pe.value_load(tile_ei[0:1, bass.ds(4 * i + c, 1)], min_val=0, max_val=E - 1)
                pe.wait_ge(s["slotT_ok"], 4 * i + c + 1)
                for n, w in enumerate(PIECES):
                    for kc in range(DC):
                        mm = pe.matmul(bank[2 + n][:, 0:2 * w], slotT[:, kc * P:(kc + 1) * P],
                                       W1[:, bass.ds(e * W1_EXP + (kc * W1_COLS + 2 * PIECE * n), 2 * w)],
                                       start=(kc == 0), stop=(kc == DC - 1))
                    mm.then_inc(s["gu_done"], 1)
                return e

            def turn_act(i, c):
                pe.wait_ge(s["act_ok"], len(PIECES) * (4 * i + c + 1))
                for fc in range(FC):
                    rows = min(P, F - fc * P)
                    bk, col = (bank[5], fc * P) if fc < 4 else (bank[6], (fc - 4) * P)
                    mm = pe.transpose(bk[0:rows, col:col + P], act[:, fc * P:fc * P + rows], turned(P))
                    if fc == 3:
                        mm.then_inc(s["at_done"], 1)
                mm.then_inc(s["at_done"], 1)

            def down(i, c):
                e = pe.value_load(tile_ei[0:1, bass.ds(4 * i + c, 1)], min_val=0, max_val=E - 1)
                pe.wait_ge(s["actT_v"], 4 * i + c + 1)
                pe.wait_ge(s["actT_a"], 4 * i + c + 1)
                if not (isinstance(i, int) and 4 * i + c < 1):
                    pe.wait_ge(s["y_ok"], 4 * i + c)
                for fc in range(FC):
                    rows = min(P, F - fc * P)
                    mm = pe.matmul(bank[7][:, 0:D], actT[0:rows, fc * P:(fc + 1) * P],
                                   W2[0:rows, bass.ds(e * W2_EXP + fc * D, D)],
                                   start=(fc == 0), stop=(fc == FC - 1))
                mm.then_inc(s["down_done"], 1)

            pe.wait_ge(s["turn_act"], count_groups(FIRST + GROUPS_E * E, 0))
            pe.wait_ge(s["turn_dve"], count_groups(FIRST + GROUPS_E * E, 1))
            turn_slots(0, 0)
            pe.wait_ge(s["tile_ok"], 1)

            def tile_step(i, c):
                gate_up(i, c)
                if not (isinstance(i, int) and c == SLOT_TILES - 1):
                    turn_slots(i, c + 1)
                if c >= 1:
                    down(i, c - 1)
                turn_act(i, c)

            turns(pe, tile_step)
            down(0, SLOT_TILES - 1)

        @block.scalar
        def _(sc):
            sc.dma_start(small_rows[R_C:R_BIN, :], cond.rearrange("b (c p) -> (b c) p", p=P)).then_inc(s["smallsrc"], 16)
            sc.dma_start(small_rows[R_BIN:R_BOUT, :], b_in.rearrange("(c p) -> c p", p=P)).then_inc(s["smallsrc"], 16)
            sc.dma_start(small_rows[R_BOUT:R_ROUTER, :], b_out.rearrange("(c p) -> c p", p=P)).then_inc(s["smallsrc"], 16)
            sc.dma_start(small_rows[R_ROUTER:R_ALL, :], router_w.rearrange("e (c p) -> (e c) p", p=P)).then_inc(s["smallsrc"], 32)
            sc.dma_start(swap[:], swap_d).then_inc(s["small_in"], 16)
            sc.wait_ge(s["smallT_ok"], 1)
            sc.activation(v3(condT[:], DC), smallT[:, R_C:R_BIN].rearrange("p (b c) -> p c b", c=DC),
                          ACT.Silu).then_inc(s["cond_ok"], 1)

            def copy(o, i_):
                return sc.activation(o, i_, ACT.Copy)

            def turn_out(g):
                sc.wait_ge(s["turn_done"], g + 1)
                evacuate(copy, g).then_inc(s["turn_act"], 1)

            for g in range(0, FIRST, 2):
                turn_out(g)
            sc.wait_ge(s["mod_ok"], 1)
            for k in range(STEPS):
                for b in at_step(k, 0):
                    sc.wait_ge(s["t_done"], b + 1)
                    for dc in range(DC):
                        sc.activation(hT[:, dc * TOKENS + b * S:dc * TOKENS + (b + 1) * S],
                                      bank[2][:, dc * S:(dc + 1) * S], ACT.Identity,
                                      scale=modcol(SCALE_A, dc, b), bias=modcol(SHIFT_A, dc, b)).then_inc(s["hT_ok"], 1)
                for b in at_step(k, 1):
                    for t in range(TB):
                        sc.wait_ge(s["kvsb_ok"], b * TB + t + 1)
                        if b or t:
                            sc.wait_ge(s["ksq_ok"], b * TB + t)
                        sc.activation(sink, kv_at(b, t)[:, 0:D], ACT.Square,
                                      accum_out=ksq[:, b * TB + t:b * TB + t + 1]).then_inc(s["ksq_ok"], 1)
                    sc.wait_ge(s["q_done"], b + 1)
                    sc.activation(qT[:, TOKENS + b * S:TOKENS + (b + 1) * S], bank[6][:, 0:S], ACT.Identity,
                                  bias=smallT[:, R_BIN + 1:R_BIN + 2]).then_inc(s["q1_ok"], 1)
                    for dc in range(DC):
                        h = hT[:, dc * TOKENS + b * S:dc * TOKENS + (b + 1) * S]
                        sc.activation(h, h, ACT.Identity, scale=modcol(GATE_A, dc, b),
                                      bias=gate_bias[:, dc * B + b:dc * B + b + 1]).then_inc(s["hg_ok"], 1)
                for b in at_step(k, 8):
                    sc.wait_ge(s["th_done"], b + 1)
                    if b:
                        sc.wait_ge(s["r_done"], b)
                    sc.activation(h2T[:], bank[2][:], ACT.Copy).then_inc(s["h2T_ok"], 1)
                for e in step_experts(k):
                    if e == 4:
                        sc.wait_ge(s["q_done"], B)
                        sc.wait_ge(s["kvp_ok"], B)
                        sc.wait_ge(s["kvsb_ok"], B * TB)
                    if e == 6:
                        sc.wait_ge(s["tz_done"], B)
                        sc.wait_ge(s["h2_ok"], B)
                        sc.wait_ge(s["a_done"], B)
                        sc.wait_ge(s["ksq_ok"], B * TB)
                        sc.wait_ge(s["qr_ok"], B)
                    for g in groups_of(e):
                        if g % 2 == 0:
                            turn_out(g)
                if k == 12:
                    sc.wait_ge(s["sub_ok"], 1)
                    sc.activation(rt[1][:], rt[0][:], ACT.Exp).then_inc(s["expo_ok"], 1)

            def slots_out(i, c):
                sc.wait_ge(s["xt_done"], 4 * i + c + 1)
                sc.activation(slotT, bank[0][:, 0:D], ACT.Copy).then_inc(s["slotT_ok"], 1)

            def tile_step(i, c):
                for n, w in enumerate(PIECES):
                    sc.wait_ge(s["gu_done"], len(PIECES) * (4 * i + c) + n + 1)
                    sc.activation(sig[:, n * PIECE:n * PIECE + w], bank[2 + n][:, 0:w], ACT.Silu).then_inc(s["sig_ok"], 1)
                if not (isinstance(i, int) and c == SLOT_TILES - 1):
                    slots_out(i, c + 1)
                sc.wait_ge(s["at_done"], 2 * (4 * i + c) + 2)
                sc.activation(actT[:, 4 * P:5 * P], bank[6][:, 0:P], ACT.Copy)
                sc.activation(actT[0:F_LAST, 5 * P:6 * P], bank[6][0:F_LAST, P:2 * P], ACT.Copy).then_inc(s["actT_a"], 1)

            sc.wait_ge(s["turn_done"], FIRST + GROUPS_E * E)
            slots_out(0, 0)
            turns(sc, tile_step)

        def bc_mid(ap, n):
            return ap.rearrange("p (a m) -> p a m", a=1).to_broadcast([P, n, ap.shape[1]])

        def bc_last(ap, n):
            return ap.rearrange("p (m a) -> p m a", a=1).to_broadcast([P, ap.shape[1], n])

        def routing_choice(ve, link):
            ve.wait_ge(s["r_done"], B)
            link(ve.tensor_copy(lg[:], bank[3][:, 0:NR]))
            link(ve.tensor_reduce(r8[0][:], v3(lg[:], TT), AX.X, ALU.max))
            ve.tensor_tensor(v3(rt[0][:], TT), v3(lg[:], TT), bc_last(r8[0][:], E), ALU.subtract).then_inc(s["sub_ok"], 1)
            rev = bc_mid(keep[:, C_REV:C_REV + E], TT)
            cur, mx = lg, r8[0]
            for n, sel in ((0, rt[3]), (1, rt[4])):
                if n:
                    link(ve.scalar_tensor_tensor(rt[2][:], rt[3][:], -3.0e38, lg[:], ALU.mult, ALU.add))
                    link(ve.tensor_reduce(r8[1][:], v3(rt[2][:], TT), AX.X, ALU.max))
                    cur, mx = rt[2], r8[1]
                link(ve.tensor_tensor(v3(sel[:], TT), v3(cur[:], TT), bc_last(mx[:], E), ALU.is_equal))
                link(ve.tensor_tensor(v3(sel[:], TT), v3(sel[:], TT), rev, ALU.mult))
                link(ve.tensor_reduce(r8[2][:], v3(sel[:], TT), AX.X, ALU.max))
                link(ve.tensor_tensor(v3(sel[:], TT), v3(sel[:], TT), bc_last(r8[2][:], E), ALU.is_equal))
            ve.tensor_tensor(chosen[:, E:E + NR], rt[3][:], rt[4][:], ALU.add).then_inc(s["sel_ok"], 1)

        def routing_places(ve, link):
            ve.wait_ge(s["expo_ok"], 1)
            for n, sel in ((0, rt[3]), (1, rt[4])):
                link(ve.tensor_tensor(rt[6][:], rt[1][:], sel[:], ALU.mult))
                link(ve.tensor_reduce(r8[3 + n][:], v3(rt[6][:], TT), AX.X, ALU.add))
            link(ve.tensor_tensor(r8[5][:], r8[3][:], r8[4][:], ALU.add))
            link(ve.reciprocal(r8[5][:], r8[5][:]))
            rows = [v3(r[:], TT) for r in (rows1, rows2)]
            ve.wait_ge(s["y_done"], B)
            for n in range(2):
                ve.tensor_tensor(rows[n][:, :, WEIGHT], r8[3 + n][:], r8[5][:], ALU.mult)
                ve.tensor_copy(rows[n][:, :, DEST], keep[:, C_TOKEN + n * TT:C_TOKEN + (n + 1) * TT])
                ve.memset(rows[n][:, :, WEIGHT + 1:ROW], 0.0)
            ve.wait_ge(s["cnt_done"], 1)
            n_e, steps, incl, excl = cnt[:, 0:E], cnt[:, E:2 * E], cnt[:, 2 * E:3 * E], cnt[:, 3 * E:4 * E]
            link(ve.tensor_copy(n_e, bank[7][:, 0:E]))
            link(ve.tensor_tensor(v3(stp[:, 0:7 * E], E), bc_last(n_e, 7), bc_mid(keep[:, C_STEP:C_STEP + 7], E), ALU.is_gt))
            link(ve.tensor_reduce(steps, v3(stp[:, 0:7 * E], E), AX.X, ALU.add))
            link(ve.tensor_scalar(steps, steps, 1.0, None, ALU.add))
            link(ve.tensor_tensor_scan(incl, keep[:, C_ONE:C_ONE + E], steps, 0.0, ALU.mult, ALU.add))
            link(ve.tensor_tensor(excl, incl, steps, ALU.subtract))
            link(ve.tensor_scalar(excl, excl, float(P), None, ALU.mult))
            link(ve.tensor_tensor(v3(rt[7][:], TT), v3(bank[4][:, 0:NR], TT), bc_mid(excl, TT), ALU.add))
            for n, sel in ((0, rt[3]), (1, rt[4])):
                link(ve.tensor_tensor(rt[6][:], rt[7][:], sel[:], ALU.mult))
                link(ve.tensor_reduce(r8[6][:], v3(rt[6][:], TT), AX.X, ALU.add))
                ve.tensor_copy(slot_i[n][:], r8[6][:]).then_inc(s["slots_ok"], 1)
                ve.wait_ge(s["slots_ok"], n + 1)
            link(ve.tensor_tensor(v3(til[:], 24), bc_mid(incl, 24), bc_last(keep[:, C_TILE:C_TILE + 24], E), ALU.is_le))
            link(ve.tensor_reduce(tile_e[:], v3(til[:], 24), AX.X, ALU.add))
            ve.tensor_scalar(tile_ei[:], tile_e[:], float(E - 1), None, ALU.min).then_inc(s["tile_ok"], 1)

        @block.vector
        def _(ve):
            links = [0]

            def link(ins):
                links[0] += 1
                ins.then_inc(s["dchain"], 1)
                ve.wait_ge(s["dchain"], links[0])

            def turn_out(g):
                ve.wait_ge(s["turn_done"], g + 1)
                evacuate(ve.tensor_copy, g).then_inc(s["turn_dve"], 1)

            def norm_stats(b, src, st, mv, ve_, inc_st, inc_ve):
                for t in range(TB):
                    j = b * TB + t
                    ve.bn_stats(st[:, j * 6:(j + 1) * 6], src[:, j * D:(j + 1) * D]).then_inc(s[inc_st], 1)
                for t in range(TB):
                    j = b * TB + t
                    ve.wait_ge(s[inc_st], 2 * b * TB + t + 1)
                    ve.bn_aggr(mv[:, 2 * j:2 * j + 2], st[:, j * 6:(j + 1) * 6]).then_inc(s[inc_st], 1)
                ve.wait_ge(s[inc_st], 2 * (b + 1) * TB)
                ve.tensor_scalar(ve_[:, b * TB:(b + 1) * TB],
                                 mv[:, 2 * b * TB:2 * (b + 1) * TB].rearrange("p (t c) -> p t c", c=2)[:, :, 1],
                                 EPS, None, ALU.add).then_inc(s[inc_ve], 1)

            ve.wait_ge(s["small_done"], 1)
            ve.tensor_copy(smallT[:], bank[2][:, 0:R_ALL]).then_inc(s["smallT_ok"], 1)
            ve.memset(half_neg[:], -0.5).then_inc(s["half_ok"], 1)
            ve.memset(chosen[:, 0:E], 0.0)
            ve.wait_ge(x_in[0], 16)
            norm_stats(0, x, stats, mean_var, var_eps, "stat_ok", "veps_ok")

            ve.wait_ge(s["modT_done"], 1)
            link(ve.tensor_copy(mod[:], bank[3][:, 0:MODS * DC * B]))
            ga = mod[:, GATE_A * DC * B:(GATE_A + 1) * DC * B]
            sca = mod[:, SCALE_A * DC * B:(SCALE_A + 1) * DC * B]
            n8 = DC * B

            def guard(g, t1, t2):
                link(ve.tensor_scalar(t1, g, -1.0, None, ALU.mult))
                link(ve.tensor_tensor(t1, t1, g, ALU.max))
                ve.tensor_scalar(t2, g, 0.0, 2.0, ALU.is_ge, ALU.mult)
                link(ve.tensor_scalar(t1, t1, GATE_MIN, None, ALU.max))
                return ve.scalar_tensor_tensor(g, t2, -1.0, t1, ALU.add, ALU.mult)

            link(guard(ga, gatetmp[:, 0:n8], gatetmp[:, n8:2 * n8]))
            link(ve.tensor_scalar(sca, sca, 1.0, None, ALU.add))
            for dc in range(DC):
                ins = ve.tensor_scalar(gate_bias[:, dc * B:(dc + 1) * B], ga[:, dc * B:(dc + 1) * B],
                                       smallT[:, R_BOUT + dc:R_BOUT + dc + 1], None, ALU.mult)
            ins.then_inc(s["mod_ok"], 1)
            ve.wait_ge(s["modrow_done"], 1)
            ve.tensor_copy(modrow[:, 0:D], bank[4][0:B, 0:D]).then_inc(s["modrow_ok"], 1)
            ve.tensor_scalar(modrow[:, D:2 * D], bank[4][0:B, D:2 * D], 1.0, None, ALU.add).then_inc(s["modrow_ok"], 1)
            link(ve.tensor_copy(modrow[:, 2 * D:3 * D], bank[5][0:B, 0:D]))
            guard(modrow[:, 2 * D:3 * D], modtmp[:, 0:D], modtmp[:, D:2 * D]).then_inc(s["modrow_ok"], 1)
            turn_out(1)
            turn_out(3)
            ve.wait_ge(s["bq_done"], 1)
            link(ve.tensor_copy(bias_q[:], bank[6][:, 0:1]))

            for k in range(STEPS):
                for b in at_step(k, 0):
                    ve.wait_ge(s["rstd_ok"], b + 1)
                    if b:
                        ve.wait_ge(s["t_done"], b)
                    for t in range(TB):
                        j = b * TB + t
                        ins = ve.tensor_scalar(xn[:, t * D:(t + 1) * D], x[:, j * D:(j + 1) * D],
                                               mean_var[:, 2 * j:2 * j + 1], rstd[:, j:j + 1],
                                               ALU.subtract, ALU.mult)
                    ins.then_inc(s["xn_ok"], 1)
                for b in at_step(k, -1):
                    if b:
                        ve.wait_ge(x_in[b], 16)
                        norm_stats(b, x, stats, mean_var, var_eps, "stat_ok", "veps_ok")
                for b in at_step(k, 1):
                    if b == 0:
                        ve.wait_ge(s["bkv_in"], 16)
                        ve.wait_ge(s["rotf_in"], 16)
                    for t in range(TB):
                        ve.wait_ge(s["kv_done"], b * TB + t + 1)
                        if b >= 2:
                            ve.wait_ge(s["kvp_ok"], b - 1)
                        ve.tensor_tensor(kv_at(b, t), bank[3 + t][:], bias_kv, ALU.add).then_inc(s["kvsb_ok"], 1)
                    ve.wait_ge(s["q_done"], b + 1)
                    if b:
                        ve.wait_ge(s["qr_ok"], b)
                    ve.scalar_tensor_tensor(qsin, bank[5][:, S:2 * S], bias_q[:, 0:1], rot_feature[:, S:2 * S],
                                            ALU.add, ALU.mult).then_inc(s["q0_ok"], 1)
                    ve.scalar_tensor_tensor(qT[:, b * S:(b + 1) * S], bank[5][:, 0:S], smallT[:, R_BIN:R_BIN + 1],
                                            rot_feature[:, 0:S], ALU.add, ALU.mult).then_inc(s["q0_ok"], 1)
                for b in at_step(k, 5):
                    ve.wait_ge(s["a_done"], b + 1)
                    ve.tensor_copy(attn_sum[:, b * DC:(b + 1) * DC], bank[6][:, 0:DC]).then_inc(s["asum_ok"], 1)
                    ve.wait_ge(s["asum_ok"], b + 1)
                    if b >= 2:
                        ve.wait_ge(s["y_done"], b - 1)
                    for dc in range(DC):
                        c = (b % 2) * DC * D + dc * D
                        ve.tensor_scalar(wA[:, c:c + D], w_outT[:, dc * D:(dc + 1) * D],
                                         attn_sum[:, b * DC + dc:b * DC + dc + 1], None, ALU.mult).then_inc(s["wA_ok"], 1)
                for b in at_step(k, 6):
                    ve.wait_ge(s["y_done"], b + 1)
                    ve.wait_ge(s["hg_ok"], DC * (b + 1))
                    for dc in range(DC):
                        h = hT[:, dc * TOKENS + b * S:dc * TOKENS + (b + 1) * S]
                        ve.scalar_tensor_tensor(h, bank[7][:, dc * S:(dc + 1) * S], modcol(GATE_A, dc, b), h,
                                                ALU.mult, ALU.add).then_inc(s["z_ok"], 1)
                for b in at_step(k, 7):
                    ve.wait_ge(s["tz_done"], b + 1)
                    xb = x[:, b * TB * D:(b + 1) * TB * D]
                    ve.tensor_tensor(xb, bank[5][:], xb, ALU.add).then_inc(s["x2_ok"], 1)
                    ve.wait_ge(s["x2_ok"], b + 1)
                    norm_stats(b, x, stats2, mean_var2, var_eps2, "stat2_ok", "veps2_ok")
                for e in step_experts(k):
                    if e == 4:
                        ve.wait_ge(s["q_done"], B)
                        ve.wait_ge(s["kvp_ok"], B)
                        ve.wait_ge(s["kvsb_ok"], B * TB)
                    if e == 6:
                        ve.wait_ge(s["z_ok"], DC * B)
                        ve.wait_ge(s["wA_ok"], DC * B)
                        ve.wait_ge(s["q0_ok"], 2 * B)
                        ve.wait_ge(s["tz_done"], B)
                        ve.wait_ge(s["h2_ok"], B)
                        ve.wait_ge(s["a_done"], B)
                        ve.wait_ge(s["ksq_ok"], B * TB)
                        ve.wait_ge(s["qr_ok"], B)
                    for g in groups_of(e):
                        if g % 2 == 1:
                            turn_out(g)
                for b in at_step(k, 7):
                    ve.wait_ge(s["rstd2_ok"], b + 1)
                    if b >= 2:
                        ve.wait_ge(s["h2_ok"], b - 1)
                    for t in range(TB):
                        j = b * TB + t
                        ins = ve.tensor_scalar(xn2[b % 2][:, t * D:(t + 1) * D], x[:, j * D:(j + 1) * D],
                                               mean_var2[:, 2 * j:2 * j + 1], rstd2[:, j:j + 1],
                                               ALU.subtract, ALU.mult)
                    ins.then_inc(s["xn2_ok"], 1)
                if k == 12:
                    routing_choice(ve, link)
                if k == 13:
                    routing_places(ve, link)

            def mult_pieces(i, c):
                for n, w in enumerate(PIECES):
                    ve.wait_ge(s["sig_ok"], len(PIECES) * (4 * i + c) + n + 1)
                    ve.tensor_tensor(act[:, n * PIECE:n * PIECE + w], bank[2 + n][:, w:2 * w],
                                     sig[:, n * PIECE:n * PIECE + w], ALU.mult).then_inc(s["act_ok"], 1)

            def result(i, c, r):
                ve.wait_ge(s["down_done"], 4 * i + c + 1)
                if not (isinstance(i, int) and 4 * i + c < 2):
                    ve.wait_ge(y_out[r], 16 * (2 * i + c // 2))
                ve.tensor_copy(dest[r][:], xs[c % 4][:, DEST:DEST + 1])
                ve.tensor_scalar(y_sb[r], bank[7][:, 0:D], xs[c % 4][:, WEIGHT:WEIGHT + 1], None,
                                 ALU.mult).then_inc(s["y_ok"], 1)

            def tile_step(i, c):
                mult_pieces(i, c)
                if c >= 1:
                    result(i, c - 1, (c - 1) % 2)
                ve.wait_ge(s["at_done"], 2 * (4 * i + c) + 1)
                ve.tensor_copy(actT[:, 0:4 * P], bank[5][:]).then_inc(s["actT_v"], 1)

            turns(ve, tile_step)
            result(0, SLOT_TILES - 1, (SLOT_TILES - 1) % 2)

            ve.wait_ge(s["gateb_in"], 16 * B)
            for b in range(B):
                cols = slice(b * TB * D, (b + 1) * TB * D)
                ve.wait_ge(part_in[b], 32)
                link(ve.tensor_tensor(part1[:, cols], part1[:, cols], part2[:, cols], ALU.add))
                g3 = gate_b[:, b * D:(b + 1) * D].rearrange("p (a d) -> p a d", a=1).to_broadcast([P, TB, D])
                link(ve.tensor_tensor(v3(part1[:, cols], TB), v3(part1[:, cols], TB), g3, ALU.mult))
                ve.tensor_tensor(x[:, cols], part1[:, cols], x[:, cols], ALU.add).then_inc(s["fin_ok"], 1)

        @block.gpsimd
        def _(po):
            po.memset(empty[:], 0.0).then_inc(s["empty_ok"], 1)
            po.wait_ge(s["empty_ok"], 1)
            po.memset(empty[:, DEST:DEST + 1], float(NOWHERE)).then_inc(s["empty_ok"], 1)
            po.wait_ge(s["half_ok"], 1)
            kc_ = [0]

            def klink(ins):
                kc_[0] += 1
                ins.then_inc(s["kchain"], 1)
                po.wait_ge(s["kchain"], kc_[0])

            for k in range(-1, STEPS):
                for b in at_step(k, -1):
                    po.wait_ge(s["veps_ok"], b + 1)
                    po.tensor_tensor(rstd[:, b * TB:(b + 1) * TB], var_eps[:, b * TB:(b + 1) * TB],
                                     half_neg[:, 0:TB], ALU.pow).then_inc(s["rstd_ok"], 1)
                for b in at_step(k, 1):
                    if b == 0:
                        po.wait_ge(s["rott_in"], 16)
                    po.wait_ge(s["q0_ok"], 2 * (b + 1))
                    q = qT[:, b * S:(b + 1) * S]
                    po.tensor_tensor(q, q, qsin, ALU.add).then_inc(s["qr_ok"], 1)
                    po.wait_ge(s["kvsb_ok"], TB * (b + 1))
                    kvb = v3(kv_b(b), TB)
                    k1 = kvb[:, :, 0:P]
                    flip = kvb[:, :, 0:P]
                    kr = v3(ksw, TB)
                    sinr = v3(rot_token[:, 2 * P:4 * P], TB)
                    po.wait_ge(s["ksq_ok"], TB * (b + 1))
                    if b:
                        po.wait_ge(s["kvp_ok"], b)
                    for t in range(TB):
                        kt = kv_at(b, t)[:, 0:P].rearrange("p (i two) -> p i two", two=2)[:, :, ::-1]
                        ins = po.tensor_tensor(ksw[:, t * P:(t + 1) * P].rearrange("p (i two) -> p i two", two=2), kt,
                                               rot_token[:, (2 + t) * P:(3 + t) * P].rearrange("p (i two) -> p i two", two=2),
                                               ALU.mult)
                    klink(ins)
                    klink(po.tensor_tensor(k1, k1, v3(rot_token[:, 0:2 * P], TB), ALU.mult))
                    klink(po.tensor_tensor(k1, k1, kr, ALU.add))
                    po.tensor_tensor(v3(kvp[:, b * TB * D:(b + 1) * TB * D], TB), kvb[:, :, 0:D], kvb[:, :, D:2 * D],
                                     ALU.mult).then_inc(s["kvp_ok"], 1)
                    cols = slice(b * TB, (b + 1) * TB)
                    klink(po.tensor_scalar(ksq_max[:, cols], ksq[:, cols], TINY, None, ALU.max))
                    po.tensor_tensor(kinv[:, cols], ksq_max[:, cols], half_neg[:, 0:TB], ALU.pow).then_inc(s["kinv_ok"], 1)
                for b in at_step(k, 7):
                    if b == 0:
                        po.wait_ge(s["modb_in"], 16 * B)
                    po.wait_ge(s["veps2_ok"], b + 1)
                    po.tensor_tensor(rstd2[:, b * TB:(b + 1) * TB], var_eps2[:, b * TB:(b + 1) * TB],
                                     half_neg[:, 0:TB], ALU.pow).then_inc(s["rstd2_ok"], 1)
                    po.wait_ge(s["xn2_ok"], b + 1)
                    xn_b = v3(xn2[b % 2][:], TB)
                    sc_b = bc_mid(mod_b[:, b * 2 * D + D:(b + 1) * 2 * D], TB)
                    sh_b = bc_mid(mod_b[:, b * 2 * D:b * 2 * D + D], TB)
                    klink(po.tensor_tensor(xn_b, xn_b, sc_b, ALU.mult))
                    rb = rows1[:, b * TB * ROW:(b + 1) * TB * ROW].rearrange("p (t r) -> p t r", t=TB)[:, :, 0:D]
                    po.tensor_tensor(rb, xn_b, sh_b, ALU.add).then_inc(s["h2_ok"], 1)
            po.wait_ge(s["y_done"], B)
            po.wait_ge(s["h2_ok"], B)
            r1, r2 = (v3(r[:], TT)[:, :, 0:D] for r in (rows1, rows2))
            po.tensor_scalar(r2, r1, 1.0, 0.0, ALU.mult, ALU.add).then_inc(s["ids2_ok"], 1)
            po.wait_ge(s["ids2_ok"], 1)
            po.wait_ge(s["empty_out"], 16)
            for n, rows in enumerate((rows1, rows2)):
                po.wait_ge(s["slots_ok"], n + 1)
                for t in range(TT):
                    po.indirect_dma_start(slots_d, bass.IndirectOffsetOnAxis(slot_i[n][:, t:t + 1], 0),
                                          rows[:, t * ROW:(t + 1) * ROW], None,
                                          bounds_check=SLOTS - 1, oob_is_err=False).then_inc(s["slots_out"], 16)

            last_part = po.to_reg(2 * TOKENS - 1)

            for j in range(SLOT_TILES):
                r = j % 2
                po.wait_ge(s["y_ok"], j + 1)
                po.indirect_dma_start(parts_d, bass.IndirectOffsetOnAxis(dest[r][:, 0:1], 0), y_sb[r], None,
                                      bounds_check=last_part, oob_is_err=False).then_inc(y_out[r], 16)


_ORDER = ["L0_attn_X", "L0_attn_W_in", "L0_attn_b_in", "L0_attn_W_out", "L0_attn_b_out", "L0_ffn_router_w",
          "L0_ffn_Wg", "L0_ffn_Wu", "L0_ffn_Wd", "L0_c", "L0_wmod"]


def kernel(**inputs):
    import concourse.bacc as bacc
    from concourse.bass_utils import run_bass_kernel_spmd

    nc = bacc.Bacc("TRN2", target_bir_lowering=False, num_devices=1)
    arrays = {name: np.ascontiguousarray(inputs[name]) for name in _ORDER}
    for name, a in zip(("keep", "swap", "rot_feature", "rot_token"), shape_constants()):
        arrays[name] = a
    args = [nc.dram_tensor(f"in_{n}", a.shape, F32, kind="ExternalInput").ap() for n, a in arrays.items()]
    out = nc.dram_tensor("out", (B, S, D), F32, kind="ExternalOutput").ap()
    layer(nc, *args, out)
    r = run_bass_kernel_spmd(nc, [{f"in_{n}": a for n, a in arrays.items()}], core_ids=[0])
    return r.results[0]["out"]
```

```python
from contextlib import ExitStack

import numpy as np
import concourse.bass as bass
from concourse import mybir

ALU = mybir.AluOpType
ACT = mybir.ActivationFunctionType
AX = mybir.AxisListType
F32 = mybir.dt.float32
U32 = mybir.dt.uint32
I32 = mybir.dt.int32

P = 128
B, S, D = 4, 256, 256
E, F = 8, 704
TOKENS = B * S
TT = TOKENS // P
TB = S // P
DC = D // P
FC = (F + P - 1) // P
F_LAST = F - (FC - 1) * P
SLOT_TILES = (2 * TOKENS + E * (P - 1)) // P
SLOTS = SLOT_TILES * P
ROW = D + 4
DEST, WEIGHT = D, D + 1
NOWHERE = 1 << 20
PIECE = 256
PIECES = [min(PIECE, F - PIECE * n) for n in range((F + PIECE - 1) // PIECE)]
W1_COLS = 2 * F
W1_EXP = DC * W1_COLS
W2_EXP = FC * D
MODS = 6
SHIFT_A, SCALE_A, GATE_A, SHIFT_B, SCALE_B, GATE_B = range(MODS)
STAGED = 4
EPS = 1e-5
TINY = 1e-24
GATE_MIN = 0.25
UNROLL = 4
TURNS = (SLOT_TILES - 1) // UNROLL
PEELED_LAST = range(1 + TURNS * UNROLL, SLOT_TILES)

C_ID, C_TRI, C_ONE = 0, P, 2 * P
C_REV = 3 * P
C_STEP = C_REV + E
C_TILE = C_STEP + 8
C_TOKEN = C_TILE + 24
C_COLS = C_TOKEN + 2 * TT
R_C, R_BIN, R_BOUT, R_ROUTER = 0, B * DC, B * DC + 6, B * DC + 8
R_ALL = R_ROUTER + E * DC
T_BOUT = R_BOUT - R_BIN


def shape_constants():
    keep = np.zeros((P, C_COLS), np.float32)
    keep[:, C_ID:C_ID + P] = np.eye(P)
    keep[:, C_TRI:C_TRI + P] = np.triu(np.ones((P, P)), 1)
    keep[:, C_ONE:C_ONE + P] = 1.0
    keep[:, C_REV:C_REV + E] = E - np.arange(E)
    keep[:, C_STEP:C_STEP + 8] = P * (1 + np.arange(8))
    keep[:, C_TILE:C_TILE + 24] = np.arange(24)
    token = np.arange(TT)[None, :] * P + np.arange(P)[:, None]
    keep[:, C_TOKEN:C_TOKEN + TT] = token
    keep[:, C_TOKEN + TT:C_TOKEN + 2 * TT] = token + TOKENS
    half = D // 4
    inv = (1.0 / 10000.0 ** (np.arange(0, D // 2, 2, dtype=np.float32) / np.float32(D // 2))).astype(np.float32)
    freqs = (np.arange(S, dtype=np.float32)[:, None] * inv[None, :]).astype(np.float32)
    cos, sin = np.cos(freqs), np.sin(freqs)
    cos2, sin2 = np.repeat(cos, 2, axis=1), np.repeat(sin, 2, axis=1)
    swap = np.zeros((P, P), np.float32)
    for i in range(half):
        swap[2 * i + 1, 2 * i] = -1.0
        swap[2 * i, 2 * i + 1] = 1.0
    by_feature = np.concatenate([cos2.T, sin2.T], axis=1)
    sign = np.where(np.arange(P) % 2 == 0, -1.0, 1.0)[None, :]
    by_token = np.concatenate([cos2[:P], cos2[P:], (sin2 * sign)[:P], (sin2 * sign)[P:]], axis=1)
    return keep, swap, np.ascontiguousarray(by_feature, np.float32), by_token.astype(np.float32)


def layer(nc, X, W_in, b_in, W_out, b_out, router_w, Wg, Wu, Wd, cond, wmod,
          keep_d, swap_d, rot_feature_d, rot_token_d, out):
    ctx = ExitStack()
    with ctx:
        def sb(name, cols, dt=F32, parts=P):
            return ctx.enter_context(nc.sbuf_tensor(name, [parts, cols], dt))

        def sem(name):
            return ctx.enter_context(nc.semaphore(name))

        slots_d = nc.dram_tensor("slot_rows", (SLOTS, ROW), F32, kind="Internal").ap()
        parts_d = nc.dram_tensor("expert_parts", (2 * TOKENS, D), F32, kind="Internal").ap()
        modrow_d = nc.dram_tensor("mod_rows", (B, 3 * D), F32, kind="Internal").ap()

        bank = [ctx.enter_context(nc.psum_tensor(f"bank{i}", [P, 512], F32)) for i in range(8)]

        W1 = sb("W1", E * W1_EXP)
        W2 = sb("W2", E * W2_EXP)
        staged = [sb(f"staged{m}", FC * D) for m in range(STAGED)]
        x = sb("x", TT * D)
        rows1 = sb("rows1", TT * ROW)
        rows2 = sb("rows2", TT * ROW)
        gate_b = sb("gate_b", B * D)
        keep = sb("keep", C_COLS)
        swap = sb("swap", P)
        small_rows = sb("cond_rows", P, parts=R_BIN)
        rest_rows = sb("bias_router_rows", P, parts=R_ALL - R_BIN)
        smallT = sb("smallT", R_ALL - R_BIN)
        condT = sb("condT", B * DC)
        mod = sb("mod", 3 * DC * B)
        gatetmp = sb("gatetmp", 2 * DC * B)
        gate_bias = sb("gate_bias", DC * B)
        bias_q = sb("bias_q", 1)
        half_neg = sb("half_neg", 8)
        stats = sb("stats", TT * 6)
        mean_var = sb("mean_var", TT * 2)
        var_eps = sb("var_eps", TT)
        rstd = sb("rstd", TT)
        stats2 = sb("stats2", TT * 6)
        mean_var2 = sb("mean_var2", TT * 2)
        var_eps2 = sb("var_eps2", TT)
        rstd2 = sb("rstd2", TT)
        ksq = sb("ksq", TT)
        ksq_max = sb("ksq_max", TT)
        kinv = sb("kinv", TT)
        attn_sum = sb("attn_sum", B * DC)
        modrow = sb("modrow", MODS * D, parts=B)
        scratch = sb("scratch", 2 * D)
        modtmp = scratch[0:B, :]
        empty = sb("empty", ROW)

        def under(buf, start):
            at = [start]

            def take(n):
                at[0] += n
                return buf[:, at[0] - n:at[0]]
            return take

        early1, early2 = under(W1, 4 * W1_EXP), under(W2, 4 * W2_EXP)
        wmod_sb = early1(DC * MODS * D)
        w_inT = early1(DC * 7 * P)
        xn = [early1(TB * D), wmod_sb[:, 2 * MODS * D - TB * D:]]
        w_in_nat = early2(6 * D)
        w_out_nat = early2(DC * D)
        bias_kv = early2(2 * D)
        rot_token = early2(4 * P)
        late1, late2 = under(W1, 6 * W1_EXP), under(W2, 6 * W2_EXP)
        hT = late1(DC * TOKENS)
        mod_b = late1(B * 2 * D)
        wA = late1(2 * DC * D)
        w_outT = late1(DC * D)
        kv = late2(2 * TB * 2 * D)
        rot_feature = late2(2 * S)
        sink = late2(D)
        ksw = late2(D)
        qT = rows2[:, 0:DC * TOKENS]
        kvp = rows1[:, 0:TT * D]
        qsin = sb("qsin", S)[:]
        h2T = kv[:, 0:DC * S]
        diff = [kv[:, DC * S + t * D:DC * S + (t + 1) * D] for t in range(TB)]

        xs = [staged[0][:, r * ROW:(r + 1) * ROW] for r in range(4)]
        slotT = staged[1][:, 0:D]
        sig = staged[1][:, D:D + F]
        y_sb = [staged[1][:, D + F + r * D:D + F + (r + 1) * D] for r in range(2)]
        act = staged[2][:, 0:F]
        actT = staged[2][:, F:F + FC * P]
        dest = [sb(f"dest{r}", 1, U32) for r in range(2)]
        part1 = W1[:, 0:TT * D]
        part2 = W1[:, TT * D:2 * TT * D]

        NR = TT * E
        SUM0 = 8 * E
        lg = sb("lg", NR)
        rt = [sb(f"rt{i}", NR) for i in range(8)]
        chosen = sb("chosen", NR)
        tiles_sum = [scratch[:, i * P:(i + 1) * P] for i in range(3)]
        r8 = [sb(f"r8_{i}", TT) for i in range(8)]
        cnt = sb("cnt", 8 * E)
        stp = sb("stp", E * 8)
        til = sb("til", 24 * E)
        tile_e = sb("tile_e", 24)
        tile_ei = sb("tile_ei", 24, I32)
        slot_i = [sb(f"slot_i{k}", TT, U32) for k in range(2)]

        def v3(ap, a):
            return ap.rearrange("p (a b) -> p a b", a=a)

        def turned(k):
            return keep[:, C_ID:C_ID + P] if k == P else keep[0:k, C_ID:C_ID + k]

        def modcol(m, dc, b):
            c = (m * DC + dc) * B + b
            return mod[:, c:c + 1]

        def kv_b(b):
            return kv[:, (b % 2) * TB * 2 * D:(b % 2 + 1) * TB * 2 * D]

        def kv_at(b, t):
            return kv_b(b)[:, t * 2 * D:(t + 1) * 2 * D]

        def kvp_col(b, t, dc):
            return (b * TB + t) * D + dc * P

        smallT_r = smallT[:, R_ROUTER - R_BIN:R_ALL - R_BIN].rearrange("p (e c) -> p e c", c=DC)

        names = """const_in small_in rotf_in rott_in win_in wout_in bkv_in modrow_out modb_in gateb_in
            empty_ok empty_out half_ok smallsrc small_done smallT_ok cond_ok condsrc cond_done modT_done modrow_done bq_done modA_ok mod_ok dchain
            rowsA_ok row_ga_ok rowsB_ok turn_done turn_act turn_dve stat_ok veps_ok rstd_ok xn_ok t_done hT_ok kv_done q_done kvsb_ok
            ksq_ok kchain kvp_ok kinv_ok q0_ok qr_ok q1_ok hg_ok a_done asum_ok wA_ok y_done z_ok tz_done x2_ok stat2_ok veps2_ok
            rstd2_ok diff_ok h2_ok th_done h2T_ok r_done expo_ok sub_ok sel_ok sums_ok cnt_done tile_ok slots_ok ids2_ok
            slots_out gu_done sig_ok act_ok xt_done slotT_ok at_done actT_a actT_v down_done y_ok
            fin_ok finchain out_done""".split()
        s = {n: sem(n) for n in names}
        x_in = [sem(f"x_in{b}") for b in range(B)]
        staged_in = [sem(f"staged_in{r}") for r in range(STAGED)]
        xs_in = [sem(f"xs_in{r}") for r in range(4)]
        y_out = [sem(f"y_out{r}") for r in range(2)]
        wmod_in = [sem(f"wmod_in{n}") for n in range(3)]
        part_in = [sem(f"part_in{b}") for b in range(B)]

        FIRST = 5
        GROUPS_E = 9

        STEPS = 11
        STEP_GROUPS = [0, 1, 2, 2, 2, 4, 6, 6, 6, 5, 3]
        ROUTE_GROUPS = 10
        ALL_GROUPS = FIRST + GROUPS_E * E
        route_first = FIRST + sum(STEP_GROUPS[:-1])
        route_mid = FIRST + sum(STEP_GROUPS)
        route_last = route_mid + ROUTE_GROUPS

        def by_act(g):
            return g % 2 == 0 or route_first <= g < route_last

        def wait_turned(eng, upto):
            eng.wait_ge(s["turn_act"], sum(by_act(g) for g in range(upto)))
            eng.wait_ge(s["turn_dve"], sum(not by_act(g) for g in range(upto)))

        def wait_out(eng, g):
            n = sum(by_act(h) == by_act(g) for h in range(g + 1))
            eng.wait_ge(s["turn_act" if by_act(g) else "turn_dve"], n)

        def step_groups(k):
            at = FIRST + sum(STEP_GROUPS[:k])
            return range(at, at + STEP_GROUPS[k])

        def matrix_place(e, m):
            return (3 * e + m) % STAGED, (3 * e + m) // STAGED

        def last_group(q):
            e, m = divmod(q, 3)
            return FIRST + GROUPS_E * e + (4 + m if m < 2 else 8)

        def wait_places(eng, g):
            for e in (4, 6):
                late = [h for h in range(FIRST + GROUPS_E * e, ALL_GROUPS) if by_act(h) == by_act(g)]
                if g != late[0]:
                    continue
                if e == 4:
                    eng.wait_ge(s["q_done"], B)
                    eng.wait_ge(s["kvsb_ok"], B * TB)
                    eng.wait_ge(s["kvp_ok"], B)
                    eng.wait_ge(s["modrow_done"], 3)
                else:
                    eng.wait_ge(s["r_done"], B)

        def w1_col(kc, m, f):
            n, w = f // PIECE, PIECES[f // PIECE]
            return kc * W1_COLS + 2 * PIECE * n + m * w + f % PIECE

        def group_moves(g):
            if g < 3:
                return [(0, 512, P, v3(w_inT, DC)[:, :, 2 * g * P:2 * g * P + 2 * P], DC)]
            if g == 3:
                return [(0, 256, P, v3(w_inT, DC)[:, :, 6 * P:7 * P], DC)]
            if g == 4:
                return [(0, 512, P, w_outT, None)]
            e, k = (g - FIRST) // GROUPS_E, (g - FIRST) % GROUPS_E
            if k < 6:
                m, n = k % 2, k // 2
                w = PIECES[n]
                c = w1_col(0, m, PIECE * n)
                return [(0, DC * w, P, v3(W1[:, e * W1_EXP:(e + 1) * W1_EXP], DC)[:, :, c:c + w], DC)]
            n = k - 6
            base = e * W2_EXP + 2 * n * D
            if n < 2:
                return [(0, 512, P, W2[:, base:base + 512], None)]
            return [(0, D, P, W2[:, base:base + D], None),
                    (D, D, F_LAST, W2[0:F_LAST, base + D:base + 2 * D], None)]

        def evacuate(copy, g):
            for c, n, parts, place, a in group_moves(g):
                src = bank[g % 2][0:parts, c:c + n]
                last = copy(place, v3(src, a) if a else src)
            return last

        def at_step(k, off):
            b = k - off
            return [b] if 0 <= b < B else []

        def turns(eng, step):
            step(0, 0)
            with eng.Fori(0, TURNS) as i:
                for c in range(1, 1 + UNROLL):
                    step(i, c)
            for j in PEELED_LAST:
                step(0, j)

        block = ctx.enter_context(nc.Block())

        @block.sync
        def _(sp):
            def load_x(b):
                sp.dma_start(v3(x[:, b * TB * D:(b + 1) * TB * D], TB),
                             X[b].rearrange("(t p) d -> p t d", p=P)).then_inc(x_in[b], 16)

            def load_wmod(n):
                sp.dma_start(v3(wmod_sb, DC)[:, :, 2 * n * D:2 * (n + 1) * D],
                             wmod.rearrange("(c p) n -> p c n", p=P)[:, :, 2 * n * D:2 * (n + 1) * D]
                             ).then_inc(wmod_in[n], 16)
            sp.dma_start(keep[:], keep_d).then_inc(s["const_in"], 16)
            load_wmod(0)
            load_x(0)
            sp.dma_start(v3(w_in_nat, 6), W_in.rearrange("(c p) d -> p c d", p=P)).then_inc(s["win_in"], 16)
            load_wmod(1)
            load_x(1)
            load_wmod(2)
            sp.dma_start(bias_kv, b_in[D:3 * D].rearrange("(a n) -> a n", a=1).to_broadcast([P, 2 * D])).then_inc(s["bkv_in"], 16)
            sp.dma_start(rot_feature, rot_feature_d).then_inc(s["rotf_in"], 16)
            sp.dma_start(rot_token, rot_token_d).then_inc(s["rott_in"], 16)
            sp.dma_start(v3(w_out_nat, DC), W_out.rearrange("(c p) d -> p c d", p=P)).then_inc(s["wout_in"], 16)
            for b in range(2, B):
                load_x(b)

            def load_matrix(q):
                e, m = divmod(q, 3)
                r = q % STAGED
                if q >= STAGED:
                    sp.wait_ge(s["turn_done"], last_group(q - STAGED) + 1)
                if m < 2:
                    W = (Wg, Wu)[m]
                    full = (FC - 1) * P
                    sp.dma_start(v3(staged[r][:, 0:(FC - 1) * D], FC - 1),
                                 W[e, 0:full].rearrange("(c p) d -> p c d", p=P)).then_inc(staged_in[r], 16)
                    sp.dma_start(staged[r][0:F_LAST, (FC - 1) * D:FC * D], W[e, full:F]).then_inc(staged_in[r], 16)
                else:
                    sp.dma_start(v3(staged[r][:, 0:DC * F], DC),
                                 Wd[e].rearrange("(c p) f -> p c f", p=P)).then_inc(staged_in[r], 32)

            load_matrix(0)
            sp.wait_ge(s["rowsB_ok"], 4)
            sp.dma_start(modrow_d, modrow[:, SHIFT_B * D:MODS * D]).then_inc(s["modrow_out"], 16)
            for q in range(1, STAGED):
                load_matrix(q)
            sp.wait_ge(s["modrow_out"], 16)
            for b in range(B):
                sp.dma_start(mod_b[:, b * 2 * D:(b + 1) * 2 * D],
                             modrow_d[b:b + 1, 0:2 * D].to_broadcast([P, 2 * D])).then_inc(s["modb_in"], 16)
                sp.dma_start(gate_b[:, b * D:(b + 1) * D],
                             modrow_d[b:b + 1, 2 * D:3 * D].to_broadcast([P, D])).then_inc(s["gateb_in"], 16)
            sp.wait_ge(s["empty_ok"], 2)
            sp.dma_start(slots_d.rearrange("(j p) n -> p j n", p=P),
                         empty[:].rearrange("p (a n) -> p a n", a=1).to_broadcast([P, SLOT_TILES, ROW])).then_inc(s["empty_out"], 16)
            for q in range(STAGED, 3 * E):
                load_matrix(q)

            sp.wait_ge(s["slots_out"], 16 * 2 * TT)
            sp.wait_ge(s["turn_done"], ALL_GROUPS)

            def load_slots(i, r):
                if not (isinstance(i, int) and i == 0):
                    sp.wait_ge(s["y_ok"], 4 * i + r - 3)
                sp.dma_start(xs[r], slots_d[bass.ds((4 * i + r) * P, P), :]).then_inc(xs_in[r], 16)

            for r in range(4):
                load_slots(0, r)
            with sp.Fori(1, SLOT_TILES // 4) as i:
                for r in range(4):
                    load_slots(i, r)
            for r in range(SLOT_TILES % 4):
                load_slots(SLOT_TILES // 4, r)

            for r in range(2):
                sp.wait_ge(y_out[r], 16 * len(range(r, SLOT_TILES, 2)))
            for b in range(B):
                for k, part in enumerate((part1, part2)):
                    sp.dma_start(v3(part[:, b * TB * D:(b + 1) * TB * D], TB),
                                 parts_d[k * TOKENS + b * S:k * TOKENS + (b + 1) * S].rearrange("(t p) d -> p t d", p=P)
                                 ).then_inc(part_in[b], 16)
            for b in range(B):
                sp.wait_ge(s["fin_ok"], b + 1)
                sp.dma_start(out[b].rearrange("(t p) d -> p t d", p=P),
                             v3(x[:, b * TB * D:(b + 1) * TB * D], TB)).then_inc(s["out_done"], 16)
            sp.wait_ge(s["out_done"], 16 * B)

        @block.tensor
        def _(pe):
            def turn(g):
                if g >= 2:
                    wait_out(pe, g - 2)
                bk = bank[g % 2]
                if g < 3:
                    for j in range(2):
                        for dc in range(DC):
                            ec = 2 * g + j
                            mm = pe.transpose(bk[:, (dc * 2 + j) * P:(dc * 2 + j + 1) * P],
                                              w_in_nat[:, ec * D + dc * P:ec * D + (dc + 1) * P], turned(P))
                elif g == 3:
                    for dc in range(DC):
                        mm = pe.matmul(bk[:, dc * P:(dc + 1) * P], w_in_nat[:, dc * P:(dc + 1) * P],
                                       swap[:], start=True, stop=True)
                elif g == 4:
                    for ec in range(DC):
                        for dc in range(DC):
                            mm = pe.transpose(bk[:, dc * D + ec * P:dc * D + (ec + 1) * P],
                                              w_out_nat[:, ec * D + dc * P:ec * D + (dc + 1) * P], turned(P))
                else:
                    e, k = (g - FIRST) // GROUPS_E, (g - FIRST) % GROUPS_E
                    if k < 6:
                        m, n = k % 2, k // 2
                        r, uses = matrix_place(e, m)
                        if n == 0:
                            pe.wait_ge(staged_in[r], 32 * (uses + 1))
                        for fc in (2 * n, 2 * n + 1):
                            rows = min(P, F - fc * P)
                            for kc in range(DC):
                                c = kc * PIECES[n] + (fc % 2) * P
                                mm = pe.transpose(bk[:, c:c + rows],
                                                  staged[r][0:rows, fc * D + kc * P:fc * D + (kc + 1) * P],
                                                  turned(rows))
                    else:
                        n = k - 6
                        r, uses = matrix_place(e, 2)
                        if n == 0:
                            pe.wait_ge(staged_in[r], 32 * (uses + 1))
                        for fc in (2 * n, 2 * n + 1):
                            rows = min(P, F - fc * P)
                            for hc in range(DC):
                                c = (fc % 2) * D + hc * P
                                mm = pe.transpose(bk[0:rows, c:c + P],
                                                  staged[r][:, hc * F + fc * P:hc * F + fc * P + rows], turned(P))
                mm.then_inc(s["turn_done"], 1)

            def mod_rows(n):
                pe.wait_ge(wmod_in[n], 16)
                for kc in range(DC):
                    mm = pe.matmul(bank[3 + n][0:B, :], condT[:, kc * B:(kc + 1) * B],
                                   v3(wmod_sb, DC)[:, kc, 2 * n * D:2 * (n + 1) * D],
                                   start=(kc == 0), stop=(kc == DC - 1))
                mm.then_inc(s["modrow_done"], 1)

            def turn_mod(m0, m1, rows_ok, rows):
                pe.wait_ge(rows_ok, rows)
                for c in range(m0 * DC, m1 * DC):
                    mm = pe.transpose(bank[6][:, c * B:(c + 1) * B], modrow[:, c * P:(c + 1) * P], turned(B))
                mm.then_inc(s["modT_done"], 1)

            pe.wait_ge(s["const_in"], 16)
            pe.wait_ge(s["condsrc"], 16)
            pe.transpose(bank[2][:, 0:R_BIN], small_rows[0:R_BIN, :], turned(R_BIN)).then_inc(s["cond_done"], 1)
            pe.wait_ge(s["cond_ok"], 1)
            mod_rows(0)
            pe.wait_ge(s["smallsrc"], 16 * 4)
            pe.transpose(bank[2][:, R_BIN:R_ALL], rest_rows[:, :], turned(R_ALL - R_BIN)).then_inc(s["small_done"], 1)
            pe.wait_ge(s["win_in"], 16)
            turn(0)
            turn_mod(SHIFT_A, GATE_A, s["rowsA_ok"], 2)
            turn(1)

            for k in range(STEPS):
                for b in at_step(k, 0):
                    pe.wait_ge(s["xn_ok"], b + 1)
                    if b:
                        pe.wait_ge(s["hT_ok"], DC * b)
                    else:
                        pe.wait_ge(s["smallT_ok"], 1)
                    for t in range(TB):
                        for dc in range(DC):
                            mm = pe.transpose(bank[2][:, dc * S + t * P:dc * S + (t + 1) * P],
                                              xn[b % 2][:, t * D + dc * P:t * D + (dc + 1) * P], turned(P))
                    mm.then_inc(s["t_done"], 1)
                if k == 0:
                    turn(2)
                    pe.wait_ge(s["small_in"], 16)
                    turn(3)
                    pe.wait_ge(s["modA_ok"], 1)
                    pe.matmul(bank[6][:, 3 * DC * B:3 * DC * B + 1], swap[:], smallT[:, 0:1],
                              start=True, stop=True).then_inc(s["bq_done"], 1)
                    mod_rows(1)
                    mod_rows(2)
                    pe.wait_ge(s["wout_in"], 16)
                    turn(4)
                    turn_mod(GATE_A, SHIFT_B, s["row_ga_ok"], 1)
                for b in at_step(k, 3):
                    pe.wait_ge(s["kvp_ok"], b + 1)
                    pe.wait_ge(s["kinv_ok"], b + 1)
                    pe.wait_ge(s["q1_ok"], min(k - 1, B))
                    if b:
                        pe.wait_ge(s["asum_ok"], b)
                    for dc in range(DC):
                        for t in range(TB):
                            mm = pe.matmul(bank[6][:, S + dc:S + dc + 1], kvp[:, kvp_col(b, t, dc):kvp_col(b, t, dc) + P],
                                           kinv[:, b * TB + t:b * TB + t + 1],
                                           start=(t == 0), stop=(t == TB - 1))
                    mm.then_inc(s["a_done"], 1)
                for b in at_step(k, 1):
                    pe.wait_ge(s["hT_ok"], DC * (b + 1))
                    if b == 0:
                        wait_turned(pe, FIRST)
                        pe.wait_ge(s["rowsB_ok"], 3)
                        pe.wait_ge(s["mod_ok"], 1)
                    for t in range(TB):
                        if b:
                            pe.wait_ge(s["kvsb_ok"], TB * (b - 1) + t + 1)
                        for dc in range(DC):
                            col = dc * TOKENS + b * S + t * P
                            mm = pe.matmul(bank[3 + t][:, :], hT[:, col:col + P],
                                           v3(w_inT, DC)[:, dc, D:3 * D], start=(dc == 0), stop=(dc == DC - 1))
                        mm.then_inc(s["kv_done"], 1)
                    if b:
                        pe.wait_ge(s["q0_ok"], 2 * b)
                        pe.wait_ge(s["q1_ok"], b)
                    if k >= 3:
                        pe.wait_ge(s["asum_ok"], k - 2)
                    for bk, c, w0 in ((5, 0, 0), (5, S, 6 * P), (6, 0, P)):
                        for dc in range(DC):
                            mm = pe.matmul(bank[bk][:, c:c + S], v3(w_inT, DC)[:, dc, w0:w0 + P],
                                           hT[:, dc * TOKENS + b * S:dc * TOKENS + (b + 1) * S],
                                           start=(dc == 0), stop=(dc == DC - 1))
                    mm.then_inc(s["q_done"], 1)
                for b in at_step(k, 4):
                    pe.wait_ge(s["wA_ok"], DC * (b + 1))
                    pe.wait_ge(s["qr_ok"], b + 1)
                    if b:
                        pe.wait_ge(s["z_ok"], DC * b)
                    for ec in range(DC):
                        for dc in range(DC):
                            c = (b % 2) * DC * D + dc * D + ec * P
                            mm = pe.matmul(bank[7][:, ec * S:(ec + 1) * S], wA[:, c:c + P],
                                           qT[:, dc * TOKENS + b * S:dc * TOKENS + (b + 1) * S],
                                           start=(dc == 0), stop=(dc == DC - 1))
                    mm.then_inc(s["y_done"], 1)
                for b in at_step(k, 5):
                    pe.wait_ge(s["z_ok"], DC * (b + 1))
                    if b:
                        pe.wait_ge(s["x2_ok"], b)
                    else:
                        pe.wait_ge(s["q0_ok"], 2 * B)
                    for t in range(TB):
                        for dc in range(DC):
                            mm = pe.transpose(bank[5][:, t * D + dc * P:t * D + (dc + 1) * P],
                                              hT[:, dc * TOKENS + b * S + t * P:dc * TOKENS + b * S + (t + 1) * P],
                                              turned(P))
                    mm.then_inc(s["tz_done"], 1)
                for b in at_step(k, 6):
                    pe.wait_ge(s["h2_ok"], b + 1)
                    if b:
                        pe.wait_ge(s["h2T_ok"], b)
                    for t in range(TB):
                        for dc in range(DC):
                            c = (b * TB + t) * ROW + dc * P
                            mm = pe.transpose(bank[2][:, dc * S + t * P:dc * S + (t + 1) * P],
                                              rows1[:, c:c + P], turned(P))
                    mm.then_inc(s["th_done"], 1)
                for b in at_step(k, 7):
                    pe.wait_ge(s["h2T_ok"], b + 1)
                    for t in range(TB):
                        for dc in range(DC):
                            mm = pe.matmul(bank[3][:, (b * TB + t) * E:(b * TB + t + 1) * E],
                                           h2T[:, dc * S + t * P:dc * S + (t + 1) * P],
                                           smallT_r[:, :, dc], start=(dc == 0), stop=(dc == DC - 1))
                    mm.then_inc(s["r_done"], 1)
                for g in step_groups(k):
                    turn(g)
                if k == STEPS - 1:
                    pe.wait_ge(s["sel_ok"], 1)
                    pe.matmul(bank[4][:, 0:NR], keep[:, C_TRI:C_TRI + P], chosen[:], start=True, stop=False)
                    pe.wait_ge(s["sums_ok"], 1)
                    pe.matmul(bank[4][:, 0:NR], keep[:, C_ONE:C_ONE + P],
                              tiles_sum[2][:, SUM0 - E:SUM0 - E + NR], start=False, stop=True)
                    mm = pe.matmul(bank[7][:, 0:E], keep[:, C_ONE:C_ONE + P],
                                   tiles_sum[2][:, SUM0 + NR - E:SUM0 + NR], start=True, stop=True)
                    mm.then_inc(s["cnt_done"], 1)
                    for g in range(route_mid, ALL_GROUPS):
                        turn(g)

            def turn_slots(i, c):
                pe.wait_ge(xs_in[c % 4], 16 * (i + c // 4) + 16)
                for dc in range(DC):
                    mm = pe.transpose(bank[0][:, dc * P:(dc + 1) * P], xs[c % 4][:, dc * P:(dc + 1) * P], turned(P))
                mm.then_inc(s["xt_done"], 1)

            def gate_up(i, c):
                e = pe.value_load(tile_ei[0:1, bass.ds(4 * i + c, 1)], min_val=0, max_val=E - 1)
                pe.wait_ge(s["slotT_ok"], 4 * i + c + 1)
                for n, w in enumerate(PIECES):
                    for kc in range(DC):
                        mm = pe.matmul(bank[2 + n][:, 0:2 * w], slotT[:, kc * P:(kc + 1) * P],
                                       W1[:, bass.ds(e * W1_EXP + (kc * W1_COLS + 2 * PIECE * n), 2 * w)],
                                       start=(kc == 0), stop=(kc == DC - 1))
                    mm.then_inc(s["gu_done"], 1)
                return e

            def turn_act(i, c):
                pe.wait_ge(s["act_ok"], len(PIECES) * (4 * i + c + 1))
                for fc in range(FC):
                    rows = min(P, F - fc * P)
                    bk, col = (bank[5], fc * P) if fc < 4 else (bank[6], (fc - 4) * P)
                    mm = pe.transpose(bk[0:rows, col:col + P], act[:, fc * P:fc * P + rows], turned(P))
                    if fc == 3:
                        mm.then_inc(s["at_done"], 1)
                mm.then_inc(s["at_done"], 1)

            def down(i, c):
                e = pe.value_load(tile_ei[0:1, bass.ds(4 * i + c, 1)], min_val=0, max_val=E - 1)
                pe.wait_ge(s["actT_v"], 4 * i + c + 1)
                pe.wait_ge(s["actT_a"], 4 * i + c + 1)
                if not (isinstance(i, int) and 4 * i + c < 1):
                    pe.wait_ge(s["y_ok"], 4 * i + c)
                for fc in range(FC):
                    rows = min(P, F - fc * P)
                    mm = pe.matmul(bank[7][:, 0:D], actT[0:rows, fc * P:(fc + 1) * P],
                                   W2[0:rows, bass.ds(e * W2_EXP + fc * D, D)],
                                   start=(fc == 0), stop=(fc == FC - 1))
                mm.then_inc(s["down_done"], 1)

            wait_turned(pe, ALL_GROUPS)
            turn_slots(0, 0)
            pe.wait_ge(s["tile_ok"], 1)

            def tile_step(i, c):
                gate_up(i, c)
                if not (isinstance(i, int) and c == SLOT_TILES - 1):
                    turn_slots(i, c + 1)
                if c >= 1:
                    down(i, c - 1)
                turn_act(i, c)

            turns(pe, tile_step)
            down(0, SLOT_TILES - 1)

        @block.scalar
        def _(sc):
            sc.dma_start(small_rows[:], cond.rearrange("b (c p) -> (b c) p", p=P)).then_inc(s["condsrc"], 16)
            r0 = R_BOUT - R_BIN
            r1 = R_ROUTER - R_BIN
            sc.dma_start(rest_rows[0:r0, :], b_in.rearrange("(c p) -> c p", p=P)).then_inc(s["smallsrc"], 16)
            sc.dma_start(rest_rows[r0:r1, :], b_out.rearrange("(c p) -> c p", p=P)).then_inc(s["smallsrc"], 16)
            sc.dma_start(rest_rows[r1:, :], router_w.rearrange("e (c p) -> (e c) p", p=P)).then_inc(s["smallsrc"], 32)
            sc.dma_start(swap[:], swap_d).then_inc(s["small_in"], 16)
            sc.wait_ge(s["cond_done"], 1)
            sc.activation(v3(condT[:], DC), bank[2][:, 0:R_BIN].rearrange("p (b c) -> p c b", c=DC),
                          ACT.Silu).then_inc(s["cond_ok"], 1)

            def copy(o, i_):
                return sc.activation(o, i_, ACT.Copy)

            def turn_out(g):
                sc.wait_ge(s["turn_done"], g + 1)
                evacuate(copy, g).then_inc(s["turn_act"], 1)

            turn_out(0)
            for k in range(STEPS):
                for b in at_step(k, 0):
                    sc.wait_ge(s["t_done"], b + 1)
                    if b == 0:
                        sc.wait_ge(s["modA_ok"], 1)
                    for dc in range(DC):
                        sc.activation(hT[:, dc * TOKENS + b * S:dc * TOKENS + (b + 1) * S],
                                      bank[2][:, dc * S:(dc + 1) * S], ACT.Identity,
                                      scale=modcol(SCALE_A, dc, b), bias=modcol(SHIFT_A, dc, b)).then_inc(s["hT_ok"], 1)
                if k == 0:
                    turn_out(2)
                    for m in (SHIFT_B, SCALE_B, GATE_B):
                        sc.wait_ge(s["modrow_done"], m // 2 + 1)
                        sc.wait_ge(s["row_ga_ok"], 1)
                        sc.activation(modrow[:, m * D:(m + 1) * D], bank[3 + m // 2][0:B, m % 2 * D:(m % 2 + 1) * D],
                                      ACT.Identity, bias=1.0 if m == SCALE_B else 0.0).then_inc(s["rowsB_ok"], 1)
                    turn_out(4)
                for b in at_step(k, 1):
                    if b == 0:
                        sc.wait_ge(s["mod_ok"], 1)
                    for t in range(TB):
                        sc.wait_ge(s["kvsb_ok"], b * TB + t + 1)
                        if b or t:
                            sc.wait_ge(s["ksq_ok"], b * TB + t)
                        sc.activation(sink, kv_at(b, t)[:, 0:D], ACT.Square,
                                      accum_out=ksq[:, b * TB + t:b * TB + t + 1]).then_inc(s["ksq_ok"], 1)
                    sc.wait_ge(s["q_done"], b + 1)
                    sc.activation(qT[:, TOKENS + b * S:TOKENS + (b + 1) * S], bank[6][:, 0:S], ACT.Identity,
                                  bias=smallT[:, 1:2]).then_inc(s["q1_ok"], 1)
                    for dc in range(DC):
                        h = hT[:, dc * TOKENS + b * S:dc * TOKENS + (b + 1) * S]
                        sc.activation(h, h, ACT.Identity, scale=modcol(GATE_A, dc, b),
                                      bias=gate_bias[:, dc * B + b:dc * B + b + 1]).then_inc(s["hg_ok"], 1)
                for b in at_step(k, 6):
                    sc.wait_ge(s["th_done"], b + 1)
                    if b:
                        sc.wait_ge(s["r_done"], b)
                    else:
                        sc.wait_ge(s["kvp_ok"], B - 1)
                    sc.activation(h2T, bank[2][:], ACT.Copy).then_inc(s["h2T_ok"], 1)
                for g in step_groups(k):
                    if k == STEPS - 1 and g == step_groups(k)[2]:
                        sc.wait_ge(s["sub_ok"], 1)
                        sc.activation(rt[1][:], rt[0][:], ACT.Exp).then_inc(s["expo_ok"], 1)
                    if by_act(g):
                        wait_places(sc, g)
                        turn_out(g)
            for g in range(route_mid, ALL_GROUPS):
                if by_act(g):
                    wait_places(sc, g)
                    turn_out(g)

            def slots_out(i, c):
                sc.wait_ge(s["xt_done"], 4 * i + c + 1)
                sc.activation(slotT, bank[0][:, 0:D], ACT.Copy).then_inc(s["slotT_ok"], 1)

            def tile_step(i, c):
                for n, w in enumerate(PIECES):
                    sc.wait_ge(s["gu_done"], len(PIECES) * (4 * i + c) + n + 1)
                    sc.activation(sig[:, n * PIECE:n * PIECE + w], bank[2 + n][:, 0:w], ACT.Silu).then_inc(s["sig_ok"], 1)
                if not (isinstance(i, int) and c == SLOT_TILES - 1):
                    slots_out(i, c + 1)
                sc.wait_ge(s["at_done"], 2 * (4 * i + c) + 2)
                sc.activation(actT[:, 4 * P:5 * P], bank[6][:, 0:P], ACT.Copy)
                sc.activation(actT[0:F_LAST, 5 * P:6 * P], bank[6][0:F_LAST, P:2 * P], ACT.Copy).then_inc(s["actT_a"], 1)

            sc.wait_ge(s["turn_done"], ALL_GROUPS)
            slots_out(0, 0)
            turns(sc, tile_step)

        def bc_mid(ap, n):
            return ap.rearrange("p (a m) -> p a m", a=1).to_broadcast([P, n, ap.shape[1]])

        def bc_last(ap, n):
            return ap.rearrange("p (m a) -> p m a", a=1).to_broadcast([P, ap.shape[1], n])

        def routing_choice(ve, link):
            for i in range(3):
                ve.memset(tiles_sum[i][:, 0:SUM0], 0.0)
            ve.wait_ge(s["r_done"], B)
            link(ve.tensor_copy(lg[:], bank[3][:, 0:NR]))
            link(ve.tensor_reduce(r8[0][:], v3(lg[:], TT), AX.X, ALU.max))
            ve.tensor_tensor(v3(rt[0][:], TT), v3(lg[:], TT), bc_last(r8[0][:], E), ALU.subtract).then_inc(s["sub_ok"], 1)
            rev = bc_mid(keep[:, C_REV:C_REV + E], TT)
            cur, mx = lg, r8[0]
            for n, sel in ((0, rt[3]), (1, rt[4])):
                if n:
                    link(ve.scalar_tensor_tensor(rt[2][:], rt[3][:], -3.0e38, lg[:], ALU.mult, ALU.add))
                    link(ve.tensor_reduce(r8[1][:], v3(rt[2][:], TT), AX.X, ALU.max))
                    cur, mx = rt[2], r8[1]
                link(ve.tensor_tensor(v3(sel[:], TT), v3(cur[:], TT), bc_last(mx[:], E), ALU.is_equal))
                link(ve.tensor_tensor(v3(sel[:], TT), v3(sel[:], TT), rev, ALU.mult))
                link(ve.tensor_reduce(r8[2][:], v3(sel[:], TT), AX.X, ALU.max))
                link(ve.tensor_tensor(v3(sel[:], TT), v3(sel[:], TT), bc_last(r8[2][:], E), ALU.is_equal))
            ve.tensor_tensor(chosen[:], rt[3][:], rt[4][:], ALU.add).then_inc(s["sel_ok"], 1)
            ve.wait_ge(s["sel_ok"], 1)
            for i, d in enumerate((1, 2, 4)):
                if i == 0:
                    link(ve.tensor_copy(tiles_sum[2][:, SUM0:SUM0 + NR], chosen[:]))
                prev, this = tiles_sum[(i + 2) % 3], tiles_sum[i]
                ins = ve.tensor_tensor(this[:, SUM0:SUM0 + NR], prev[:, SUM0:SUM0 + NR],
                                       prev[:, SUM0 - d * E:SUM0 - d * E + NR], ALU.add)
                if i < 2:
                    link(ins)
                else:
                    ins.then_inc(s["sums_ok"], 1)

        def routing_places(ve, link):
            ve.wait_ge(s["expo_ok"], 1)
            for n, sel in ((0, rt[3]), (1, rt[4])):
                link(ve.tensor_tensor(rt[6][:], rt[1][:], sel[:], ALU.mult))
                link(ve.tensor_reduce(r8[3 + n][:], v3(rt[6][:], TT), AX.X, ALU.add))
            link(ve.tensor_tensor(r8[5][:], r8[3][:], r8[4][:], ALU.add))
            link(ve.reciprocal(r8[5][:], r8[5][:]))
            rows = [v3(r[:], TT) for r in (rows1, rows2)]
            ve.wait_ge(s["y_done"], B)
            for n in range(2):
                ve.tensor_tensor(rows[n][:, :, WEIGHT], r8[3 + n][:], r8[5][:], ALU.mult)
                ve.tensor_copy(rows[n][:, :, DEST], keep[:, C_TOKEN + n * TT:C_TOKEN + (n + 1) * TT])
                ve.memset(rows[n][:, :, WEIGHT + 1:ROW], 0.0)
            ve.wait_ge(s["cnt_done"], 1)
            n_e, steps, incl, excl = cnt[:, 0:E], cnt[:, E:2 * E], cnt[:, 2 * E:3 * E], cnt[:, 3 * E:4 * E]
            link(ve.tensor_copy(n_e, bank[7][:, 0:E]))
            link(ve.tensor_tensor(v3(stp[:, 0:7 * E], E), bc_last(n_e, 7), bc_mid(keep[:, C_STEP:C_STEP + 7], E), ALU.is_gt))
            link(ve.tensor_reduce(steps, v3(stp[:, 0:7 * E], E), AX.X, ALU.add))
            link(ve.tensor_scalar(steps, steps, 1.0, None, ALU.add))
            link(ve.tensor_tensor_scan(incl, keep[:, C_ONE:C_ONE + E], steps, 0.0, ALU.mult, ALU.add))
            link(ve.tensor_tensor(excl, incl, steps, ALU.subtract))
            link(ve.tensor_scalar(excl, excl, float(P), None, ALU.mult))
            link(ve.tensor_tensor(v3(rt[7][:], TT), v3(bank[4][:, 0:NR], TT), bc_mid(excl, TT), ALU.add))
            for n, sel in ((0, rt[3]), (1, rt[4])):
                link(ve.tensor_tensor(rt[6][:], rt[7][:], sel[:], ALU.mult))
                link(ve.tensor_reduce(r8[6][:], v3(rt[6][:], TT), AX.X, ALU.add))
                ve.tensor_copy(slot_i[n][:], r8[6][:]).then_inc(s["slots_ok"], 1)
                ve.wait_ge(s["slots_ok"], n + 1)
            link(ve.tensor_tensor(v3(til[:], 24), bc_mid(incl, 24), bc_last(keep[:, C_TILE:C_TILE + 24], E), ALU.is_le))
            link(ve.tensor_reduce(tile_e[:], v3(til[:], 24), AX.X, ALU.add))
            ve.tensor_scalar(tile_ei[:], tile_e[:], float(E - 1), None, ALU.min).then_inc(s["tile_ok"], 1)

        @block.vector
        def _(ve):
            links = [0]

            def link(ins):
                links[0] += 1
                ins.then_inc(s["dchain"], 1)
                ve.wait_ge(s["dchain"], links[0])

            def turn_out(g):
                ve.wait_ge(s["turn_done"], g + 1)
                evacuate(ve.tensor_copy, g).then_inc(s["turn_dve"], 1)

            def norm_stats(b, src, st, mv, ve_, inc_st, inc_ve):
                for t in range(TB):
                    j = b * TB + t
                    ve.bn_stats(st[:, j * 6:(j + 1) * 6], src[:, j * D:(j + 1) * D]).then_inc(s[inc_st], 1)
                for t in range(TB):
                    j = b * TB + t
                    ve.wait_ge(s[inc_st], 2 * b * TB + t + 1)
                    ve.bn_aggr(mv[:, 2 * j:2 * j + 2], st[:, j * 6:(j + 1) * 6]).then_inc(s[inc_st], 1)
                ve.wait_ge(s[inc_st], 2 * (b + 1) * TB)
                ve.tensor_scalar(ve_[:, b * TB:(b + 1) * TB],
                                 mv[:, 2 * b * TB:2 * (b + 1) * TB].rearrange("p (t c) -> p t c", c=2)[:, :, 1],
                                 EPS, None, ALU.add).then_inc(s[inc_ve], 1)

            def normed(b):
                ve.wait_ge(s["rstd_ok"], b + 1)
                if b == 1:
                    ve.wait_ge(s["modrow_done"], 3)
                if b >= 2:
                    ve.wait_ge(s["t_done"], b - 1)
                for t in range(TB):
                    j = b * TB + t
                    ins = ve.tensor_scalar(xn[b % 2][:, t * D:(t + 1) * D], x[:, j * D:(j + 1) * D],
                                           mean_var[:, 2 * j:2 * j + 1], rstd[:, j:j + 1],
                                           ALU.subtract, ALU.mult)
                ins.then_inc(s["xn_ok"], 1)

            ve.memset(half_neg[:], -0.5).then_inc(s["half_ok"], 1)
            ve.wait_ge(x_in[0], 16)
            norm_stats(0, x, stats, mean_var, var_eps, "stat_ok", "veps_ok")
            normed(0)

            def mod_row(m, out_row):
                ve.wait_ge(s["modrow_done"], m // 2 + 1)
                src = bank[3 + m // 2][0:B, m % 2 * D:(m % 2 + 1) * D]
                if m == SCALE_A:
                    return ve.tensor_scalar(out_row, src, 1.0, None, ALU.add)
                return ve.tensor_copy(out_row, src)

            def guard(g, t1, t2):
                link(ve.tensor_scalar(t1, g, -1.0, None, ALU.mult))
                link(ve.tensor_tensor(t1, t1, g, ALU.max))
                ve.tensor_scalar(t2, g, 0.0, 2.0, ALU.is_ge, ALU.mult)
                link(ve.tensor_scalar(t1, t1, GATE_MIN, None, ALU.max))
                return ve.scalar_tensor_tensor(g, t2, -1.0, t1, ALU.add, ALU.mult)

            for m in (SHIFT_A, SCALE_A):
                mod_row(m, modrow[:, m * D:(m + 1) * D]).then_inc(s["rowsA_ok"], 1)
            ve.wait_ge(s["small_done"], 1)
            ve.tensor_copy(smallT[:], bank[2][:, R_BIN:R_ALL]).then_inc(s["smallT_ok"], 1)
            n16, n8 = GATE_A * DC * B, DC * B
            ve.wait_ge(s["modT_done"], 1)
            ve.tensor_copy(mod[:, 0:n16], bank[6][:, 0:n16]).then_inc(s["modA_ok"], 1)
            turn_out(1)
            ve.wait_ge(x_in[1], 16)
            norm_stats(1, x, stats, mean_var, var_eps, "stat_ok", "veps_ok")
            turn_out(3)
            ve.wait_ge(s["bq_done"], 1)
            link(ve.tensor_copy(bias_q[:], bank[6][:, 3 * DC * B:3 * DC * B + 1]))
            mod_row(GATE_A, modrow[:, GATE_A * D:(GATE_A + 1) * D]).then_inc(s["row_ga_ok"], 1)
            normed(1)
            ve.wait_ge(s["modT_done"], 2)
            ga = mod[:, n16:n16 + n8]
            link(ve.tensor_copy(ga, bank[6][:, n16:n16 + n8]))
            link(guard(ga, gatetmp[:, 0:n8], gatetmp[:, n8:2 * n8]))
            for dc in range(DC):
                ins = ve.tensor_scalar(gate_bias[:, dc * B:(dc + 1) * B], ga[:, dc * B:(dc + 1) * B],
                                       smallT[:, T_BOUT + dc:T_BOUT + dc + 1], None, ALU.mult)
            ins.then_inc(s["mod_ok"], 1)

            for k in range(STEPS):
                for b in at_step(k, -1):
                    if b > 1:
                        normed(b)
                for b in at_step(k, 3):
                    ve.wait_ge(s["a_done"], b + 1)
                    ve.tensor_copy(attn_sum[:, b * DC:(b + 1) * DC], bank[6][:, S:S + DC]).then_inc(s["asum_ok"], 1)
                    ve.wait_ge(s["asum_ok"], b + 1)
                    if b >= 2:
                        ve.wait_ge(s["y_done"], b - 1)
                    for dc in range(DC):
                        c = (b % 2) * DC * D + dc * D
                        ve.tensor_scalar(wA[:, c:c + D], w_outT[:, dc * D:(dc + 1) * D],
                                         attn_sum[:, b * DC + dc:b * DC + dc + 1], None, ALU.mult).then_inc(s["wA_ok"], 1)
                for b in at_step(k, 1):
                    if b == 0:
                        ve.wait_ge(s["bkv_in"], 16)
                        ve.wait_ge(s["rotf_in"], 16)
                    for t in range(TB):
                        ve.wait_ge(s["kv_done"], b * TB + t + 1)
                        if b >= 2:
                            ve.wait_ge(s["kvp_ok"], b - 1)
                        ve.tensor_tensor(kv_at(b, t), bank[3 + t][:], bias_kv, ALU.add).then_inc(s["kvsb_ok"], 1)
                    ve.wait_ge(s["q_done"], b + 1)
                    if b:
                        ve.wait_ge(s["qr_ok"], b)
                    ve.scalar_tensor_tensor(qsin, bank[5][:, S:2 * S], bias_q[:, 0:1], rot_feature[:, S:2 * S],
                                            ALU.add, ALU.mult).then_inc(s["q0_ok"], 1)
                    ve.scalar_tensor_tensor(qT[:, b * S:(b + 1) * S], bank[5][:, 0:S], smallT[:, 0:1],
                                            rot_feature[:, 0:S], ALU.add, ALU.mult).then_inc(s["q0_ok"], 1)
                for b in at_step(k, -2):
                    ve.wait_ge(x_in[b], 16)
                    norm_stats(b, x, stats, mean_var, var_eps, "stat_ok", "veps_ok")
                if k == 1:
                    ve.wait_ge(s["rowsB_ok"], 3)
                    guard(modrow[:, GATE_B * D:MODS * D], modtmp[:, 0:D], modtmp[:, D:2 * D]).then_inc(s["rowsB_ok"], 1)
                for b in at_step(k, 4):
                    ve.wait_ge(s["y_done"], b + 1)
                    ve.wait_ge(s["hg_ok"], DC * (b + 1))
                    for dc in range(DC):
                        h = hT[:, dc * TOKENS + b * S:dc * TOKENS + (b + 1) * S]
                        ve.scalar_tensor_tensor(h, bank[7][:, dc * S:(dc + 1) * S], modcol(GATE_A, dc, b), h,
                                                ALU.mult, ALU.add).then_inc(s["z_ok"], 1)
                for b in at_step(k, 5):
                    ve.wait_ge(s["tz_done"], b + 1)
                    xb = x[:, b * TB * D:(b + 1) * TB * D]
                    ve.tensor_tensor(xb, bank[5][:], xb, ALU.add).then_inc(s["x2_ok"], 1)
                    ve.wait_ge(s["x2_ok"], b + 1)
                    norm_stats(b, x, stats2, mean_var2, var_eps2, "stat2_ok", "veps2_ok")
                    if b == 0:
                        ve.wait_ge(s["modb_in"], 16 * B)
                        ve.wait_ge(s["kvp_ok"], B - 1)
                    else:
                        ve.wait_ge(s["h2_ok"], b)
                    for t in range(TB):
                        j = b * TB + t
                        ve.scalar_tensor_tensor(diff[t], x[:, j * D:(j + 1) * D], mean_var2[:, 2 * j:2 * j + 1],
                                                mod_b[:, b * 2 * D + D:(b + 1) * 2 * D],
                                                ALU.subtract, ALU.mult).then_inc(s["diff_ok"], 1)
                for g in step_groups(k):
                    if not by_act(g):
                        wait_places(ve, g)
                        turn_out(g)
                for b in at_step(k, 5):
                    ve.wait_ge(s["rstd2_ok"], b + 1)
                    for t in range(TB):
                        j = b * TB + t
                        ve.wait_ge(s["diff_ok"], j + 1)
                        ins = ve.scalar_tensor_tensor(rows1[:, j * ROW:j * ROW + D], diff[t], rstd2[:, j:j + 1],
                                                      mod_b[:, b * 2 * D:b * 2 * D + D], ALU.mult, ALU.add)
                    ins.then_inc(s["h2_ok"], 1)
            routing_choice(ve, link)
            routing_places(ve, link)
            for g in range(route_last, ALL_GROUPS):
                if not by_act(g):
                    wait_places(ve, g)
                    turn_out(g)

            def mult_pieces(i, c):
                for n, w in enumerate(PIECES):
                    ve.wait_ge(s["sig_ok"], len(PIECES) * (4 * i + c) + n + 1)
                    ve.tensor_tensor(act[:, n * PIECE:n * PIECE + w], bank[2 + n][:, w:2 * w],
                                     sig[:, n * PIECE:n * PIECE + w], ALU.mult).then_inc(s["act_ok"], 1)

            def result(i, c, r):
                ve.wait_ge(s["down_done"], 4 * i + c + 1)
                if not (isinstance(i, int) and 4 * i + c < 2):
                    ve.wait_ge(y_out[r], 16 * (2 * i + c // 2))
                ve.tensor_copy(dest[r][:], xs[c % 4][:, DEST:DEST + 1])
                ve.tensor_scalar(y_sb[r], bank[7][:, 0:D], xs[c % 4][:, WEIGHT:WEIGHT + 1], None,
                                 ALU.mult).then_inc(s["y_ok"], 1)

            def tile_step(i, c):
                mult_pieces(i, c)
                if c >= 1:
                    result(i, c - 1, (c - 1) % 2)
                ve.wait_ge(s["at_done"], 2 * (4 * i + c) + 1)
                ve.tensor_copy(actT[:, 0:4 * P], bank[5][:]).then_inc(s["actT_v"], 1)

            turns(ve, tile_step)
            result(0, SLOT_TILES - 1, (SLOT_TILES - 1) % 2)

            ve.wait_ge(s["gateb_in"], 16 * B)
            for b in range(B):
                cols = slice(b * TB * D, (b + 1) * TB * D)
                ve.wait_ge(part_in[b], 32)
                link(ve.tensor_tensor(part1[:, cols], part1[:, cols], part2[:, cols], ALU.add))
                g3 = gate_b[:, b * D:(b + 1) * D].rearrange("p (a d) -> p a d", a=1).to_broadcast([P, TB, D])
                link(ve.tensor_tensor(v3(part1[:, cols], TB), v3(part1[:, cols], TB), g3, ALU.mult))
                ve.tensor_tensor(x[:, cols], part1[:, cols], x[:, cols], ALU.add).then_inc(s["fin_ok"], 1)

        @block.gpsimd
        def _(po):
            po.memset(empty[:], 0.0).then_inc(s["empty_ok"], 1)
            po.wait_ge(s["empty_ok"], 1)
            po.memset(empty[:, DEST:DEST + 1], float(NOWHERE)).then_inc(s["empty_ok"], 1)
            po.wait_ge(s["half_ok"], 1)
            kc_ = [0]

            def klink(ins):
                kc_[0] += 1
                ins.then_inc(s["kchain"], 1)
                po.wait_ge(s["kchain"], kc_[0])

            for k in range(-2, STEPS):
                for b in at_step(k, -2):
                    po.wait_ge(s["veps_ok"], b + 1)
                    po.tensor_tensor(rstd[:, b * TB:(b + 1) * TB], var_eps[:, b * TB:(b + 1) * TB],
                                     half_neg[:, 0:TB], ALU.pow).then_inc(s["rstd_ok"], 1)
                for b in at_step(k, 1):
                    if b == 0:
                        po.wait_ge(s["rott_in"], 16)
                    po.wait_ge(s["q0_ok"], 2 * (b + 1))
                    q = qT[:, b * S:(b + 1) * S]
                    po.tensor_tensor(q, q, qsin, ALU.add).then_inc(s["qr_ok"], 1)
                    po.wait_ge(s["kvsb_ok"], TB * (b + 1))
                    kvb = v3(kv_b(b), TB)
                    k1 = kvb[:, :, 0:P]
                    flip = kvb[:, :, 0:P]
                    kr = v3(ksw, TB)
                    sinr = v3(rot_token[:, 2 * P:4 * P], TB)
                    po.wait_ge(s["ksq_ok"], TB * (b + 1))
                    if b:
                        po.wait_ge(s["kvp_ok"], b)
                    for t in range(TB):
                        kt = kv_at(b, t)[:, 0:P].rearrange("p (i two) -> p i two", two=2)[:, :, ::-1]
                        ins = po.tensor_tensor(ksw[:, t * P:(t + 1) * P].rearrange("p (i two) -> p i two", two=2), kt,
                                               rot_token[:, (2 + t) * P:(3 + t) * P].rearrange("p (i two) -> p i two", two=2),
                                               ALU.mult)
                    klink(ins)
                    klink(po.tensor_tensor(k1, k1, v3(rot_token[:, 0:2 * P], TB), ALU.mult))
                    klink(po.tensor_tensor(k1, k1, kr, ALU.add))
                    po.tensor_tensor(v3(kvp[:, b * TB * D:(b + 1) * TB * D], TB), kvb[:, :, 0:D], kvb[:, :, D:2 * D],
                                     ALU.mult).then_inc(s["kvp_ok"], 1)
                    cols = slice(b * TB, (b + 1) * TB)
                    klink(po.tensor_scalar(ksq_max[:, cols], ksq[:, cols], TINY, None, ALU.max))
                    po.tensor_tensor(kinv[:, cols], ksq_max[:, cols], half_neg[:, 0:TB], ALU.pow).then_inc(s["kinv_ok"], 1)
                for b in at_step(k, 5):
                    po.wait_ge(s["veps2_ok"], b + 1)
                    po.tensor_tensor(rstd2[:, b * TB:(b + 1) * TB], var_eps2[:, b * TB:(b + 1) * TB],
                                     half_neg[:, 0:TB], ALU.pow).then_inc(s["rstd2_ok"], 1)
                for b in at_step(k, 8):
                    po.wait_ge(s["y_done"], B)
                    po.wait_ge(s["h2_ok"], b + 1)
                    r1, r2 = (v3(r[:], TT)[:, b * TB:(b + 1) * TB, 0:D] for r in (rows1, rows2))
                    po.tensor_scalar(r2, r1, 1.0, 0.0, ALU.mult, ALU.add).then_inc(s["ids2_ok"], 1)
            b = B - 1
            po.wait_ge(s["h2_ok"], B)
            r1, r2 = (v3(r[:], TT)[:, b * TB:(b + 1) * TB, 0:D] for r in (rows1, rows2))
            po.tensor_scalar(r2, r1, 1.0, 0.0, ALU.mult, ALU.add).then_inc(s["ids2_ok"], 1)
            po.wait_ge(s["ids2_ok"], B)
            po.wait_ge(s["empty_out"], 16)
            for n, rows in enumerate((rows1, rows2)):
                po.wait_ge(s["slots_ok"], n + 1)
                for t in range(TT):
                    po.indirect_dma_start(slots_d, bass.IndirectOffsetOnAxis(slot_i[n][:, t:t + 1], 0),
                                          rows[:, t * ROW:(t + 1) * ROW], None,
                                          bounds_check=SLOTS - 1, oob_is_err=False).then_inc(s["slots_out"], 16)

            last_part = po.to_reg(2 * TOKENS - 1)

            for j in range(SLOT_TILES):
                r = j % 2
                po.wait_ge(s["y_ok"], j + 1)
                po.indirect_dma_start(parts_d, bass.IndirectOffsetOnAxis(dest[r][:, 0:1], 0), y_sb[r], None,
                                      bounds_check=last_part, oob_is_err=False).then_inc(y_out[r], 16)


_ORDER = ["L0_attn_X", "L0_attn_W_in", "L0_attn_b_in", "L0_attn_W_out", "L0_attn_b_out", "L0_ffn_router_w",
          "L0_ffn_Wg", "L0_ffn_Wu", "L0_ffn_Wd", "L0_c", "L0_wmod"]


def kernel(**inputs):
    import concourse.bacc as bacc
    from concourse.bass_utils import run_bass_kernel_spmd

    nc = bacc.Bacc("TRN2", target_bir_lowering=False, num_devices=1)
    arrays = {name: np.ascontiguousarray(inputs[name]) for name in _ORDER}
    for name, a in zip(("keep", "swap", "rot_feature", "rot_token"), shape_constants()):
        arrays[name] = a
    args = [nc.dram_tensor(f"in_{n}", a.shape, F32, kind="ExternalInput").ap() for n, a in arrays.items()]
    out = nc.dram_tensor("out", (B, S, D), F32, kind="ExternalOutput").ap()
    layer(nc, *args, out)
    r = run_bass_kernel_spmd(nc, [{f"in_{n}": a for n, a in arrays.items()}], core_ids=[0])
    return r.results[0]["out"]
```

```python
from contextlib import ExitStack

import numpy as np
import concourse.bass as bass
from concourse import mybir

ALU = mybir.AluOpType
ACT = mybir.ActivationFunctionType
AX = mybir.AxisListType
F32 = mybir.dt.float32
U32 = mybir.dt.uint32
I32 = mybir.dt.int32
F16 = mybir.dt.float16

P = 128
B, S, D = 4, 256, 256
E, F = 8, 704
TOKENS = B * S
TT = TOKENS // P
TB = S // P
DC = D // P
FC = (F + P - 1) // P
F_LAST = F - (FC - 1) * P
SLOT_TILES = (2 * TOKENS + E * (P - 1)) // P
ROW = D + 4
WEIGHT, WEIGHT_STEP, UNSCALE = D, D + 1, D + 2
NOWHERE = 1 << 20
PIECE = 256
PIECES = [min(PIECE, F - PIECE * n) for n in range((F + PIECE - 1) // PIECE)]
W1_COLS = 2 * F
W1_EXP = DC * W1_COLS
W2_EXP = FC * D
MODS = 6
SHIFT_A, SCALE_A, GATE_A, SHIFT_B, SCALE_B, GATE_B = range(MODS)
FINISH_DVE, FINISH_POOL = [0, 2, 3], [1]
STAGED = 4
FULL = 2.0 ** 15
LEAST = 1e-30
NORMED_MAX = float(D) ** 0.5
EPS = 1e-5
TINY = 1e-24
GATE_MIN = 0.25
UNROLL = 4
TURNS = (SLOT_TILES - 1) // UNROLL
PEELED_LAST = range(1 + TURNS * UNROLL, SLOT_TILES)

C_ID, C_TRI, C_ONE = 0, P, 2 * P
C_REV = 3 * P
C_STEP = C_REV + E
C_TILE = C_STEP + 8
NT = 24
C_TOKEN = C_TILE + NT
C_LOW = C_TOKEN + 2 * TT
C_COLS = C_LOW + P
R_C, R_BIN, R_BOUT, R_ROUTER = 0, B * DC, B * DC + 6, B * DC + 8
R_ALL = R_ROUTER + E * DC
T_BOUT = R_BOUT - R_BIN


def shape_constants():
    keep = np.zeros((P, C_COLS), np.float32)
    keep[:, C_ID:C_ID + P] = np.eye(P)
    keep[:, C_TRI:C_TRI + P] = np.triu(np.ones((P, P)), 1)
    keep[:, C_ONE:C_ONE + P] = 1.0
    keep[:, C_REV:C_REV + E] = E - np.arange(E)
    keep[:, C_STEP:C_STEP + 8] = P * (1 + np.arange(8))
    keep[:, C_TILE:C_TILE + NT] = np.arange(NT)
    token = np.arange(TT)[None, :] * P + np.arange(P)[:, None]
    keep[:, C_TOKEN:C_TOKEN + TT] = token + 1
    keep[:, C_TOKEN + TT:C_TOKEN + 2 * TT] = token + TOKENS + 1
    keep[:, C_LOW:C_LOW + P] = np.arange(P) - P
    half = D // 4
    inv = (1.0 / 10000.0 ** (np.arange(0, D // 2, 2, dtype=np.float32) / np.float32(D // 2))).astype(np.float32)
    freqs = (np.arange(S, dtype=np.float32)[:, None] * inv[None, :]).astype(np.float32)
    cos, sin = np.cos(freqs), np.sin(freqs)
    cos2, sin2 = np.repeat(cos, 2, axis=1), np.repeat(sin, 2, axis=1)
    swap = np.zeros((P, P), np.float32)
    for i in range(half):
        swap[2 * i + 1, 2 * i] = -1.0
        swap[2 * i, 2 * i + 1] = 1.0
    by_feature = np.concatenate([cos2.T, sin2.T], axis=1)
    sign = np.where(np.arange(P) % 2 == 0, -1.0, 1.0)[None, :]
    by_token = np.concatenate([cos2[:P], cos2[P:], (sin2 * sign)[:P], (sin2 * sign)[P:]], axis=1)
    return keep, swap, np.ascontiguousarray(by_feature, np.float32), by_token.astype(np.float32)


def layer(nc, X, W_in, b_in, W_out, b_out, router_w, Wg, Wu, Wd, cond, wmod,
          keep_d, swap_d, rot_feature_d, rot_token_d, out):
    ctx = ExitStack()
    with ctx:
        def sb(name, cols, dt=F32, parts=P):
            return ctx.enter_context(nc.sbuf_tensor(name, [parts, cols], dt))

        def sem(name):
            return ctx.enter_context(nc.semaphore(name))

        rows_d = nc.dram_tensor("token_rows", (TOKENS, ROW), F32, kind="Internal").ap()
        parts_d = nc.dram_tensor("expert_parts", (2 * TOKENS, D), F32, kind="Internal").ap()
        modrow_d = nc.dram_tensor("mod_rows", (B, 3 * D + 1), F32, kind="Internal").ap()

        bank = [ctx.enter_context(nc.psum_tensor(f"bank{i}", [P, 512], F32)) for i in range(8)]

        W1 = sb("W1", E * W1_EXP)
        W2 = sb("W2", E * W2_EXP)
        staged = [sb(f"staged{m}", FC * D) for m in range(STAGED)]
        x = sb("x", TT * D)
        rows1 = sb("rows1", TT * ROW)
        shared = sb("shared", DC * TOKENS)
        gate_b = sb("gate_b", B * (D + 1))
        keep = sb("keep", C_COLS)
        swap = sb("swap", P)
        small_rows = sb("cond_rows", P, parts=R_BIN)
        rest_rows = sb("bias_router_rows", P, parts=R_ALL - R_BIN)
        smallT = sb("smallT", R_ALL - R_BIN)
        condT = sb("condT", B * DC)
        mod = sb("mod", 3 * DC * B)
        gatetmp = sb("gatetmp", 2 * DC * B)
        gate_bias = sb("gate_bias", DC * B)
        bias_q = sb("bias_q", 1)
        half_neg = sb("half_neg", 8)
        stats = sb("stats", TT * 6)
        mean_var = sb("mean_var", TT * 2)
        var_eps = sb("var_eps", TT)
        rstd = sb("rstd", TT)
        stats2 = sb("stats2", TT * 6)
        mean_var2 = sb("mean_var2", TT * 2)
        var_eps2 = sb("var_eps2", TT)
        rstd2 = sb("rstd2", TT)
        ksq = sb("ksq", TT)
        ksq_max = sb("ksq_max", TT)
        kinv = sb("kinv", TT)
        attn_sum = sb("attn_sum", B * DC)
        modrow = sb("modrow", MODS * D + 1, parts=B)
        scratch = sb("scratch", 2 * D)
        modtmp = scratch[0:B, :]
        bounds = sb("bounds", 4, parts=B)
        sumsq = sb("sumsq", E * 4)
        w_norm2 = sb("w_norm2", E * 2)
        w_power = sb("w_power", E * 2, I32)
        w_scale_bits = sb("w_scale_bits", E * 2, I32)
        w_unscale_bits = sb("w_unscale_bits", E * 2, I32)
        w_scale, w_unscale = w_scale_bits[:].bitcast(F32), w_unscale_bits[:].bitcast(F32)
        W1_b16 = W1[:].bitcast(mybir.dt.bfloat16)
        W1_16 = W1[:].bitcast(F16)

        def under(buf, start):
            at = [start]

            def take(n):
                at[0] += n
                return buf[:, at[0] - n:at[0]]
            return take

        early1, early2 = under(W1, 4 * W1_EXP), under(W2, 4 * W2_EXP)
        wmod_sb = early1(DC * MODS * D)
        w_inT = early1(DC * 7 * P)
        xn = [early1(TB * D), wmod_sb[:, 2 * MODS * D - TB * D:]]
        w_in_nat = early2(6 * D)
        w_out_nat = early2(DC * D)
        bias_kv = early2(2 * D)
        rot_token = early2(4 * P)
        late1, late2 = under(W1, 6 * W1_EXP), under(W2, 6 * W2_EXP)
        hT = late1(DC * TOKENS)
        mod_b = late1(B * 2 * D)
        wA = late1(2 * DC * D)
        w_outT = late1(DC * D)
        kv = late2(2 * TB * 2 * D)
        rot_feature = late2(2 * S)
        sink = late2(D)
        ksw = late2(D)
        qT = shared[:, 0:DC * TOKENS]
        kvp = rows1[:, 0:TT * D]
        qsin = sb("qsin", S)[:]
        h2T = kv[:, 0:DC * S]
        diff = [kv[:, DC * S + t * D:DC * S + (t + 1) * D] for t in range(TB)]

        xs = [rows1[:, r * ROW:(r + 1) * ROW] for r in range(4)]
        slot_hi = rows1[:, 4 * ROW:4 * ROW + D // 2].bitcast(F16)
        slot_lo = rows1[:, 4 * ROW + D // 2:4 * ROW + D].bitcast(F16)
        sig = rows1[:, 4 * ROW + D:4 * ROW + D + F]
        y_sb = [shared[:, r * D:(r + 1) * D] for r in range(2)]
        act = shared[:, 2 * D:2 * D + F]
        actT = shared[:, 2 * D + F:2 * D + F + FC * P]
        unscale = [sb(f"unscale{r}", 2) for r in range(2)]

        part1 = W1[:, 0:TT * D]
        part2 = W1[:, TT * D:2 * TT * D]

        NR = TT * E
        SUM0 = 8 * E
        lg = sb("lg", NR)
        logit_less_max = sb("logit_less_max", NR)
        expo = sb("expo", NR)
        lg2 = sb("logits_without_first", NR)
        choice = [sb(f"choice{n}", NR) for n in range(2)]
        picked = sb("picked", NR)
        slot_all = sb("slot_all", NR)
        chosen = sb("chosen", NR)
        tiles_sum = [scratch[:, i * P:(i + 1) * P] for i in range(3)]
        top = [sb(f"top{n}", TT) for n in range(2)]
        top_rev = sb("top_rev", TT)
        weight = [sb(f"weight{n}", TT) for n in range(2)]
        weight_sum = sb("weight_sum", TT)
        cnt = sb("cnt", 8 * E)
        stp = sb("stp", E * 8)
        til = sb("til", NT * E)
        tile_e = sb("tile_e", NT)
        tile_ei = sb("tile_ei", NT, I32)
        slot = sb("slot", 2 * TT)
        slot_tile = sb("slot_tile", 2 * TT)
        slot_low = sb("slot_low", 2 * TT)
        PAIRS = 2 * TT
        one_hot_place = shared[:, 0:PAIRS * P // 2].bitcast(F16)
        one_hot_tile = shared[:, PAIRS * P // 2:PAIRS * P // 2 + PAIRS * NT]
        token_tile = shared[:, PAIRS * P // 2 + PAIRS * NT:PAIRS * P // 2 + PAIRS * NT + PAIRS * NT // 2].bitcast(F16)
        filled = sb("filled", NT)
        second = sb("second", NT)
        nobody = sb("nobody", NT)
        source = sb("source", NT)
        source_i = sb("source_i", NT, U32)
        dest_i = sb("dest_i", NT, U32)
        slot_weight = [sb(f"slot_weight{r}", 1) for r in range(4)]

        def v3(ap, a):
            return ap.rearrange("p (a b) -> p a b", a=a)

        def turned(k):
            return keep[:, C_ID:C_ID + P] if k == P else keep[0:k, C_ID:C_ID + k]

        def modcol(m, dc, b):
            c = (m * DC + dc) * B + b
            return mod[:, c:c + 1]

        def kv_b(b):
            return kv[:, (b % 2) * TB * 2 * D:(b % 2 + 1) * TB * 2 * D]

        def kv_at(b, t):
            return kv_b(b)[:, t * 2 * D:(t + 1) * 2 * D]

        def kvp_col(b, t, dc):
            return (b * TB + t) * D + dc * P

        smallT_r = smallT[:, R_ROUTER - R_BIN:R_ALL - R_BIN].rearrange("p (e c) -> p e c", c=DC)

        names = """const_in small_in rotf_in rott_in win_in wout_in bkv_in modrow_out modb_in gateb_in
            half_ok smallsrc small_done smallT_ok cond_ok condsrc cond_done modT_done modrow_done bq_done modA_ok mod_ok dchain
            rowsA_ok row_ga_ok rowsB_ok turn_done turn_act turn_dve stat_ok veps_ok rstd_ok xn_ok t_done hT_ok kv_done q_done kvsb_ok
            ksq_ok kchain kvp_ok kinv_ok q0_ok qr_ok q1_ok hg_ok a_done asum_ok wA_ok y_done z_ok tz_done x2_ok stat2_ok veps2_ok
            rstd2_ok diff_ok h2_ok th_done h2T_ok r_done expo_ok sub_ok sel_ok sums_ok cnt_done tile_ok rows_ok rows_out place_ok table_done source_ok dest_ok
            gu_done sig_ok act_ok xt_done slot_hi_ok slot_lo_ok unscale_ok sumsq_ok wscale_ok at_done actT_a actT_v down_done y_ok
            fin_ok pool_fin_ok out_done""".split()
        s = {n: sem(n) for n in names}
        x_in = [sem(f"x_in{b}") for b in range(B)]
        staged_in = [sem(f"staged_in{r}") for r in range(STAGED)]
        xs_in = [sem(f"xs_in{r}") for r in range(4)]
        y_out = [sem(f"y_out{r}") for r in range(2)]
        wmod_in = [sem(f"wmod_in{n}") for n in range(3)]
        part_in = [sem(f"part_in{b}") for b in range(B)]

        groups = [("w_in", None, n) for n in range(3)] + [("w_in_swapped", None, 0), ("w_out", None, 0)]
        FIRST = len(groups)
        groups += [("norm", 0, 0)]
        for e in range(E):
            groups += [("gate", e, n) for n in range(3)] + [("up", e, n) for n in range(3)]
            groups += [("down", e, n) for n in range(3)] + [("norm", e + 1, 0)] * (e + 1 < E)
        MATRIX = {"gate": 0, "up": 1, "down": 2}
        STEPS = 10
        STEP_GROUPS = {1: (0, 0, 0, 0, 0, 1), 2: (1, 1, 1, 0, 0, 0), 3: (1, 1, 1, 0, 0, 0), 4: (1, 1, 0, 0, 0, 0),
                       5: (1, 0, 0, 1, 1, 0), 6: (1, 0, 0, 1, 1, 0), 7: (1, 0, 0, 1, 1, 0),
                       8: (1, 0, 0, 1, 1, 0), 9: (1, 0, 0, 2, 2, 1)}
        TILE_GROUPS = ((1, 1, 1, 1, 1, 1),) * 7 + ((1, 0, 0, 0, 0, 0),) + ((0,) * 6,)
        ALL_GROUPS = len(groups)
        tiles_first = ALL_GROUPS - sum(map(sum, TILE_GROUPS))
        route_first = FIRST + sum(map(sum, STEP_GROUPS.values()))
        route_mid = route_first + 5

        def step_slot(k, n):
            at = FIRST + sum(sum(STEP_GROUPS[h]) for h in range(1, k)) + sum(STEP_GROUPS.get(k, ())[:n])
            return range(at, at + STEP_GROUPS[k][n]) if k in STEP_GROUPS else range(0)

        group_bank = [g % 2 for g in range(ALL_GROUPS)]
        stage_two = step_slot(5, 0).start
        for g in range(stage_two, route_first):
            group_bank[g] = (0, 1, 4)[(g - stage_two) % 3]
        for g in range(route_first, tiles_first):
            group_bank[g] = (0, 1, 4, 2, 5)[g - route_first] if g < route_mid else (g - route_mid) % 2
        for g in range(tiles_first, ALL_GROUPS):
            group_bank[g] = (g - route_mid) % 2

        def last_on_bank(g):
            before = [h for h in range(g) if group_bank[h] == group_bank[g]]
            return before[-1] if before else None

        def tile_slot(i, c, n):
            if not (isinstance(i, int) and i == 0 and c < len(TILE_GROUPS)):
                return range(0)
            at = tiles_first + sum(map(sum, TILE_GROUPS[:c])) + sum(TILE_GROUPS[c][:n])
            return range(at, at + TILE_GROUPS[c][n])

        def split(g):
            return groups[g][0] in ("gate", "up")

        def by_act(g):
            return split(g) or (g < FIRST and g % 2 == 0) or (groups[g][0] == "down" and g < tiles_first)

        def by_dve(g):
            return split(g) or not by_act(g)

        def wait_turned(eng, upto):
            eng.wait_ge(s["turn_act"], sum(by_act(g) for g in range(upto)))
            eng.wait_ge(s["turn_dve"], sum(by_dve(g) for g in range(upto)))

        def wait_out(eng, g):
            by = by_dve if by_dve(g) else by_act
            eng.wait_ge(s["turn_dve" if by_dve(g) else "turn_act"], sum(by(h) for h in range(g + 1)))

        def matrix_place(e, m):
            return (3 * e + m) % STAGED, (3 * e + m) // STAGED

        def last_group(q):
            e, m = divmod(q, 3)
            return groups.index((("gate", "up", "down")[m], e, 2))

        def wait_places(eng, e):
            if e == 4:
                eng.wait_ge(s["q_done"], B)
                eng.wait_ge(s["kvsb_ok"], B * TB)
                eng.wait_ge(s["kvp_ok"], B)
                eng.wait_ge(s["modrow_done"], 3)
            if e == 6:
                eng.wait_ge(s["r_done"], B)

        def w1_col(kc, m, f):
            n, w = f // PIECE, PIECES[f // PIECE]
            return kc * W1_COLS + 2 * PIECE * n + m * w + f % PIECE

        def group_moves(g):
            kind, e, n = groups[g]
            if kind == "w_in":
                return [(0, 512, P, v3(w_inT, DC)[:, :, 2 * n * P:2 * n * P + 2 * P], DC)]
            if kind == "w_in_swapped":
                return [(0, 256, P, v3(w_inT, DC)[:, :, 6 * P:7 * P], DC)]
            if kind == "w_out":
                return [(0, 512, P, w_outT, None)]
            base = e * W2_EXP + 2 * n * D
            if n < 2:
                return [(0, 512, P, W2[:, base:base + 512], None)]
            return [(0, D, P, W2[:, base:base + D], None),
                    (D, D, F_LAST, W2[0:F_LAST, base + D:base + 2 * D], None)]

        def evacuate(copy, g):
            for c, n, parts, place, a in group_moves(g):
                src = bank[group_bank[g]][0:parts, c:c + n]
                last = copy(place, v3(src, a) if a else src)
            return last

        def split_views(g):
            kind, e, n = groups[g]
            w = PIECES[n]
            c = w1_col(0, MATRIX[kind], PIECE * n)
            hi, lo = (v3(W1_16[:, (2 * e + part) * W1_EXP:(2 * e + part + 1) * W1_EXP], DC)[:, :, c:c + w]
                      for part in range(2))
            return v3(bank[group_bank[g]][:, 0:DC * w], DC), hi, lo

        def at_step(k, off):
            b = k - off
            return [b] if 0 <= b < B else []

        def turns(eng, step):
            for j in range(1 + 2 * UNROLL):
                step(0, j)
            with eng.Fori(2, TURNS) as i:
                for c in range(1, 1 + UNROLL):
                    step(i, c)
            for j in PEELED_LAST:
                step(0, j)

        def finish(eng, batches, link, done):
            for b in batches:
                cols = slice(b * TB * D, (b + 1) * TB * D)
                eng.wait_ge(part_in[b], 32)
                link(eng.tensor_tensor(part1[:, cols], part1[:, cols], part2[:, cols], ALU.add))
                g3 = gate_b[:, b * (D + 1):b * (D + 1) + D].rearrange("p (a d) -> p a d", a=1).to_broadcast([P, TB, D])
                link(eng.tensor_tensor(v3(part1[:, cols], TB), v3(part1[:, cols], TB), g3, ALU.mult))
                eng.tensor_tensor(x[:, cols], part1[:, cols], x[:, cols], ALU.add).then_inc(done, 1)

        block = ctx.enter_context(nc.Block())

        @block.sync
        def _(sp):
            def load_x(b):
                sp.dma_start(v3(x[:, b * TB * D:(b + 1) * TB * D], TB),
                             X[b].rearrange("(t p) d -> p t d", p=P)).then_inc(x_in[b], 16)

            def load_wmod(n):
                sp.dma_start(v3(wmod_sb, DC)[:, :, 2 * n * D:2 * (n + 1) * D],
                             wmod.rearrange("(c p) n -> p c n", p=P)[:, :, 2 * n * D:2 * (n + 1) * D]
                             ).then_inc(wmod_in[n], 16)
            sp.dma_start(keep[:], keep_d).then_inc(s["const_in"], 16)
            load_wmod(0)
            load_x(0)
            sp.dma_start(v3(w_in_nat, 6), W_in.rearrange("(c p) d -> p c d", p=P)).then_inc(s["win_in"], 16)
            load_wmod(1)
            load_x(1)
            load_wmod(2)
            sp.dma_start(bias_kv, b_in[D:3 * D].rearrange("(a n) -> a n", a=1).to_broadcast([P, 2 * D])).then_inc(s["bkv_in"], 16)
            sp.dma_start(rot_feature, rot_feature_d).then_inc(s["rotf_in"], 16)
            sp.dma_start(rot_token, rot_token_d).then_inc(s["rott_in"], 16)
            sp.dma_start(v3(w_out_nat, DC), W_out.rearrange("(c p) d -> p c d", p=P)).then_inc(s["wout_in"], 16)
            for b in range(2, B):
                load_x(b)

            def load_matrix(q):
                e, m = divmod(q, 3)
                r = q % STAGED
                if q >= STAGED:
                    sp.wait_ge(s["turn_done"], last_group(q - STAGED) + 1)
                if m < 2:
                    W = (Wg, Wu)[m]
                    full = (FC - 1) * P
                    sp.dma_start(v3(staged[r][:, 0:(FC - 1) * D], FC - 1),
                                 W[e, 0:full].rearrange("(c p) d -> p c d", p=P)).then_inc(staged_in[r], 16)
                    sp.dma_start(staged[r][0:F_LAST, (FC - 1) * D:FC * D], W[e, full:F]).then_inc(staged_in[r], 16)
                else:
                    sp.dma_start(v3(staged[r][:, 0:DC * F], DC),
                                 Wd[e].rearrange("(c p) f -> p c f", p=P)).then_inc(staged_in[r], 32)

            for q in range(STAGED):
                load_matrix(q)
            sp.wait_ge(s["rowsB_ok"], 4)
            sp.dma_start(modrow_d, modrow[:, SHIFT_B * D:]).then_inc(s["modrow_out"], 16)
            sp.wait_ge(s["modrow_out"], 16)
            for b in range(B):
                sp.dma_start(mod_b[:, b * 2 * D:(b + 1) * 2 * D],
                             modrow_d[b:b + 1, 0:2 * D].to_broadcast([P, 2 * D])).then_inc(s["modb_in"], 16)
                sp.dma_start(gate_b[:, b * (D + 1):(b + 1) * (D + 1)],
                             modrow_d[b:b + 1, 2 * D:].to_broadcast([P, D + 1])).then_inc(s["gateb_in"], 16)
            early = [q for q in range(STAGED, 3 * E) if last_group(q - STAGED) < route_first]
            for q in early:
                load_matrix(q)
            sp.wait_ge(s["rows_ok"], 1)
            sp.dma_start(rows_d.rearrange("(t p) n -> p t n", p=P), v3(rows1[:], TT)).then_inc(s["rows_out"], 16)
            for q in range(early[-1] + 1, 3 * E):
                load_matrix(q)

            for r in range(2):
                sp.wait_ge(y_out[r], 16 * len(range(r, SLOT_TILES, 2)))
            for b in range(B):
                for k, part in enumerate((part1, part2)):
                    sp.dma_start(v3(part[:, b * TB * D:(b + 1) * TB * D], TB),
                                 parts_d[k * TOKENS + b * S:k * TOKENS + (b + 1) * S].rearrange("(t p) d -> p t d", p=P)
                                 ).then_inc(part_in[b], 16)
            for b in FINISH_DVE[:-1] + FINISH_POOL + FINISH_DVE[-1:]:
                if b in FINISH_POOL:
                    sp.wait_ge(s["pool_fin_ok"], FINISH_POOL.index(b) + 1)
                else:
                    sp.wait_ge(s["fin_ok"], FINISH_DVE.index(b) + 1)
                sp.dma_start(out[b].rearrange("(t p) d -> p t d", p=P),
                             v3(x[:, b * TB * D:(b + 1) * TB * D], TB)).then_inc(s["out_done"], 16)
            sp.wait_ge(s["out_done"], 16 * B)

        @block.tensor
        def _(pe):
            def turn(g):
                if last_on_bank(g) is None and group_bank[g] == 4:
                    pe.wait_ge(s["kvsb_ok"], B * TB)
                if last_on_bank(g) is not None:
                    wait_out(pe, last_on_bank(g))
                bk = bank[group_bank[g]]
                kind, e, n = groups[g]
                if kind == "w_in":
                    for j in range(2):
                        for dc in range(DC):
                            ec = 2 * n + j
                            mm = pe.transpose(bk[:, (dc * 2 + j) * P:(dc * 2 + j + 1) * P],
                                              w_in_nat[:, ec * D + dc * P:ec * D + (dc + 1) * P], turned(P))
                elif kind == "w_in_swapped":
                    for dc in range(DC):
                        mm = pe.matmul(bk[:, dc * P:(dc + 1) * P], w_in_nat[:, dc * P:(dc + 1) * P],
                                       swap[:], start=True, stop=True)
                elif kind == "w_out":
                    for ec in range(DC):
                        for dc in range(DC):
                            mm = pe.transpose(bk[:, dc * D + ec * P:dc * D + (ec + 1) * P],
                                              w_out_nat[:, ec * D + dc * P:ec * D + (dc + 1) * P], turned(P))
                elif kind == "norm":
                    pe.wait_ge(s["sumsq_ok"], 2 * (e + 1))
                    mm = pe.matmul(bk[:, 0:4], keep[:, C_ONE:C_ONE + P], sumsq[:, 4 * e:4 * e + 4],
                                   start=True, stop=True)
                elif kind == "down":
                    r, uses = matrix_place(e, MATRIX[kind])
                    if n == 0:
                        pe.wait_ge(staged_in[r], 32 * (uses + 1))
                    for fc in (2 * n, 2 * n + 1):
                        rows = min(P, F - fc * P)
                        for hc in range(DC):
                            c = (fc % 2) * D + hc * P
                            mm = pe.transpose(bk[0:rows, c:c + P],
                                              staged[r][:, hc * F + fc * P:hc * F + fc * P + rows], turned(P))
                else:
                    r, uses = matrix_place(e, MATRIX[kind])
                    if n == 0:
                        pe.wait_ge(staged_in[r], 32 * (uses + 1))
                    for fc in (2 * n, 2 * n + 1):
                        rows = min(P, F - fc * P)
                        for kc in range(DC):
                            c = kc * PIECES[n] + (fc % 2) * P
                            mm = pe.transpose(bk[:, c:c + rows],
                                              staged[r][0:rows, fc * D + kc * P:fc * D + (kc + 1) * P],
                                              turned(rows))
                mm.then_inc(s["turn_done"], 1)

            def mod_rows(n):
                pe.wait_ge(wmod_in[n], 16)
                for kc in range(DC):
                    mm = pe.matmul(bank[3 + n][0:B, :], condT[:, kc * B:(kc + 1) * B],
                                   v3(wmod_sb, DC)[:, kc, 2 * n * D:2 * (n + 1) * D],
                                   start=(kc == 0), stop=(kc == DC - 1))
                mm.then_inc(s["modrow_done"], 1)

            def turn_mod(m0, m1, rows_ok, rows):
                pe.wait_ge(rows_ok, rows)
                for c in range(m0 * DC, m1 * DC):
                    mm = pe.transpose(bank[6][:, c * B:(c + 1) * B], modrow[:, c * P:(c + 1) * P], turned(B))
                mm.then_inc(s["modT_done"], 1)

            pe.wait_ge(s["const_in"], 16)
            pe.wait_ge(s["condsrc"], 16)
            pe.transpose(bank[2][:, 0:R_BIN], small_rows[0:R_BIN, :], turned(R_BIN)).then_inc(s["cond_done"], 1)
            pe.wait_ge(s["cond_ok"], 1)
            mod_rows(0)
            pe.wait_ge(s["smallsrc"], 16 * 4)
            pe.transpose(bank[2][:, R_BIN:R_ALL], rest_rows[:, :], turned(R_ALL - R_BIN)).then_inc(s["small_done"], 1)
            pe.wait_ge(s["win_in"], 16)
            turn(0)
            turn_mod(SHIFT_A, GATE_A, s["rowsA_ok"], 2)
            turn(1)

            for k in range(STEPS):
                for b in at_step(k, 0):
                    pe.wait_ge(s["xn_ok"], b + 1)
                    if b:
                        pe.wait_ge(s["hT_ok"], DC * b)
                    else:
                        pe.wait_ge(s["smallT_ok"], 1)
                    for t in range(TB):
                        for dc in range(DC):
                            mm = pe.transpose(bank[2][:, dc * S + t * P:dc * S + (t + 1) * P],
                                              xn[b % 2][:, t * D + dc * P:t * D + (dc + 1) * P], turned(P))
                    mm.then_inc(s["t_done"], 1)
                if k == 0:
                    turn(2)
                    pe.wait_ge(s["small_in"], 16)
                    turn(3)
                    pe.wait_ge(s["modA_ok"], 1)
                    pe.matmul(bank[6][:, 3 * DC * B:3 * DC * B + 1], swap[:], smallT[:, 0:1],
                              start=True, stop=True).then_inc(s["bq_done"], 1)
                    mod_rows(1)
                    mod_rows(2)
                    pe.wait_ge(s["wout_in"], 16)
                    turn(4)
                    turn_mod(GATE_A, SHIFT_B, s["row_ga_ok"], 1)
                for g in step_slot(k, 0):
                    turn(g)
                for b in at_step(k, 1):
                    pe.wait_ge(s["hT_ok"], DC * (b + 1))
                    if b == 0:
                        wait_turned(pe, FIRST)
                        pe.wait_ge(s["rowsB_ok"], 3)
                        pe.wait_ge(s["mod_ok"], 1)
                    for t in range(TB):
                        if b:
                            pe.wait_ge(s["kvsb_ok"], TB * (b - 1) + t + 1)
                        for dc in range(DC):
                            col = dc * TOKENS + b * S + t * P
                            mm = pe.matmul(bank[3 + t][:, :], hT[:, col:col + P],
                                           v3(w_inT, DC)[:, dc, D:3 * D], start=(dc == 0), stop=(dc == DC - 1))
                        mm.then_inc(s["kv_done"], 1)
                for g in step_slot(k, 1):
                    turn(g)
                for b in at_step(k, 1):
                    if b:
                        pe.wait_ge(s["q0_ok"], 2 * b)
                        pe.wait_ge(s["q1_ok"], b)
                    if k >= 3:
                        pe.wait_ge(s["asum_ok"], k - 2)
                    for bk, c, w0 in ((5, 0, 0), (5, S, 6 * P), (6, 0, P)):
                        for dc in range(DC):
                            mm = pe.matmul(bank[bk][:, c:c + S], v3(w_inT, DC)[:, dc, w0:w0 + P],
                                           hT[:, dc * TOKENS + b * S:dc * TOKENS + (b + 1) * S],
                                           start=(dc == 0), stop=(dc == DC - 1))
                    mm.then_inc(s["q_done"], 1)
                for b in at_step(k, 2):
                    pe.wait_ge(s["kvp_ok"], b + 1)
                    pe.wait_ge(s["kinv_ok"], b + 1)
                    pe.wait_ge(s["q1_ok"], min(k, B))
                    if b:
                        pe.wait_ge(s["asum_ok"], b)
                    for dc in range(DC):
                        for t in range(TB):
                            mm = pe.matmul(bank[6][:, S + dc:S + dc + 1], kvp[:, kvp_col(b, t, dc):kvp_col(b, t, dc) + P],
                                           kinv[:, b * TB + t:b * TB + t + 1],
                                           start=(t == 0), stop=(t == TB - 1))
                    mm.then_inc(s["a_done"], 1)
                for g in step_slot(k, 2):
                    turn(g)
                for b in at_step(k, 3):
                    pe.wait_ge(s["wA_ok"], DC * (b + 1))
                    pe.wait_ge(s["qr_ok"], b + 1)
                    if b:
                        pe.wait_ge(s["z_ok"], DC * b)
                    for ec in range(DC):
                        for dc in range(DC):
                            c = (b % 2) * DC * D + dc * D + ec * P
                            mm = pe.matmul(bank[7][:, ec * S:(ec + 1) * S], wA[:, c:c + P],
                                           qT[:, dc * TOKENS + b * S:dc * TOKENS + (b + 1) * S],
                                           start=(dc == 0), stop=(dc == DC - 1))
                    mm.then_inc(s["y_done"], 1)
                for g in step_slot(k, 3):
                    turn(g)
                for b in at_step(k, 4):
                    pe.wait_ge(s["z_ok"], DC * (b + 1))
                    if b:
                        pe.wait_ge(s["x2_ok"], b)
                    else:
                        pe.wait_ge(s["q0_ok"], 2 * B)
                    for t in range(TB):
                        for dc in range(DC):
                            mm = pe.transpose(bank[5][:, t * D + dc * P:t * D + (dc + 1) * P],
                                              hT[:, dc * TOKENS + b * S + t * P:dc * TOKENS + b * S + (t + 1) * P],
                                              turned(P))
                    mm.then_inc(s["tz_done"], 1)
                for b in at_step(k, 5):
                    pe.wait_ge(s["h2_ok"], b + 1)
                    if b:
                        pe.wait_ge(s["h2T_ok"], b)
                    for t in range(TB):
                        for dc in range(DC):
                            c = (b * TB + t) * ROW + dc * P
                            mm = pe.transpose(bank[2][:, dc * S + t * P:dc * S + (t + 1) * P],
                                              rows1[:, c:c + P], turned(P))
                    mm.then_inc(s["th_done"], 1)
                for g in step_slot(k, 4):
                    turn(g)
                for b in at_step(k, 6):
                    pe.wait_ge(s["h2T_ok"], b + 1)
                    for t in range(TB):
                        for dc in range(DC):
                            mm = pe.matmul(bank[3][:, (b * TB + t) * E:(b * TB + t + 1) * E],
                                           h2T[:, dc * S + t * P:dc * S + (t + 1) * P],
                                           smallT_r[:, :, dc], start=(dc == 0), stop=(dc == DC - 1))
                    mm.then_inc(s["r_done"], 1)
                for g in step_slot(k, 5):
                    turn(g)
                if k == STEPS - 1:
                    pe.wait_ge(s["sel_ok"], 1)
                    pe.matmul(bank[7][:, P:P + NR], keep[:, C_TRI:C_TRI + P], chosen[:], start=True, stop=False)
                    pe.wait_ge(s["sums_ok"], 1)
                    pe.matmul(bank[7][:, P:P + NR], keep[:, C_ONE:C_ONE + P],
                              tiles_sum[2][:, SUM0 - E:SUM0 - E + NR], start=False, stop=True)
                    mm = pe.matmul(bank[7][:, 0:E], keep[:, C_ONE:C_ONE + P],
                                   tiles_sum[2][:, SUM0 + NR - E:SUM0 + NR], start=True, stop=True)
                    mm.then_inc(s["cnt_done"], 1)
                    for g in range(route_first, route_mid):
                        turn(g)
                    for i in range(PAIRS):
                        pe.wait_ge(s["place_ok"], i + 1)
                        mm = pe.matmul(bank[7][:, 2 * P:2 * P + NT], one_hot_place[:, i * P:(i + 1) * P],
                                       token_tile[:, i * NT:(i + 1) * NT], start=(i == 0), stop=(i == PAIRS - 1))
                    mm.then_inc(s["table_done"], 1)
                    for g in range(route_mid, tiles_first):
                        turn(g)

            def turn_slots(i, c):
                pe.wait_ge(xs_in[c % 4], 16 * (i + c // 4) + 16)
                if not (isinstance(i, int) and 4 * i + c < 2):
                    pe.wait_ge(s["actT_a"], 4 * i + c - 1)
                for dc in range(DC):
                    mm = pe.transpose(bank[6][:, DC * P + dc * P:DC * P + (dc + 1) * P],
                                      xs[c % 4][:, dc * P:(dc + 1) * P], turned(P))
                mm.then_inc(s["xt_done"], 1)

            def gate_up(i, c, turn_some):
                e = pe.value_load(tile_ei[0:1, bass.ds(4 * i + c, 1)], min_val=0, max_val=E - 1)
                pe.wait_ge(s["slot_lo_ok"], 4 * i + c + 1)
                terms = [(slot, kc, part) for kc in range(DC) for slot, part in ((slot_hi, 0), (slot_hi, 1), (slot_lo, 0))]
                for n, w in enumerate(PIECES):
                    for k, (slot, kc, part) in enumerate(terms):
                        at = part * W1_EXP + kc * W1_COLS + 2 * PIECE * n
                        mm = pe.matmul(bank[2 + n][:, 0:2 * w], slot[:, kc * P:(kc + 1) * P],
                                       W1_16[:, bass.ds(e * (2 * W1_EXP) + at, 2 * w)],
                                       start=(k == 0), stop=(k == len(terms) - 1))
                    mm.then_inc(s["gu_done"], 1)
                    turn_some(n)

            def turn_act(i, c):
                pe.wait_ge(s["act_ok"], len(PIECES) * (4 * i + c + 1))
                if not (isinstance(i, int) and c == SLOT_TILES - 1):
                    pe.wait_ge(s["slot_lo_ok"], 4 * i + c + 2)
                for fc in range(FC):
                    rows = min(P, F - fc * P)
                    bk, col = (bank[5], fc * P) if fc < 4 else (bank[6], (fc - 4) * P)
                    mm = pe.transpose(bk[0:rows, col:col + P], act[:, fc * P:fc * P + rows], turned(P))
                    if fc == 3:
                        mm.then_inc(s["at_done"], 1)
                mm.then_inc(s["at_done"], 1)

            def down(i, c, turn_some=None):
                e = pe.value_load(tile_ei[0:1, bass.ds(4 * i + c, 1)], min_val=0, max_val=E - 1)
                pe.wait_ge(s["actT_v"], 4 * i + c + 1)
                pe.wait_ge(s["actT_a"], 4 * i + c + 1)
                if not (isinstance(i, int) and 4 * i + c < 1):
                    pe.wait_ge(s["y_ok"], 4 * i + c)
                for fc in range(FC):
                    rows = min(P, F - fc * P)
                    mm = pe.matmul(bank[7][:, 0:D], actT[0:rows, fc * P:(fc + 1) * P],
                                   W2[0:rows, bass.ds(e * W2_EXP + fc * D, D)],
                                   start=(fc == 0), stop=(fc == FC - 1))
                    if fc == 2 and turn_some:
                        turn_some(3)
                mm.then_inc(s["down_done"], 1)

            turn_slots(0, 0)
            pe.wait_ge(s["tile_ok"], 1)

            def tile_step(i, c):
                def turn_some(n):
                    for g in tile_slot(i, c, n):
                        turn(g)
                if isinstance(i, int) and i == 0 and c < E:
                    done = tile_slot(0, c, 0).start
                    if c == 0:
                        for h in range(route_first, route_mid):
                            wait_out(pe, h)
                    need = [g for g in range(done) if groups[g][0] in ("gate", "up") and groups[g][1] <= c
                            or groups[g][0] == "down" and groups[g][1] < c]
                    wait_turned(pe, need[-1] + 1)
                gate_up(i, c, turn_some)
                if not (isinstance(i, int) and c == SLOT_TILES - 1):
                    turn_slots(i, c + 1)
                if c >= 1:
                    down(i, c - 1, turn_some)
                else:
                    turn_some(3)
                turn_some(4)
                turn_act(i, c)
                turn_some(5)

            turns(pe, tile_step)
            down(0, SLOT_TILES - 1)

        @block.scalar
        def _(sc):
            sc.dma_start(small_rows[:], cond.rearrange("b (c p) -> (b c) p", p=P)).then_inc(s["condsrc"], 16)
            r0 = R_BOUT - R_BIN
            r1 = R_ROUTER - R_BIN
            sc.dma_start(rest_rows[0:r0, :], b_in.rearrange("(c p) -> c p", p=P)).then_inc(s["smallsrc"], 16)
            sc.dma_start(rest_rows[r0:r1, :], b_out.rearrange("(c p) -> c p", p=P)).then_inc(s["smallsrc"], 16)
            sc.dma_start(rest_rows[r1:, :], router_w.rearrange("e (c p) -> (e c) p", p=P)).then_inc(s["smallsrc"], 32)
            sc.dma_start(swap[:], swap_d).then_inc(s["small_in"], 16)
            sc.wait_ge(s["cond_done"], 1)
            sc.activation(v3(condT[:], DC), bank[2][:, 0:R_BIN].rearrange("p (b c) -> p c b", c=DC),
                          ACT.Silu).then_inc(s["cond_ok"], 1)

            def copy(o, i_):
                return sc.activation(o, i_, ACT.Copy)

            def sum_squares(e, m):
                if m == 0:
                    wait_places(sc, e)
                r, uses = matrix_place(e, m)
                sc.wait_ge(staged_in[r], 32 * (uses + 1))
                full, at = (FC - 1) * D, 2 * e * W1_EXP + m * FC * D
                sc.activation(W1_b16[:, at:at + full], staged[r][:, 0:full], ACT.Square,
                              accum_out=sumsq[:, 4 * e + 2 * m:4 * e + 2 * m + 1])
                sc.activation(W1_b16[0:F_LAST, at + full:at + FC * D], staged[r][0:F_LAST, full:FC * D], ACT.Square,
                              accum_out=sumsq[0:F_LAST, 4 * e + 2 * m + 1:4 * e + 2 * m + 2]).then_inc(s["sumsq_ok"], 1)

            def turn_out(g):
                kind, e, n = groups[g]
                if (kind, n) == ("down", 1) and e + 1 < E:
                    sum_squares(e + 1, 1)
                if split(g):
                    if (kind, n) == ("gate", 0):
                        sc.wait_ge(s["wscale_ok"], e + 1)
                    sc.wait_ge(s["turn_done"], g + 1)
                    src, hi, lo = split_views(g)
                    c = 2 * e + MATRIX[kind]
                    sc.activation(hi, src, ACT.Identity, scale=w_scale[:, c:c + 1]).then_inc(s["turn_act"], 1)
                    if (kind, n) == ("gate", 2) and e + 1 < E:
                        sum_squares(e + 1, 0)
                elif by_act(g):
                    if kind == "down" and n == 0:
                        wait_places(sc, e)
                    sc.wait_ge(s["turn_done"], g + 1)
                    evacuate(copy, g).then_inc(s["turn_act"], 1)

            turn_out(0)
            for k in range(STEPS):
                for b in at_step(k, 0):
                    sc.wait_ge(s["t_done"], b + 1)
                    if b == 0:
                        sc.wait_ge(s["modA_ok"], 1)
                    for dc in range(DC):
                        sc.activation(hT[:, dc * TOKENS + b * S:dc * TOKENS + (b + 1) * S],
                                      bank[2][:, dc * S:(dc + 1) * S], ACT.Identity,
                                      scale=modcol(SCALE_A, dc, b), bias=modcol(SHIFT_A, dc, b)).then_inc(s["hT_ok"], 1)
                for g in step_slot(k, 0):
                    turn_out(g)
                if k == 0:
                    turn_out(2)
                    for m in (SHIFT_B, SCALE_B, GATE_B):
                        sc.wait_ge(s["modrow_done"], m // 2 + 1)
                        sc.wait_ge(s["row_ga_ok"], 1)
                        sc.activation(modrow[:, m * D:(m + 1) * D], bank[3 + m // 2][0:B, m % 2 * D:(m % 2 + 1) * D],
                                      ACT.Identity, bias=1.0 if m == SCALE_B else 0.0).then_inc(s["rowsB_ok"], 1)
                    turn_out(4)
                    sc.wait_ge(s["half_ok"], 2)
                    sum_squares(0, 0)
                    sum_squares(0, 1)
                for b in at_step(k, 1):
                    if b == 0:
                        sc.wait_ge(s["mod_ok"], 1)
                    for t in range(TB):
                        sc.wait_ge(s["kvsb_ok"], b * TB + t + 1)
                        if b or t:
                            sc.wait_ge(s["ksq_ok"], b * TB + t)
                        sc.activation(sink, kv_at(b, t)[:, 0:D], ACT.Square,
                                      accum_out=ksq[:, b * TB + t:b * TB + t + 1]).then_inc(s["ksq_ok"], 1)
                for g in step_slot(k, 1):
                    turn_out(g)
                for b in at_step(k, 1):
                    sc.wait_ge(s["q_done"], b + 1)
                    sc.activation(qT[:, TOKENS + b * S:TOKENS + (b + 1) * S], bank[6][:, 0:S], ACT.Identity,
                                  bias=smallT[:, 1:2]).then_inc(s["q1_ok"], 1)
                    for dc in range(DC):
                        h = hT[:, dc * TOKENS + b * S:dc * TOKENS + (b + 1) * S]
                        sc.activation(h, h, ACT.Identity, scale=modcol(GATE_A, dc, b),
                                      bias=gate_bias[:, dc * B + b:dc * B + b + 1]).then_inc(s["hg_ok"], 1)
                for b in at_step(k, 2):
                    sc.wait_ge(s["a_done"], b + 1)
                    sc.activation(attn_sum[:, b * DC:(b + 1) * DC], bank[6][:, S:S + DC], ACT.Copy).then_inc(s["asum_ok"], 1)
                    sc.wait_ge(s["asum_ok"], b + 1)
                    if b >= 2:
                        sc.wait_ge(s["y_done"], b - 1)
                    else:
                        sc.wait_ge(s["turn_act"], sum(by_act(g) for g in range(FIRST)))
                    for dc in range(DC):
                        c = (b % 2) * DC * D + dc * D
                        sc.activation(wA[:, c:c + D], w_outT[:, dc * D:(dc + 1) * D], ACT.Identity,
                                      scale=attn_sum[:, b * DC + dc:b * DC + dc + 1]).then_inc(s["wA_ok"], 1)
                for n in (2, 3):
                    for g in step_slot(k, n):
                        turn_out(g)
                for b in at_step(k, 5):
                    sc.wait_ge(s["th_done"], b + 1)
                    if b:
                        sc.wait_ge(s["r_done"], b)
                    else:
                        sc.wait_ge(s["kvp_ok"], B - 1)
                    sc.activation(h2T, bank[2][:], ACT.Copy).then_inc(s["h2T_ok"], 1)
                for n in (4, 5):
                    for g in step_slot(k, n):
                        turn_out(g)
            sc.wait_ge(s["sub_ok"], 1)
            sc.activation(expo[:], logit_less_max[:], ACT.Exp).then_inc(s["expo_ok"], 1)
            for g in range(route_first, tiles_first):
                turn_out(g)

            def slots_out(i, c):
                sc.wait_ge(s["xt_done"], 4 * i + c + 1)
                sc.activation(slot_hi, bank[6][:, D:2 * D], ACT.Copy).then_inc(s["slot_hi_ok"], 1)

            def tile_step(i, c):
                def turn_some(n):
                    for g in tile_slot(i, c, n):
                        turn_out(g)
                sc.wait_ge(s["unscale_ok"], 4 * i + c + 1)
                for n, w in enumerate(PIECES):
                    sc.wait_ge(s["gu_done"], len(PIECES) * (4 * i + c) + n + 1)
                    sc.activation(sig[:, n * PIECE:n * PIECE + w], bank[2 + n][:, 0:w], ACT.Silu,
                                  scale=unscale[c % 2][:, 0:1]).then_inc(s["sig_ok"], 1)
                    turn_some(n)
                if not (isinstance(i, int) and c == SLOT_TILES - 1):
                    slots_out(i, c + 1)
                turn_some(3)
                turn_some(4)
                sc.wait_ge(s["at_done"], 2 * (4 * i + c) + 2)
                sc.activation(actT[:, 4 * P:5 * P], bank[6][:, 0:P], ACT.Copy)
                sc.activation(actT[0:F_LAST, 5 * P:6 * P], bank[6][0:F_LAST, P:2 * P], ACT.Copy).then_inc(s["actT_a"], 1)
                turn_some(5)

            slots_out(0, 0)
            turns(sc, tile_step)

        def bc_mid(ap, n):
            return ap.rearrange("p (a m) -> p a m", a=1).to_broadcast([P, n, ap.shape[1]])

        def bc_last(ap, n):
            return ap.rearrange("p (m a) -> p m a", a=1).to_broadcast([P, ap.shape[1], n])

        def routing_choice(ve, link):
            for i in range(3):
                ve.memset(tiles_sum[i][:, 0:SUM0], 0.0)
            ve.wait_ge(s["r_done"], B)
            ve.wait_ge(s["gateb_in"], 16 * B)
            for b in range(B):
                ins = ve.tensor_scalar(lg[:, b * TB * E:(b + 1) * TB * E], bank[3][:, b * TB * E:(b + 1) * TB * E],
                                       gate_b[:, b * (D + 1) + D:(b + 1) * (D + 1)], None, ALU.mult)
            link(ins)
            link(ve.tensor_reduce(top[0][:], v3(lg[:], TT), AX.X, ALU.max))
            ve.tensor_tensor(v3(logit_less_max[:], TT), v3(lg[:], TT), bc_last(top[0][:], E), ALU.subtract).then_inc(s["sub_ok"], 1)
            rev = bc_mid(keep[:, C_REV:C_REV + E], TT)
            for n, sel in enumerate(choice):
                logits, largest = lg, top[0]
                if n:
                    link(ve.scalar_tensor_tensor(lg2[:], choice[0][:], -3.0e38, lg[:], ALU.mult, ALU.add))
                    link(ve.tensor_reduce(top[1][:], v3(lg2[:], TT), AX.X, ALU.max))
                    logits, largest = lg2, top[1]
                link(ve.tensor_tensor(v3(sel[:], TT), v3(logits[:], TT), bc_last(largest[:], E), ALU.is_equal))
                link(ve.tensor_tensor(v3(sel[:], TT), v3(sel[:], TT), rev, ALU.mult))
                link(ve.tensor_reduce(top_rev[:], v3(sel[:], TT), AX.X, ALU.max))
                link(ve.tensor_tensor(v3(sel[:], TT), v3(sel[:], TT), bc_last(top_rev[:], E), ALU.is_equal))
            ve.tensor_tensor(chosen[:], choice[0][:], choice[1][:], ALU.add).then_inc(s["sel_ok"], 1)
            ve.wait_ge(s["sel_ok"], 1)
            for i, d in enumerate((1, 2, 4)):
                if i == 0:
                    link(ve.tensor_copy(tiles_sum[2][:, SUM0:SUM0 + NR], chosen[:]))
                prev, this = tiles_sum[(i + 2) % 3], tiles_sum[i]
                ins = ve.tensor_tensor(this[:, SUM0:SUM0 + NR], prev[:, SUM0:SUM0 + NR],
                                       prev[:, SUM0 - d * E:SUM0 - d * E + NR], ALU.add)
                if i < 2:
                    link(ins)
                else:
                    ins.then_inc(s["sums_ok"], 1)

        def routing_places(ve, link):
            ve.wait_ge(s["expo_ok"], 1)
            for n, sel in enumerate(choice):
                link(ve.tensor_tensor(picked[:], expo[:], sel[:], ALU.mult))
                link(ve.tensor_reduce(weight[n][:], v3(picked[:], TT), AX.X, ALU.add))
            link(ve.tensor_tensor(weight_sum[:], weight[0][:], weight[1][:], ALU.add))
            link(ve.reciprocal(weight_sum[:], weight_sum[:]))
            rows = v3(rows1[:], TT)
            for n in range(2):
                link(ve.tensor_tensor(weight[n][:], weight[n][:], weight_sum[:], ALU.mult))
            ve.tensor_copy(rows[:, :, WEIGHT], weight[0][:])
            ve.tensor_tensor(rows[:, :, WEIGHT_STEP], weight[1][:], weight[0][:], ALU.subtract)
            ve.tensor_copy(rows[:, :, UNSCALE].rearrange("p (b t) -> p b t", t=TB),
                           gate_b[:].rearrange("p (b w) -> p b w", w=D + 1)[:, :, D:D + 1].to_broadcast([P, B, TB]))
            ve.memset(rows[:, :, UNSCALE + 1:ROW], 0.0).then_inc(s["rows_ok"], 1)
            ve.wait_ge(s["cnt_done"], 1)
            n_e, steps, incl, excl = cnt[:, 0:E], cnt[:, E:2 * E], cnt[:, 2 * E:3 * E], cnt[:, 3 * E:4 * E]
            link(ve.tensor_copy(n_e, bank[7][:, 0:E]))
            link(ve.tensor_tensor(v3(stp[:, 0:7 * E], E), bc_last(n_e, 7), bc_mid(keep[:, C_STEP:C_STEP + 7], E), ALU.is_gt))
            link(ve.tensor_reduce(steps, v3(stp[:, 0:7 * E], E), AX.X, ALU.add))
            link(ve.tensor_scalar(steps, steps, 1.0, None, ALU.add))
            link(ve.tensor_tensor_scan(incl, keep[:, C_ONE:C_ONE + E], steps, 0.0, ALU.mult, ALU.add))
            link(ve.tensor_tensor(excl, incl, steps, ALU.subtract))
            link(ve.tensor_scalar(excl, excl, float(P), None, ALU.mult))
            link(ve.tensor_tensor(v3(slot_all[:], TT), v3(bank[7][:, P:P + NR], TT), bc_mid(excl, TT), ALU.add))
            for n, sel in enumerate(choice):
                link(ve.tensor_tensor(picked[:], slot_all[:], sel[:], ALU.mult))
                link(ve.tensor_reduce(slot[:, n * TT:(n + 1) * TT], v3(picked[:], TT), AX.X, ALU.add))
            ve.wait_ge(s["y_done"], B)
            counter = keep[:, C_TILE:C_TILE + NT]
            link(ve.tensor_scalar(slot_low[:], slot[:], 1.0 / P, None, ALU.mult))
            link(ve.tensor_tensor(v3(one_hot_tile, PAIRS), bc_mid(counter, PAIRS), bc_last(slot_low[:], NT), ALU.is_le))
            link(ve.tensor_reduce(slot_tile[:], v3(one_hot_tile, PAIRS), AX.X, ALU.add))
            ve.scalar_tensor_tensor(slot_low[:], slot_tile[:], -float(P), slot[:], ALU.mult, ALU.add)
            link(ve.tensor_scalar(slot_tile[:], slot_tile[:], 1.0, None, ALU.subtract))
            link(ve.tensor_tensor(v3(one_hot_tile, PAIRS), bc_mid(counter, PAIRS), bc_last(slot_tile[:], NT), ALU.is_equal))
            link(ve.tensor_tensor(v3(token_tile, PAIRS), v3(one_hot_tile, PAIRS),
                                  bc_last(keep[:, C_TOKEN:C_TOKEN + PAIRS], NT), ALU.mult))
            for i in range(PAIRS):
                ve.tensor_scalar(one_hot_place[:, i * P:(i + 1) * P], keep[:, C_LOW:C_LOW + P], slot_low[:, i:i + 1],
                                 None, ALU.is_equal).then_inc(s["place_ok"], 1)

        def routing_table(ve, link):
            link(ve.tensor_tensor(v3(til[:], NT), bc_mid(cnt[:, 2 * E:3 * E], NT), bc_last(keep[:, C_TILE:C_TILE + NT], E), ALU.is_le))
            link(ve.tensor_reduce(tile_e[:], v3(til[:], NT), AX.X, ALU.add))
            ve.tensor_scalar(tile_ei[:], tile_e[:], float(E - 1), None, ALU.min).then_inc(s["tile_ok"], 1)
            ve.wait_ge(s["table_done"], 1)
            link(ve.tensor_copy(filled[:], bank[7][:, 2 * P:2 * P + NT]))
            ve.tensor_scalar(nobody[:], filled[:], 0.5, float(NOWHERE), ALU.is_lt, ALU.mult)
            link(ve.tensor_scalar(second[:], filled[:], float(TOKENS) + 0.5, None, ALU.is_gt))
            link(ve.scalar_tensor_tensor(source[:], second[:], -float(TOKENS), filled[:], ALU.mult, ALU.add))
            ve.tensor_scalar(source_i[:], source[:], -1.0, 0.0, ALU.add, ALU.max).then_inc(s["source_ok"], 1)
            link(ve.tensor_tensor(nobody[:], nobody[:], filled[:], ALU.add))
            ve.tensor_scalar(dest_i[:], nobody[:], -1.0, None, ALU.add).then_inc(s["dest_ok"], 1)

        @block.vector
        def _(ve):
            links = [0]

            def link(ins):
                links[0] += 1
                ins.then_inc(s["dchain"], 1)
                ve.wait_ge(s["dchain"], links[0])

            def turn_out(g):
                kind, e, n = groups[g]
                if not by_dve(g):
                    return
                if kind == "norm":
                    cols = slice(2 * e, 2 * e + 2)
                    ve.wait_ge(s["turn_done"], g + 1)
                    ve.tensor_reduce(w_norm2[:, cols], v3(bank[group_bank[g]][:, 0:4], 2), AX.X, ALU.add).then_inc(s["turn_dve"], 1)
                    wait_out(ve, g)
                    link(ve.tensor_scalar(w_power[:, cols], w_norm2[:, cols].bitcast(I32), 2.0 ** -24, None, ALU.mult))
                    ve.tensor_scalar(w_scale_bits[:, cols], w_power[:, cols], -2.0 ** 23, 204.0 * 2 ** 23,
                                     ALU.mult, ALU.add).then_inc(s["wscale_ok"], 1)
                    link(ve.tensor_scalar(w_unscale_bits[:, cols], w_power[:, cols], 2.0 ** 23, 50.0 * 2 ** 23,
                                          ALU.mult, ALU.add))
                elif split(g):
                    ve.wait_ge(s["turn_act"], sum(by_act(h) for h in range(g + 1)))
                    src, hi, lo = split_views(g)
                    c = 2 * e + MATRIX[kind]
                    ve.scalar_tensor_tensor(lo, src, w_scale[:, c:c + 1], hi, ALU.mult, ALU.subtract
                                            ).then_inc(s["turn_dve"], 1)
                else:
                    if n == 0 and kind == "down":
                        wait_places(ve, e)
                    ve.wait_ge(s["turn_done"], g + 1)
                    evacuate(ve.tensor_copy, g).then_inc(s["turn_dve"], 1)

            def norm_stats(b, src, st, mv, ve_, inc_st, inc_ve):
                for t in range(TB):
                    j = b * TB + t
                    ve.bn_stats(st[:, j * 6:(j + 1) * 6], src[:, j * D:(j + 1) * D]).then_inc(s[inc_st], 1)
                for t in range(TB):
                    j = b * TB + t
                    ve.wait_ge(s[inc_st], 2 * b * TB + t + 1)
                    ve.bn_aggr(mv[:, 2 * j:2 * j + 2], st[:, j * 6:(j + 1) * 6]).then_inc(s[inc_st], 1)
                ve.wait_ge(s[inc_st], 2 * (b + 1) * TB)
                ve.tensor_scalar(ve_[:, b * TB:(b + 1) * TB],
                                 mv[:, 2 * b * TB:2 * (b + 1) * TB].rearrange("p (t c) -> p t c", c=2)[:, :, 1],
                                 EPS, None, ALU.add).then_inc(s[inc_ve], 1)

            def normed(b):
                ve.wait_ge(s["rstd_ok"], b + 1)
                if b == 1:
                    ve.wait_ge(s["modrow_done"], 3)
                if b >= 2:
                    ve.wait_ge(s["t_done"], b - 1)
                for t in range(TB):
                    j = b * TB + t
                    ins = ve.tensor_scalar(xn[b % 2][:, t * D:(t + 1) * D], x[:, j * D:(j + 1) * D],
                                           mean_var[:, 2 * j:2 * j + 1], rstd[:, j:j + 1],
                                           ALU.subtract, ALU.mult)
                ins.then_inc(s["xn_ok"], 1)

            ve.memset(half_neg[:], -0.5).then_inc(s["half_ok"], 1)
            ve.memset(sumsq[:], 0.0).then_inc(s["half_ok"], 1)
            ve.wait_ge(x_in[0], 16)
            norm_stats(0, x, stats, mean_var, var_eps, "stat_ok", "veps_ok")
            normed(0)

            def mod_row(m, out_row):
                ve.wait_ge(s["modrow_done"], m // 2 + 1)
                src = bank[3 + m // 2][0:B, m % 2 * D:(m % 2 + 1) * D]
                if m == SCALE_A:
                    return ve.tensor_scalar(out_row, src, 1.0, None, ALU.add)
                return ve.tensor_copy(out_row, src)

            def guard(g, t1, t2):
                link(ve.tensor_scalar(t1, g, -1.0, None, ALU.mult))
                link(ve.tensor_tensor(t1, t1, g, ALU.max))
                ve.tensor_scalar(t2, g, 0.0, 2.0, ALU.is_ge, ALU.mult)
                link(ve.tensor_scalar(t1, t1, GATE_MIN, None, ALU.max))
                return ve.scalar_tensor_tensor(g, t2, -1.0, t1, ALU.add, ALU.mult)

            for m in (SHIFT_A, SCALE_A):
                mod_row(m, modrow[:, m * D:(m + 1) * D]).then_inc(s["rowsA_ok"], 1)
            ve.wait_ge(s["small_done"], 1)
            ve.tensor_copy(smallT[:], bank[2][:, R_BIN:R_ALL]).then_inc(s["smallT_ok"], 1)
            n16, n8 = GATE_A * DC * B, DC * B
            ve.wait_ge(s["modT_done"], 1)
            ve.tensor_copy(mod[:, 0:n16], bank[6][:, 0:n16]).then_inc(s["modA_ok"], 1)
            turn_out(1)
            ve.wait_ge(x_in[1], 16)
            norm_stats(1, x, stats, mean_var, var_eps, "stat_ok", "veps_ok")
            turn_out(3)
            ve.wait_ge(s["bq_done"], 1)
            link(ve.tensor_copy(bias_q[:], bank[6][:, 3 * DC * B:3 * DC * B + 1]))
            mod_row(GATE_A, modrow[:, GATE_A * D:(GATE_A + 1) * D]).then_inc(s["row_ga_ok"], 1)
            normed(1)
            ve.wait_ge(s["modT_done"], 2)
            ga = mod[:, n16:n16 + n8]
            link(ve.tensor_copy(ga, bank[6][:, n16:n16 + n8]))
            link(guard(ga, gatetmp[:, 0:n8], gatetmp[:, n8:2 * n8]))
            for dc in range(DC):
                ins = ve.tensor_scalar(gate_bias[:, dc * B:(dc + 1) * B], ga[:, dc * B:(dc + 1) * B],
                                       smallT[:, T_BOUT + dc:T_BOUT + dc + 1], None, ALU.mult)
            ins.then_inc(s["mod_ok"], 1)

            for k in range(STEPS):
                for b in at_step(k, -1):
                    if b > 1:
                        normed(b)
                for g in step_slot(k, 0):
                    turn_out(g)
                for b in at_step(k, 1):
                    if b == 0:
                        ve.wait_ge(s["bkv_in"], 16)
                        ve.wait_ge(s["rotf_in"], 16)
                    for t in range(TB):
                        ve.wait_ge(s["kv_done"], b * TB + t + 1)
                        if b >= 2:
                            ve.wait_ge(s["kvp_ok"], b - 1)
                        ve.tensor_tensor(kv_at(b, t), bank[3 + t][:], bias_kv, ALU.add).then_inc(s["kvsb_ok"], 1)
                for g in step_slot(k, 1):
                    turn_out(g)
                for b in at_step(k, 1):
                    ve.wait_ge(s["q_done"], b + 1)
                    if b:
                        ve.wait_ge(s["qr_ok"], b)
                    ve.scalar_tensor_tensor(qsin, bank[5][:, S:2 * S], bias_q[:, 0:1], rot_feature[:, S:2 * S],
                                            ALU.add, ALU.mult).then_inc(s["q0_ok"], 1)
                    ve.scalar_tensor_tensor(qT[:, b * S:(b + 1) * S], bank[5][:, 0:S], smallT[:, 0:1],
                                            rot_feature[:, 0:S], ALU.add, ALU.mult).then_inc(s["q0_ok"], 1)
                for b in at_step(k, -2):
                    ve.wait_ge(x_in[b], 16)
                    norm_stats(b, x, stats, mean_var, var_eps, "stat_ok", "veps_ok")
                if k == 1:
                    ve.wait_ge(s["rowsB_ok"], 3)
                    link(guard(modrow[:, GATE_B * D:MODS * D], modtmp[:, 0:D], modtmp[:, D:2 * D]))
                    both = modrow[:, SHIFT_B * D:(SCALE_B + 1) * D]
                    link(ve.tensor_scalar(modtmp, both, -1.0, None, ALU.mult))
                    link(ve.tensor_tensor(modtmp, modtmp, both, ALU.max))
                    link(ve.tensor_reduce(bounds[:, 0:2], v3(modtmp, 2), AX.X, ALU.max))
                    link(ve.scalar_tensor_tensor(bounds[:, 2:3], bounds[:, 1:2], NORMED_MAX, bounds[:, 0:1],
                                                 ALU.mult, ALU.add))
                    link(ve.tensor_scalar(modrow[:, MODS * D:MODS * D + 1], bounds[:, 2:3], 1.0 / FULL, LEAST,
                                          ALU.mult, ALU.max))
                    link(ve.reciprocal(bounds[:, 3:4], modrow[:, MODS * D:MODS * D + 1]))
                    ve.tensor_scalar(both, both, bounds[:, 3:4], None, ALU.mult).then_inc(s["rowsB_ok"], 1)
                for g in step_slot(k, 2):
                    turn_out(g)
                for b in at_step(k, 3):
                    ve.wait_ge(s["y_done"], b + 1)
                    ve.wait_ge(s["hg_ok"], DC * (b + 1))
                    for dc in range(DC):
                        h = hT[:, dc * TOKENS + b * S:dc * TOKENS + (b + 1) * S]
                        ve.scalar_tensor_tensor(h, bank[7][:, dc * S:(dc + 1) * S], modcol(GATE_A, dc, b), h,
                                                ALU.mult, ALU.add).then_inc(s["z_ok"], 1)
                for g in step_slot(k, 3):
                    turn_out(g)
                for b in at_step(k, 4):
                    ve.wait_ge(s["tz_done"], b + 1)
                    xb = x[:, b * TB * D:(b + 1) * TB * D]
                    ve.tensor_tensor(xb, bank[5][:], xb, ALU.add).then_inc(s["x2_ok"], 1)
                    ve.wait_ge(s["x2_ok"], b + 1)
                    norm_stats(b, x, stats2, mean_var2, var_eps2, "stat2_ok", "veps2_ok")
                    if b == 0:
                        ve.wait_ge(s["modb_in"], 16 * B)
                        ve.wait_ge(s["kvp_ok"], B - 1)
                    else:
                        ve.wait_ge(s["h2_ok"], b)
                    for t in range(TB):
                        j = b * TB + t
                        ve.scalar_tensor_tensor(diff[t], x[:, j * D:(j + 1) * D], mean_var2[:, 2 * j:2 * j + 1],
                                                mod_b[:, b * 2 * D + D:(b + 1) * 2 * D],
                                                ALU.subtract, ALU.mult).then_inc(s["diff_ok"], 1)
                for g in step_slot(k, 4):
                    turn_out(g)
                for b in at_step(k, 4):
                    ve.wait_ge(s["rstd2_ok"], b + 1)
                    for t in range(TB):
                        j = b * TB + t
                        ve.wait_ge(s["diff_ok"], j + 1)
                        ins = ve.scalar_tensor_tensor(rows1[:, j * ROW:j * ROW + D], diff[t], rstd2[:, j:j + 1],
                                                      mod_b[:, b * 2 * D:b * 2 * D + D], ALU.mult, ALU.add)
                    ins.then_inc(s["h2_ok"], 1)
                for g in step_slot(k, 5):
                    turn_out(g)
            routing_choice(ve, link)
            routing_places(ve, link)
            routing_table(ve, link)
            for g in range(route_first, tiles_first):
                turn_out(g)

            def slots_out(i, c):
                ve.wait_ge(s["slot_hi_ok"], 4 * i + c + 1)
                ve.tensor_tensor(slot_lo, bank[6][:, D:2 * D], slot_hi, ALU.subtract).then_inc(s["slot_lo_ok"], 1)
                row = xs[c % 4]
                ve.scalar_tensor_tensor(slot_weight[c % 4][:], row[:, WEIGHT_STEP:WEIGHT_STEP + 1],
                                        second[:, bass.ds(4 * i + c, 1)], row[:, WEIGHT:WEIGHT + 1], ALU.mult, ALU.add)
                e = ve.value_load(tile_ei[0:1, bass.ds(4 * i + c, 1)], min_val=0, max_val=E - 1)
                ve.tensor_scalar(unscale[c % 2][:], w_unscale[:, bass.ds(e * 2, 2)],
                                 xs[c % 4][:, UNSCALE:UNSCALE + 1], None, ALU.mult).then_inc(s["unscale_ok"], 1)

            def mult_pieces(i, c, turn_some):
                for n, w in enumerate(PIECES):
                    ve.wait_ge(s["sig_ok"], len(PIECES) * (4 * i + c) + n + 1)
                    ve.scalar_tensor_tensor(act[:, n * PIECE:n * PIECE + w], bank[2 + n][:, w:2 * w],
                                            unscale[c % 2][:, 1:2], sig[:, n * PIECE:n * PIECE + w],
                                            ALU.mult, ALU.mult).then_inc(s["act_ok"], 1)
                    turn_some(n)

            def result(i, c, r):
                ve.wait_ge(s["down_done"], 4 * i + c + 1)
                if not (isinstance(i, int) and 4 * i + c < 2):
                    ve.wait_ge(y_out[r], 16 * (2 * i + c // 2))
                ve.tensor_scalar(y_sb[r], bank[7][:, 0:D], slot_weight[c % 4][:, 0:1], None,
                                 ALU.mult).then_inc(s["y_ok"], 1)

            def tile_step(i, c):
                def turn_some(n):
                    for g in tile_slot(i, c, n):
                        turn_out(g)
                mult_pieces(i, c, turn_some)
                if not (isinstance(i, int) and c == SLOT_TILES - 1):
                    slots_out(i, c + 1)
                turn_some(3)
                if c >= 1:
                    result(i, c - 1, (c - 1) % 2)
                turn_some(4)
                ve.wait_ge(s["at_done"], 2 * (4 * i + c) + 1)
                ve.tensor_copy(actT[:, 0:4 * P], bank[5][:]).then_inc(s["actT_v"], 1)
                turn_some(5)

            slots_out(0, 0)
            turns(ve, tile_step)
            result(0, SLOT_TILES - 1, (SLOT_TILES - 1) % 2)

            ve.wait_ge(s["gateb_in"], 16 * B)
            finish(ve, FINISH_DVE, link, s["fin_ok"])

        @block.gpsimd
        def _(po):
            po.wait_ge(s["half_ok"], 1)
            klinks = [0]

            def klink(ins):
                klinks[0] += 1
                ins.then_inc(s["kchain"], 1)
                po.wait_ge(s["kchain"], klinks[0])

            for k in range(-2, STEPS):
                for b in at_step(k, -2):
                    po.wait_ge(s["veps_ok"], b + 1)
                    po.tensor_tensor(rstd[:, b * TB:(b + 1) * TB], var_eps[:, b * TB:(b + 1) * TB],
                                     half_neg[:, 0:TB], ALU.pow).then_inc(s["rstd_ok"], 1)
                for b in at_step(k, 1):
                    if b == 0:
                        po.wait_ge(s["rott_in"], 16)
                    po.wait_ge(s["kvsb_ok"], TB * (b + 1))
                    kvb = v3(kv_b(b), TB)
                    k1 = kvb[:, :, 0:P]
                    kr = v3(ksw, TB)
                    po.wait_ge(s["ksq_ok"], TB * (b + 1))
                    if b:
                        po.wait_ge(s["kvp_ok"], b)
                    for t in range(TB):
                        kt = kv_at(b, t)[:, 0:P].rearrange("p (i two) -> p i two", two=2)[:, :, ::-1]
                        ins = po.tensor_tensor(ksw[:, t * P:(t + 1) * P].rearrange("p (i two) -> p i two", two=2), kt,
                                               rot_token[:, (2 + t) * P:(3 + t) * P].rearrange("p (i two) -> p i two", two=2),
                                               ALU.mult)
                    klink(ins)
                    klink(po.tensor_tensor(k1, k1, v3(rot_token[:, 0:2 * P], TB), ALU.mult))
                    klink(po.tensor_tensor(k1, k1, kr, ALU.add))
                    po.tensor_tensor(v3(kvp[:, b * TB * D:(b + 1) * TB * D], TB), kvb[:, :, 0:D], kvb[:, :, D:2 * D],
                                     ALU.mult).then_inc(s["kvp_ok"], 1)
                    cols = slice(b * TB, (b + 1) * TB)
                    klink(po.tensor_scalar(ksq_max[:, cols], ksq[:, cols], TINY, None, ALU.max))
                    po.tensor_tensor(kinv[:, cols], ksq_max[:, cols], half_neg[:, 0:TB], ALU.pow).then_inc(s["kinv_ok"], 1)
                    po.wait_ge(s["q0_ok"], 2 * (b + 1))
                    q = qT[:, b * S:(b + 1) * S]
                    po.tensor_tensor(q, q, qsin, ALU.add).then_inc(s["qr_ok"], 1)
                for b in at_step(k, 4):
                    po.wait_ge(s["veps2_ok"], b + 1)
                    po.tensor_tensor(rstd2[:, b * TB:(b + 1) * TB], var_eps2[:, b * TB:(b + 1) * TB],
                                     half_neg[:, 0:TB], ALU.pow).then_inc(s["rstd2_ok"], 1)

            def gather(j):
                po.indirect_dma_start(xs[j % 4], None, rows_d, bass.IndirectOffsetOnAxis(source_i[:, j:j + 1], 0),
                                      bounds_check=last_token, oob_is_err=False).then_inc(xs_in[j % 4], 16)

            last_token = po.to_reg(TOKENS - 1)
            last_part = po.to_reg(2 * TOKENS - 1)

            po.wait_ge(s["rows_out"], 16)
            po.wait_ge(s["source_ok"], 1)
            for j in range(4):
                gather(j)
            po.wait_ge(s["dest_ok"], 1)
            for j in range(SLOT_TILES):
                r = j % 2
                po.wait_ge(s["y_ok"], j + 1)
                po.indirect_dma_start(parts_d, bass.IndirectOffsetOnAxis(dest_i[:, j:j + 1], 0), y_sb[r], None,
                                      bounds_check=last_part, oob_is_err=False).then_inc(y_out[r], 16)
                if j + 4 < SLOT_TILES:
                    gather(j + 4)
            po.wait_ge(s["gateb_in"], 16 * B)
            finish(po, FINISH_POOL, klink, s["pool_fin_ok"])


_ORDER = ["L0_attn_X", "L0_attn_W_in", "L0_attn_b_in", "L0_attn_W_out", "L0_attn_b_out", "L0_ffn_router_w",
          "L0_ffn_Wg", "L0_ffn_Wu", "L0_ffn_Wd", "L0_c", "L0_wmod"]


def kernel(**inputs):
    import concourse.bacc as bacc
    from concourse.bass_utils import run_bass_kernel_spmd

    nc = bacc.Bacc("TRN2", target_bir_lowering=False, num_devices=1)
    arrays = {name: np.ascontiguousarray(inputs[name]) for name in _ORDER}
    for name, a in zip(("keep", "swap", "rot_feature", "rot_token"), shape_constants()):
        arrays[name] = a
    args = [nc.dram_tensor(f"in_{n}", a.shape, F32, kind="ExternalInput").ap() for n, a in arrays.items()]
    out = nc.dram_tensor("out", (B, S, D), F32, kind="ExternalOutput").ap()
    layer(nc, *args, out)
    r = run_bass_kernel_spmd(nc, [{f"in_{n}": a for n, a in arrays.items()}], core_ids=[0])
    return r.results[0]["out"]
```
